# Optimizing a Trainium2 kernel written in Bass

```python
import numpy as np
import jax
import jax.numpy as jnp

def _softmax(x, axis=-1):
    return jax.nn.softmax(x, axis=axis)

def _gelu(x):
    return jax.nn.gelu(x, approximate=True)

def _silu(x):
    return jax.nn.silu(x)

def _sigmoid(x):
    return jax.nn.sigmoid(x)

def _layernorm(x, axis=-1, eps=1e-05):
    m = jnp.mean(x, axis=axis, keepdims=True)
    v = jnp.var(x, axis=axis, keepdims=True)
    return (x - m) / jnp.sqrt(v + eps)

def _scatter_add(tgt, idx, src, axis=0):
    return tgt.at[idx].add(src)

def _segment_sum(src, seg, n):
    return jax.ops.segment_sum(src, seg, n)
kernel_name = 'mk_hybrid_d2_jaxref_r8_1fa5bc'

def setup_inputs(seed: int=0):
    np.random.seed(seed)
    _w = jnp.asarray

    def _L0_attn_a_setup():
        import jax, jax.numpy as jnp
        from jax import lax
        import numpy as np
        D_MODEL = 128
        D_STATE = 16
        D_CONV = 4
        EXPAND = 2
        D_INNER = EXPAND * D_MODEL
        DT_RANK = (D_MODEL + 15) // 16
        B = 4
        L = 256

        def _layernorm(x, g, b):
            mu = x.mean(-1, keepdims=True)
            v = ((x - mu) ** 2).mean(-1, keepdims=True)
            return (x - mu) * lax.rsqrt(v + 1e-05) * g + b

        def _mamba(x, in_w, conv_w, conv_b, xp_w, dtp_w, dtp_b, A_log, Dskip, out_w):
            Bb = x.shape[0]
            xz = x @ in_w.T
            xc, z = jnp.split(xz, 2, axis=-1)
            xct = jnp.transpose(xc, (0, 2, 1))
            xct = lax.conv_general_dilated(xct, conv_w, (1,), [(D_CONV - 1, 0)], dimension_numbers=('NCH', 'OIH', 'NCH'), feature_group_count=D_INNER) + conv_b[None, :, None]
            xc = jax.nn.silu(jnp.transpose(xct, (0, 2, 1)))
            x_dbl = xc @ xp_w.T
            dt = x_dbl[..., :DT_RANK]
            Bm = x_dbl[..., DT_RANK:DT_RANK + D_STATE]
            Cm = x_dbl[..., DT_RANK + D_STATE:]
            delta = jax.nn.softplus(dt @ dtp_w.T + dtp_b)
            A = -jnp.exp(A_log)

            def step(h, inp):
                u_t, d_t, B_t, C_t = inp
                dA = jnp.exp(d_t[..., None] * A)
                h = dA * h + (d_t * u_t)[..., None] * B_t[:, None, :]
                y = jnp.sum(h * C_t[:, None, :], axis=-1)
                return (h, y)
            h0 = jnp.zeros((Bb, D_INNER, D_STATE), x.dtype)
            xs = (jnp.transpose(xc, (1, 0, 2)), jnp.transpose(delta, (1, 0, 2)), jnp.transpose(Bm, (1, 0, 2)), jnp.transpose(Cm, (1, 0, 2)))
            _, ys = lax.scan(step, h0, xs)
            y = jnp.transpose(ys, (1, 0, 2)) + xc * Dskip
            y = y * jax.nn.silu(z)
            return y @ out_w.T
        key = jax.random.key(seed)
        ks = jax.random.split(key, 16)

        def w(k, shape, s=0.02):
            return jax.random.normal(k, shape, jnp.float32) * s
        inp = {'x': jax.random.normal(ks[0], (B, L, D_MODEL), jnp.float32)}
        inp['ln_gamma'] = jnp.ones((D_MODEL,), jnp.float32)
        inp['ln_beta'] = jnp.zeros((D_MODEL,), jnp.float32)
        i = 1
        A_init = jnp.log(jnp.broadcast_to(jnp.arange(1, D_STATE + 1, dtype=jnp.float32), (D_INNER, D_STATE)))
        for sfx in ('f', 'b'):
            inp[f'in_w_{sfx}'] = w(ks[i], (2 * D_INNER, D_MODEL))
            i += 1
            inp[f'conv_w_{sfx}'] = w(ks[i], (D_INNER, 1, D_CONV), 0.1)
            i += 1
            inp[f'conv_b_{sfx}'] = jnp.zeros((D_INNER,), jnp.float32)
            inp[f'xp_w_{sfx}'] = w(ks[i], (DT_RANK + 2 * D_STATE, D_INNER))
            i += 1
            inp[f'dtp_w_{sfx}'] = w(ks[i], (D_INNER, DT_RANK), 0.1)
            i += 1
            inp[f'dtp_b_{sfx}'] = w(ks[i], (D_INNER,), 0.5)
            i += 1
            inp[f'A_log_{sfx}'] = A_init
            inp[f'D_{sfx}'] = jnp.ones((D_INNER,), jnp.float32)
            inp[f'out_w_{sfx}'] = w(ks[i], (D_MODEL, D_INNER))
            i += 1
        inp['proj_w'] = w(ks[i], (D_MODEL, 2 * D_MODEL))
        i += 1
        inp['proj_b'] = jnp.zeros((D_MODEL,), jnp.float32)
        return inp
    _L0_attn_a_in = _L0_attn_a_setup()

    def _L0_attn_b_setup():
        import jax, jax.numpy as jnp
        import numpy as np
        LN_EPS = 1e-05
        key = jax.random.key(seed)
        ks = jax.random.split(key, 4)
        B_, S, D = (32, 128, 128)
        return {'x': jax.random.normal(ks[0], (B_, S, D), dtype=jnp.float32), 'A': jax.random.normal(ks[1], (D, D), dtype=jnp.float32) * 0.01, 'B': jax.random.normal(ks[2], (D, D), dtype=jnp.float32) * 0.01, 'C': jax.random.normal(ks[3], (D, D), dtype=jnp.float32) * 0.01, 'gamma': jnp.ones((D,), dtype=jnp.float32), 'beta': jnp.zeros((D,), dtype=jnp.float32)}
    _L0_attn_b_in = _L0_attn_b_setup()

    def _L0_ffn_setup():
        import jax, jax.numpy as jnp
        import numpy as np
        from jax import lax
        B, L, D = (4, 256, 128)
        E, TOPK = (8, 2)
        K, DIL = (3, 1)
        HID = D // 4
        EPS = 1e-06

        def _rmsnorm(h, w):
            rms = jnp.sqrt(jnp.mean(h * h, axis=-1, keepdims=True) + EPS)
            return w * (h / rms)

        def _forward(x, dw_kernel, dw_bias, pw_w, pw_b, router_w, router_b, expert_w, expert_b, out_w, out_b, norm_w, ff_down_w, ff_down_b, ff_up_w, ff_up_b):
            pad = (K - 1) * DIL
            xc = jnp.transpose(x, (0, 2, 1))
            xc = lax.conv_general_dilated(xc, dw_kernel, window_strides=(1,), padding=((pad, 0),), rhs_dilation=(DIL,), dimension_numbers=('NCH', 'OIH', 'NCH'), feature_group_count=D) + dw_bias[None, :, None]
            xc = jax.nn.silu(jnp.einsum('bdl,ed->bel', xc, pw_w) + pw_b[None, :, None])
            x1 = x + jnp.transpose(xc, (0, 2, 1))
            logits = jnp.einsum('bsd,ed->bse', x1, router_w) + router_b
            top_v, top_i = lax.top_k(logits, TOPK)
            top_w = jax.nn.softmax(top_v, axis=-1)
            rw = jnp.sum(jax.nn.one_hot(top_i, E, dtype=x1.dtype) * top_w[..., None], axis=-2)
            ye = jax.nn.silu(jnp.einsum('bsd,eod->bseo', x1, expert_w) + expert_b)
            combined = jnp.einsum('bse,bseo->bso', rw, ye)
            moe_out = jnp.einsum('bsd,od->bso', combined, out_w) + out_b
            h = _rmsnorm(x1 + moe_out, norm_w)
            ff = jax.nn.gelu(jnp.einsum('bsd,hd->bsh', h, ff_down_w) + ff_down_b, approximate=False)
            ff = jnp.einsum('bsh,dh->bsd', ff, ff_up_w) + ff_up_b
            return h + ff
        key = jax.random.key(seed)
        ks = jax.random.split(key, 16)
        s = 0.02
        return {'x': jax.random.normal(ks[0], (B, L, D), dtype=jnp.float32), 'dw_kernel': jax.random.normal(ks[1], (D, 1, K), dtype=jnp.float32) * s, 'dw_bias': jnp.zeros((D,), dtype=jnp.float32), 'pw_w': jax.random.normal(ks[2], (D, D), dtype=jnp.float32) * s, 'pw_b': jnp.zeros((D,), dtype=jnp.float32), 'router_w': jax.random.normal(ks[3], (E, D), dtype=jnp.float32) * s, 'router_b': jnp.zeros((E,), dtype=jnp.float32), 'expert_w': jax.random.normal(ks[4], (E, D, D), dtype=jnp.float32) * s, 'expert_b': jnp.zeros((E, D), dtype=jnp.float32), 'out_w': jax.random.normal(ks[5], (D, D), dtype=jnp.float32) * s, 'out_b': jnp.zeros((D,), dtype=jnp.float32), 'norm_w': jnp.ones((D,), dtype=jnp.float32), 'ff_down_w': jax.random.normal(ks[6], (HID, D), dtype=jnp.float32) * s, 'ff_down_b': jnp.zeros((HID,), dtype=jnp.float32), 'ff_up_w': jax.random.normal(ks[7], (D, HID), dtype=jnp.float32) * s, 'ff_up_b': jnp.zeros((D,), dtype=jnp.float32)}
    _L0_ffn_in = _L0_ffn_setup()

    def _L1_attn_a_setup():
        import jax, jax.numpy as jnp
        import numpy as np
        D_MODEL = 128
        N_HEADS = 16
        HEAD_DIM = D_MODEL // N_HEADS
        WINDOW = 128
        LOCAL_BLOCK = 32
        LATENT_TOKENS = 64
        LATENT_D = 32
        LATENT_HEADS = 4
        LATENT_HD = LATENT_D // LATENT_HEADS
        NEG = -1000000000.0

        def _local_attention(q, k, v):
            B, H, S, hd = q.shape
            bs = min(S, max(WINDOW, LOCAL_BLOCK))
            nb = S // bs
            w = WINDOW
            L = bs + w - 1
            k_pad = jnp.pad(k, ((0, 0), (0, 0), (w - 1, 0), (0, 0)))
            v_pad = jnp.pad(v, ((0, 0), (0, 0), (w - 1, 0), (0, 0)))
            starts = jnp.arange(nb) * bs
            idx = starts[:, None] + jnp.arange(L)[None, :]
            kb = k_pad[:, :, idx]
            vb = v_pad[:, :, idx]
            qb = q.reshape(B, H, nb, bs, hd)
            q_pos = starts[:, None] + jnp.arange(bs)[None, :]
            k_gpos = starts[:, None] + jnp.arange(L)[None, :] - (w - 1)
            dist = q_pos[:, :, None] - k_gpos[:, None, :]
            allowed = (dist > 0) & (dist <= w) & (k_gpos[:, None, :] >= 0)
            scale = 1.0 / np.sqrt(hd)
            scores = jnp.einsum('bhnqd,bhnkd->bhnqk', qb, kb) * scale
            scores = jnp.where(allowed, scores, NEG)
            attn = jax.nn.softmax(scores, axis=-1)
            attn = jnp.where(allowed.any(-1)[None, None, :, :, None], attn, 0.0)
            out = jnp.einsum('bhnqk,bhnkd->bhnqd', attn, vb)
            return out.reshape(B, H, S, hd)
        key = jax.random.key(seed)
        ks = jax.random.split(key, 14)
        B, S = (2, 512)
        s = 0.02
        f32 = jnp.float32
        return {'x': jax.random.normal(ks[0], (B, S, D_MODEL), f32), 'qkv_w': jax.random.normal(ks[1], (D_MODEL, 3 * D_MODEL), f32) * s, 'qkv_b': jnp.zeros((3 * D_MODEL,), f32), 'rq_w': jax.random.normal(ks[2], (D_MODEL, LATENT_D), f32) * s, 'rq_b': jnp.zeros((LATENT_D,), f32), 'rkv_w': jax.random.normal(ks[3], (D_MODEL, 2 * LATENT_D), f32) * s, 'rkv_b': jnp.zeros((2 * LATENT_D,), f32), 'rout_w': jax.random.normal(ks[4], (LATENT_D, D_MODEL), f32) * s, 'rout_b': jnp.zeros((D_MODEL,), f32), 'out_w': jax.random.normal(ks[5], (D_MODEL, D_MODEL), f32) * s, 'out_b': jnp.zeros((D_MODEL,), f32), 'gl_w': jax.random.normal(ks[6], (HEAD_DIM, 1), f32) * s, 'gr_w': jax.random.normal(ks[7], (HEAD_DIM, 1), f32) * s}
    _L1_attn_a_in = _L1_attn_a_setup()

    def _L1_attn_b_setup():
        import jax, jax.numpy as jnp
        import numpy as np
        D_MODEL = 128
        NUM_HEADS = 16
        D_K = D_MODEL // NUM_HEADS
        THETA = 10000.0

        def apply_rope(x, positions):
            half = D_K // 2
            inv_freq = THETA ** (-jnp.arange(half, dtype=jnp.float32) * 2.0 / D_K)
            angles = positions[:, None, :, None].astype(jnp.float32) * inv_freq
            cos, sin = (jnp.cos(angles), jnp.sin(angles))
            x1 = x[..., 0::2]
            x2 = x[..., 1::2]
            out_even = x1 * cos - x2 * sin
            out_odd = x1 * sin + x2 * cos
            out = jnp.stack([out_even, out_odd], axis=-1)
            return out.reshape(x.shape)
        key = jax.random.key(seed)
        ks = jax.random.split(key, 5)
        b, s = (2, 256)
        scale = 0.02
        return {'x': jax.random.normal(ks[0], (b, s, D_MODEL), dtype=jnp.float32), 'Wq': jax.random.normal(ks[1], (D_MODEL, D_MODEL), dtype=jnp.float32) * scale, 'Wk': jax.random.normal(ks[2], (D_MODEL, D_MODEL), dtype=jnp.float32) * scale, 'Wv': jax.random.normal(ks[3], (D_MODEL, D_MODEL), dtype=jnp.float32) * scale, 'Wo': jax.random.normal(ks[4], (D_MODEL, D_MODEL), dtype=jnp.float32) * scale}
    _L1_attn_b_in = _L1_attn_b_setup()

    def _L1_ffn_setup():
        import jax, jax.numpy as jnp
        import numpy as np
        B, S, D, F, E, K = (4, 256, 128, 512, 8, 2)
        FS = 128
        LN_EPS = 1e-05

        def _swiglu(x, gu_w, dn_w):
            gate, up = jnp.split(x @ gu_w, 2, axis=-1)
            gate = jnp.clip(gate, -10.0, 10.0)
            return jax.nn.silu(gate) * up @ dn_w
        key = jax.random.key(seed)
        ks = jax.random.split(key, 6)
        s = 0.02
        return {'x': jax.random.normal(ks[0], (B, S, D), jnp.float32), 'ln_gamma': jnp.ones((D,), jnp.float32), 'ln_beta': jnp.zeros((D,), jnp.float32), 'router_w': jax.random.normal(ks[1], (D, E), jnp.float32) * s, 'gate_up_w': jax.random.normal(ks[2], (E, D, 2 * F), jnp.float32) * s, 'down_w': jax.random.normal(ks[3], (E, F, D), jnp.float32) * s, 'shared_gate_up_w': jax.random.normal(ks[4], (D, 2 * FS), jnp.float32) * s, 'shared_down_w': jax.random.normal(ks[5], (FS, D), jnp.float32) * s}
    _L1_ffn_in = _L1_ffn_setup()
    _d = {'L0_attn_a_x': _L0_attn_a_in['x'], 'L0_attn_a_ln_gamma': _L0_attn_a_in['ln_gamma'], 'L0_attn_a_ln_beta': _L0_attn_a_in['ln_beta'], 'L0_attn_a_in_w_f': _L0_attn_a_in['in_w_f'], 'L0_attn_a_conv_w_f': _L0_attn_a_in['conv_w_f'], 'L0_attn_a_conv_b_f': _L0_attn_a_in['conv_b_f'], 'L0_attn_a_xp_w_f': _L0_attn_a_in['xp_w_f'], 'L0_attn_a_dtp_w_f': _L0_attn_a_in['dtp_w_f'], 'L0_attn_a_dtp_b_f': _L0_attn_a_in['dtp_b_f'], 'L0_attn_a_A_log_f': _L0_attn_a_in['A_log_f'], 'L0_attn_a_D_f': _L0_attn_a_in['D_f'], 'L0_attn_a_out_w_f': _L0_attn_a_in['out_w_f'], 'L0_attn_a_in_w_b': _L0_attn_a_in['in_w_b'], 'L0_attn_a_conv_w_b': _L0_attn_a_in['conv_w_b'], 'L0_attn_a_conv_b_b': _L0_attn_a_in['conv_b_b'], 'L0_attn_a_xp_w_b': _L0_attn_a_in['xp_w_b'], 'L0_attn_a_dtp_w_b': _L0_attn_a_in['dtp_w_b'], 'L0_attn_a_dtp_b_b': _L0_attn_a_in['dtp_b_b'], 'L0_attn_a_A_log_b': _L0_attn_a_in['A_log_b'], 'L0_attn_a_D_b': _L0_attn_a_in['D_b'], 'L0_attn_a_out_w_b': _L0_attn_a_in['out_w_b'], 'L0_attn_a_proj_w': _L0_attn_a_in['proj_w'], 'L0_attn_a_proj_b': _L0_attn_a_in['proj_b'], 'L0_attn_b_A': _L0_attn_b_in['A'], 'L0_attn_b_B': _L0_attn_b_in['B'], 'L0_attn_b_C': _L0_attn_b_in['C'], 'L0_attn_b_gamma': _L0_attn_b_in['gamma'], 'L0_attn_b_beta': _L0_attn_b_in['beta'], 'L0_ffn_dw_kernel': _L0_ffn_in['dw_kernel'], 'L0_ffn_dw_bias': _L0_ffn_in['dw_bias'], 'L0_ffn_pw_w': _L0_ffn_in['pw_w'], 'L0_ffn_pw_b': _L0_ffn_in['pw_b'], 'L0_ffn_router_w': _L0_ffn_in['router_w'], 'L0_ffn_router_b': _L0_ffn_in['router_b'], 'L0_ffn_expert_w': _L0_ffn_in['expert_w'], 'L0_ffn_expert_b': _L0_ffn_in['expert_b'], 'L0_ffn_out_w': _L0_ffn_in['out_w'], 'L0_ffn_out_b': _L0_ffn_in['out_b'], 'L0_ffn_norm_w': _L0_ffn_in['norm_w'], 'L0_ffn_ff_down_w': _L0_ffn_in['ff_down_w'], 'L0_ffn_ff_down_b': _L0_ffn_in['ff_down_b'], 'L0_ffn_ff_up_w': _L0_ffn_in['ff_up_w'], 'L0_ffn_ff_up_b': _L0_ffn_in['ff_up_b'], 'L1_attn_a_qkv_w': _L1_attn_a_in['qkv_w'], 'L1_attn_a_qkv_b': _L1_attn_a_in['qkv_b'], 'L1_attn_a_rq_w': _L1_attn_a_in['rq_w'], 'L1_attn_a_rq_b': _L1_attn_a_in['rq_b'], 'L1_attn_a_rkv_w': _L1_attn_a_in['rkv_w'], 'L1_attn_a_rkv_b': _L1_attn_a_in['rkv_b'], 'L1_attn_a_rout_w': _L1_attn_a_in['rout_w'], 'L1_attn_a_rout_b': _L1_attn_a_in['rout_b'], 'L1_attn_a_out_w': _L1_attn_a_in['out_w'], 'L1_attn_a_out_b': _L1_attn_a_in['out_b'], 'L1_attn_a_gl_w': _L1_attn_a_in['gl_w'], 'L1_attn_a_gr_w': _L1_attn_a_in['gr_w'], 'L1_attn_b_Wq': _L1_attn_b_in['Wq'], 'L1_attn_b_Wk': _L1_attn_b_in['Wk'], 'L1_attn_b_Wv': _L1_attn_b_in['Wv'], 'L1_attn_b_Wo': _L1_attn_b_in['Wo'], 'L1_ffn_ln_gamma': _L1_ffn_in['ln_gamma'], 'L1_ffn_ln_beta': _L1_ffn_in['ln_beta'], 'L1_ffn_router_w': _L1_ffn_in['router_w'], 'L1_ffn_gate_up_w': _L1_ffn_in['gate_up_w'], 'L1_ffn_down_w': _L1_ffn_in['down_w'], 'L1_ffn_shared_gate_up_w': _L1_ffn_in['shared_gate_up_w'], 'L1_ffn_shared_down_w': _L1_ffn_in['shared_down_w']}
    _x0 = _d['L0_attn_a_x']
    _d['L0_attn_a_x'] = jax.random.normal(jax.random.fold_in(jax.random.key(seed), 1), (32, 256, 128), dtype=_x0.dtype)
    del _x0
    return _d

def reference(L0_attn_a_x, L0_attn_a_ln_gamma, L0_attn_a_ln_beta, L0_attn_a_in_w_f, L0_attn_a_conv_w_f, L0_attn_a_conv_b_f, L0_attn_a_xp_w_f, L0_attn_a_dtp_w_f, L0_attn_a_dtp_b_f, L0_attn_a_A_log_f, L0_attn_a_D_f, L0_attn_a_out_w_f, L0_attn_a_in_w_b, L0_attn_a_conv_w_b, L0_attn_a_conv_b_b, L0_attn_a_xp_w_b, L0_attn_a_dtp_w_b, L0_attn_a_dtp_b_b, L0_attn_a_A_log_b, L0_attn_a_D_b, L0_attn_a_out_w_b, L0_attn_a_proj_w, L0_attn_a_proj_b, L0_attn_b_A, L0_attn_b_B, L0_attn_b_C, L0_attn_b_gamma, L0_attn_b_beta, L0_ffn_dw_kernel, L0_ffn_dw_bias, L0_ffn_pw_w, L0_ffn_pw_b, L0_ffn_router_w, L0_ffn_router_b, L0_ffn_expert_w, L0_ffn_expert_b, L0_ffn_out_w, L0_ffn_out_b, L0_ffn_norm_w, L0_ffn_ff_down_w, L0_ffn_ff_down_b, L0_ffn_ff_up_w, L0_ffn_ff_up_b, L1_attn_a_qkv_w, L1_attn_a_qkv_b, L1_attn_a_rq_w, L1_attn_a_rq_b, L1_attn_a_rkv_w, L1_attn_a_rkv_b, L1_attn_a_rout_w, L1_attn_a_rout_b, L1_attn_a_out_w, L1_attn_a_out_b, L1_attn_a_gl_w, L1_attn_a_gr_w, L1_attn_b_Wq, L1_attn_b_Wk, L1_attn_b_Wv, L1_attn_b_Wo, L1_ffn_ln_gamma, L1_ffn_ln_beta, L1_ffn_router_w, L1_ffn_gate_up_w, L1_ffn_down_w, L1_ffn_shared_gate_up_w, L1_ffn_shared_down_w):

    def _L0_attn_a_ref(x, ln_gamma, ln_beta, in_w_f, conv_w_f, conv_b_f, xp_w_f, dtp_w_f, dtp_b_f, A_log_f, D_f, out_w_f, in_w_b, conv_w_b, conv_b_b, xp_w_b, dtp_w_b, dtp_b_b, A_log_b, D_b, out_w_b, proj_w, proj_b):
        import jax, jax.numpy as jnp
        from jax import lax
        import numpy as np
        D_MODEL = 128
        D_STATE = 16
        D_CONV = 4
        EXPAND = 2
        D_INNER = EXPAND * D_MODEL
        DT_RANK = (D_MODEL + 15) // 16
        B = 4
        L = 256

        def _layernorm(x, g, b):
            mu = x.mean(-1, keepdims=True)
            v = ((x - mu) ** 2).mean(-1, keepdims=True)
            return (x - mu) * lax.rsqrt(v + 1e-05) * g + b

        def _mamba(x, in_w, conv_w, conv_b, xp_w, dtp_w, dtp_b, A_log, Dskip, out_w):
            Bb = x.shape[0]
            xz = x @ in_w.T
            xc, z = jnp.split(xz, 2, axis=-1)
            xct = jnp.transpose(xc, (0, 2, 1))
            xct = lax.conv_general_dilated(xct, conv_w, (1,), [(D_CONV - 1, 0)], dimension_numbers=('NCH', 'OIH', 'NCH'), feature_group_count=D_INNER) + conv_b[None, :, None]
            xc = jax.nn.silu(jnp.transpose(xct, (0, 2, 1)))
            x_dbl = xc @ xp_w.T
            dt = x_dbl[..., :DT_RANK]
            Bm = x_dbl[..., DT_RANK:DT_RANK + D_STATE]
            Cm = x_dbl[..., DT_RANK + D_STATE:]
            delta = jax.nn.softplus(dt @ dtp_w.T + dtp_b)
            A = -jnp.exp(A_log)

            def step(h, inp):
                u_t, d_t, B_t, C_t = inp
                dA = jnp.exp(d_t[..., None] * A)
                h = dA * h + (d_t * u_t)[..., None] * B_t[:, None, :]
                y = jnp.sum(h * C_t[:, None, :], axis=-1)
                return (h, y)
            h0 = jnp.zeros((Bb, D_INNER, D_STATE), x.dtype)
            xs = (jnp.transpose(xc, (1, 0, 2)), jnp.transpose(delta, (1, 0, 2)), jnp.transpose(Bm, (1, 0, 2)), jnp.transpose(Cm, (1, 0, 2)))
            _, ys = lax.scan(step, h0, xs)
            y = jnp.transpose(ys, (1, 0, 2)) + xc * Dskip
            y = y * jax.nn.silu(z)
            return y @ out_w.T
        xn = _layernorm(x, ln_gamma, ln_beta)
        y_f = _mamba(xn, in_w_f, conv_w_f, conv_b_f, xp_w_f, dtp_w_f, dtp_b_f, A_log_f, D_f, out_w_f)
        y_b = jnp.flip(_mamba(jnp.flip(xn, 1), in_w_b, conv_w_b, conv_b_b, xp_w_b, dtp_w_b, dtp_b_b, A_log_b, D_b, out_w_b), 1)
        y = jnp.concatenate([y_f, y_b], axis=-1) @ proj_w.T + proj_b
        return x + y

    def _L0_attn_b_ref(x, A, B, C, gamma, beta):
        import jax, jax.numpy as jnp
        import numpy as np
        LN_EPS = 1e-05
        batch, seq_len, d = x.shape
        xb = jnp.einsum('bsd,ed->sbe', x, B)

        def step(h, xb_t):
            h = jnp.tanh(h @ A.T + xb_t)
            y = h @ C.T
            return (h, y)
        h0 = jnp.zeros((batch, d), dtype=x.dtype)
        _, ys = jax.lax.scan(step, h0, xb)
        out = jnp.transpose(ys, (1, 0, 2)) + x
        mu = jnp.mean(out, axis=-1, keepdims=True)
        var = jnp.mean(jnp.square(out - mu), axis=-1, keepdims=True)
        return (out - mu) * jax.lax.rsqrt(var + LN_EPS) * gamma + beta

    def _L0_ffn_ref(x, dw_kernel, dw_bias, pw_w, pw_b, router_w, router_b, expert_w, expert_b, out_w, out_b, norm_w, ff_down_w, ff_down_b, ff_up_w, ff_up_b):
        import jax, jax.numpy as jnp
        import numpy as np
        from jax import lax
        B, L, D = (4, 256, 128)
        E, TOPK = (8, 2)
        K, DIL = (3, 1)
        HID = D // 4
        EPS = 1e-06

        def _rmsnorm(h, w):
            rms = jnp.sqrt(jnp.mean(h * h, axis=-1, keepdims=True) + EPS)
            return w * (h / rms)

        def _forward(x, dw_kernel, dw_bias, pw_w, pw_b, router_w, router_b, expert_w, expert_b, out_w, out_b, norm_w, ff_down_w, ff_down_b, ff_up_w, ff_up_b):
            pad = (K - 1) * DIL
            xc = jnp.transpose(x, (0, 2, 1))
            xc = lax.conv_general_dilated(xc, dw_kernel, window_strides=(1,), padding=((pad, 0),), rhs_dilation=(DIL,), dimension_numbers=('NCH', 'OIH', 'NCH'), feature_group_count=D) + dw_bias[None, :, None]
            xc = jax.nn.silu(jnp.einsum('bdl,ed->bel', xc, pw_w) + pw_b[None, :, None])
            x1 = x + jnp.transpose(xc, (0, 2, 1))
            logits = jnp.einsum('bsd,ed->bse', x1, router_w) + router_b
            top_v, top_i = lax.top_k(logits, TOPK)
            top_w = jax.nn.softmax(top_v, axis=-1)
            rw = jnp.sum(jax.nn.one_hot(top_i, E, dtype=x1.dtype) * top_w[..., None], axis=-2)
            ye = jax.nn.silu(jnp.einsum('bsd,eod->bseo', x1, expert_w) + expert_b)
            combined = jnp.einsum('bse,bseo->bso', rw, ye)
            moe_out = jnp.einsum('bsd,od->bso', combined, out_w) + out_b
            h = _rmsnorm(x1 + moe_out, norm_w)
            ff = jax.nn.gelu(jnp.einsum('bsd,hd->bsh', h, ff_down_w) + ff_down_b, approximate=False)
            ff = jnp.einsum('bsh,dh->bsd', ff, ff_up_w) + ff_up_b
            return h + ff
        return _forward(x, dw_kernel, dw_bias, pw_w, pw_b, router_w, router_b, expert_w, expert_b, out_w, out_b, norm_w, ff_down_w, ff_down_b, ff_up_w, ff_up_b)

    def _L1_attn_a_ref(x, qkv_w, qkv_b, rq_w, rq_b, rkv_w, rkv_b, rout_w, rout_b, out_w, out_b, gl_w, gr_w):
        import jax, jax.numpy as jnp
        import numpy as np
        D_MODEL = 128
        N_HEADS = 16
        HEAD_DIM = D_MODEL // N_HEADS
        WINDOW = 128
        LOCAL_BLOCK = 32
        LATENT_TOKENS = 64
        LATENT_D = 32
        LATENT_HEADS = 4
        LATENT_HD = LATENT_D // LATENT_HEADS
        NEG = -1000000000.0

        def _local_attention(q, k, v):
            B, H, S, hd = q.shape
            bs = min(S, max(WINDOW, LOCAL_BLOCK))
            nb = S // bs
            w = WINDOW
            L = bs + w - 1
            k_pad = jnp.pad(k, ((0, 0), (0, 0), (w - 1, 0), (0, 0)))
            v_pad = jnp.pad(v, ((0, 0), (0, 0), (w - 1, 0), (0, 0)))
            starts = jnp.arange(nb) * bs
            idx = starts[:, None] + jnp.arange(L)[None, :]
            kb = k_pad[:, :, idx]
            vb = v_pad[:, :, idx]
            qb = q.reshape(B, H, nb, bs, hd)
            q_pos = starts[:, None] + jnp.arange(bs)[None, :]
            k_gpos = starts[:, None] + jnp.arange(L)[None, :] - (w - 1)
            dist = q_pos[:, :, None] - k_gpos[:, None, :]
            allowed = (dist > 0) & (dist <= w) & (k_gpos[:, None, :] >= 0)
            scale = 1.0 / np.sqrt(hd)
            scores = jnp.einsum('bhnqd,bhnkd->bhnqk', qb, kb) * scale
            scores = jnp.where(allowed, scores, NEG)
            attn = jax.nn.softmax(scores, axis=-1)
            attn = jnp.where(allowed.any(-1)[None, None, :, :, None], attn, 0.0)
            out = jnp.einsum('bhnqk,bhnkd->bhnqd', attn, vb)
            return out.reshape(B, H, S, hd)
        B, S, D = x.shape
        qkv = x @ qkv_w + qkv_b
        q, k, v = jnp.split(qkv, 3, axis=-1)

        def heads(t):
            return t.reshape(B, S, N_HEADS, HEAD_DIM).transpose(0, 2, 1, 3)
        local = _local_attention(heads(q), heads(k), heads(v))
        chunk = -(-S // min(LATENT_TOKENS, S))
        nlat = S // chunk
        pooled = x.reshape(B, nlat, chunk, D).mean(axis=2)
        chunk_ids = jnp.arange(S) // chunk
        rq = (x @ rq_w + rq_b).reshape(B, S, LATENT_HEADS, LATENT_HD).transpose(0, 2, 1, 3)
        rkv = pooled @ rkv_w + rkv_b
        rk, rv = jnp.split(rkv, 2, axis=-1)
        rk = rk.reshape(B, nlat, LATENT_HEADS, LATENT_HD).transpose(0, 2, 1, 3)
        rv = rv.reshape(B, nlat, LATENT_HEADS, LATENT_HD).transpose(0, 2, 1, 3)
        lscale = 1.0 / np.sqrt(LATENT_HD)
        lscores = jnp.einsum('bhsd,bhld->bhsl', rq, rk) * lscale
        lat_allowed = jnp.arange(nlat)[None, :] < chunk_ids[:, None]
        lscores = jnp.where(lat_allowed[None, None], lscores, NEG)
        lattn = jax.nn.softmax(lscores, axis=-1)
        lattn = jnp.where(lat_allowed.any(-1)[None, None, :, None], lattn, 0.0)
        lat_out = jnp.einsum('bhsl,bhld->bhsd', lattn, rv)
        lat_out = lat_out.transpose(0, 2, 1, 3).reshape(B, S, LATENT_D)
        remote = lat_out @ rout_w + rout_b
        remote_h = remote.reshape(B, S, N_HEADS, HEAD_DIM).transpose(0, 2, 1, 3)
        gate = jax.nn.sigmoid(local @ gl_w + remote_h @ gr_w)
        mixed = gate * local + (1.0 - gate) * remote_h
        mixed = mixed.transpose(0, 2, 1, 3).reshape(B, S, D)
        return mixed @ out_w + out_b

    def _L1_attn_b_ref(x, Wq, Wk, Wv, Wo):
        import jax, jax.numpy as jnp
        import numpy as np
        D_MODEL = 128
        NUM_HEADS = 16
        D_K = D_MODEL // NUM_HEADS
        THETA = 10000.0

        def apply_rope(x, positions):
            half = D_K // 2
            inv_freq = THETA ** (-jnp.arange(half, dtype=jnp.float32) * 2.0 / D_K)
            angles = positions[:, None, :, None].astype(jnp.float32) * inv_freq
            cos, sin = (jnp.cos(angles), jnp.sin(angles))
            x1 = x[..., 0::2]
            x2 = x[..., 1::2]
            out_even = x1 * cos - x2 * sin
            out_odd = x1 * sin + x2 * cos
            out = jnp.stack([out_even, out_odd], axis=-1)
            return out.reshape(x.shape)
        b, s, _ = x.shape
        Q = x @ Wq.T
        K = x @ Wk.T
        V = x @ Wv.T
        split = lambda t: t.reshape(b, s, NUM_HEADS, D_K).transpose(0, 2, 1, 3)
        Q, K, V = (split(Q), split(K), split(V))
        positions = jnp.broadcast_to(jnp.arange(s, dtype=jnp.int32), (b, s))
        Q = apply_rope(Q, positions)
        K = apply_rope(K, positions)
        scores = jnp.einsum('bhqd,bhkd->bhqk', Q, K) / jnp.sqrt(jnp.float32(D_K))
        causal = jnp.tril(jnp.ones((s, s), dtype=bool))
        scores = jnp.where(causal[None, None], scores, -jnp.inf)
        attn = jax.nn.softmax(scores, axis=-1)
        out = jnp.einsum('bhqk,bhkd->bhqd', attn, V)
        out = out.transpose(0, 2, 1, 3).reshape(b, s, D_MODEL)
        return out @ Wo.T

    def _L1_ffn_ref(x, ln_gamma, ln_beta, router_w, gate_up_w, down_w, shared_gate_up_w, shared_down_w):
        import jax, jax.numpy as jnp
        import numpy as np
        B, S, D, F, E, K = (4, 256, 128, 512, 8, 2)
        FS = 128
        LN_EPS = 1e-05

        def _swiglu(x, gu_w, dn_w):
            gate, up = jnp.split(x @ gu_w, 2, axis=-1)
            gate = jnp.clip(gate, -10.0, 10.0)
            return jax.nn.silu(gate) * up @ dn_w
        b, s, d = x.shape
        xf = x.reshape(-1, d)
        mu = jnp.mean(xf, axis=-1, keepdims=True)
        var = jnp.var(xf, axis=-1, keepdims=True)
        xn = (xf - mu) * jax.lax.rsqrt(var + LN_EPS) * ln_gamma + ln_beta
        logits = xn @ router_w
        probs = jax.nn.softmax(logits, axis=-1)
        topv, topi = jax.lax.top_k(probs, K)
        topv = topv / jnp.sum(topv, axis=-1, keepdims=True)
        comb = jnp.sum(jax.nn.one_hot(topi, E, dtype=xn.dtype) * topv[..., None], axis=1)
        out = jnp.zeros_like(xf)
        for e in range(E):
            out = out + comb[:, e:e + 1] * _swiglu(xn, gate_up_w[e], down_w[e])
        out = out + _swiglu(xn, shared_gate_up_w, shared_down_w)
        return out.reshape(b, s, d)
    x = L0_attn_a_x
    x = x + _L0_attn_a_ref(_layernorm(x, axis=-1), L0_attn_a_ln_gamma, L0_attn_a_ln_beta, L0_attn_a_in_w_f, L0_attn_a_conv_w_f, L0_attn_a_conv_b_f, L0_attn_a_xp_w_f, L0_attn_a_dtp_w_f, L0_attn_a_dtp_b_f, L0_attn_a_A_log_f, L0_attn_a_D_f, L0_attn_a_out_w_f, L0_attn_a_in_w_b, L0_attn_a_conv_w_b, L0_attn_a_conv_b_b, L0_attn_a_xp_w_b, L0_attn_a_dtp_w_b, L0_attn_a_dtp_b_b, L0_attn_a_A_log_b, L0_attn_a_D_b, L0_attn_a_out_w_b, L0_attn_a_proj_w, L0_attn_a_proj_b)
    x = x + _L0_ffn_ref(_layernorm(x, axis=-1), L0_ffn_dw_kernel, L0_ffn_dw_bias, L0_ffn_pw_w, L0_ffn_pw_b, L0_ffn_router_w, L0_ffn_router_b, L0_ffn_expert_w, L0_ffn_expert_b, L0_ffn_out_w, L0_ffn_out_b, L0_ffn_norm_w, L0_ffn_ff_down_w, L0_ffn_ff_down_b, L0_ffn_ff_up_w, L0_ffn_ff_up_b)
    x = x + _L0_attn_b_ref(_layernorm(x, axis=-1), L0_attn_b_A, L0_attn_b_B, L0_attn_b_C, L0_attn_b_gamma, L0_attn_b_beta)
    x = x + _L0_ffn_ref(_layernorm(x, axis=-1), L0_ffn_dw_kernel, L0_ffn_dw_bias, L0_ffn_pw_w, L0_ffn_pw_b, L0_ffn_router_w, L0_ffn_router_b, L0_ffn_expert_w, L0_ffn_expert_b, L0_ffn_out_w, L0_ffn_out_b, L0_ffn_norm_w, L0_ffn_ff_down_w, L0_ffn_ff_down_b, L0_ffn_ff_up_w, L0_ffn_ff_up_b)
    x = x + _L1_attn_a_ref(_layernorm(x, axis=-1), L1_attn_a_qkv_w, L1_attn_a_qkv_b, L1_attn_a_rq_w, L1_attn_a_rq_b, L1_attn_a_rkv_w, L1_attn_a_rkv_b, L1_attn_a_rout_w, L1_attn_a_rout_b, L1_attn_a_out_w, L1_attn_a_out_b, L1_attn_a_gl_w, L1_attn_a_gr_w)
    x = x + _L1_ffn_ref(_layernorm(x, axis=-1), L1_ffn_ln_gamma, L1_ffn_ln_beta, L1_ffn_router_w, L1_ffn_gate_up_w, L1_ffn_down_w, L1_ffn_shared_gate_up_w, L1_ffn_shared_down_w)
    x = x + _L1_attn_b_ref(_layernorm(x, axis=-1), L1_attn_b_Wq, L1_attn_b_Wk, L1_attn_b_Wv, L1_attn_b_Wo)
    x = x + _L1_ffn_ref(_layernorm(x, axis=-1), L1_ffn_ln_gamma, L1_ffn_ln_beta, L1_ffn_router_w, L1_ffn_gate_up_w, L1_ffn_down_w, L1_ffn_shared_gate_up_w, L1_ffn_shared_down_w)
    return x

_drawn_inputs = setup_inputs


def setup_inputs(seed=0):
    import zlib

    import numpy as np

    out = dict(_drawn_inputs(seed))
    spreads = {'L0_attn_a_ln_gamma': (1.0, 0.2),
     'L0_attn_a_ln_beta': (0.0, 0.1),
     'L0_attn_a_conv_b_f': (0.0, 0.1),
     'L0_attn_a_D_f': (1.0, 0.2),
     'L0_attn_a_conv_b_b': (0.0, 0.1),
     'L0_attn_a_D_b': (1.0, 0.2),
     'L0_attn_a_proj_b': (0.0, 0.1),
     'L0_attn_b_gamma': (1.0, 0.2),
     'L0_attn_b_beta': (0.0, 0.1),
     'L0_ffn_dw_bias': (0.0, 0.1),
     'L0_ffn_pw_b': (0.0, 0.1),
     'L0_ffn_router_b': (0.0, 0.1),
     'L0_ffn_expert_b': (0.0, 0.1),
     'L0_ffn_out_b': (0.0, 0.1),
     'L0_ffn_norm_w': (1.0, 0.2),
     'L0_ffn_ff_down_b': (0.0, 0.1),
     'L0_ffn_ff_up_b': (0.0, 0.1),
     'L1_attn_a_qkv_b': (0.0, 0.1),
     'L1_attn_a_rq_b': (0.0, 0.1),
     'L1_attn_a_rkv_b': (0.0, 0.1),
     'L1_attn_a_rout_b': (0.0, 0.1),
     'L1_attn_a_out_b': (0.0, 0.1),
     'L1_ffn_ln_gamma': (1.0, 0.2),
     'L1_ffn_ln_beta': (0.0, 0.1)}
    factors = {}
    for name, (base, spread) in spreads.items():
        noise = np.random.default_rng([zlib.crc32(name.encode()), seed]).standard_normal(out[name].shape)
        drawn = base * np.exp(spread * noise) if base else spread * noise
        out[name] = jnp.asarray(drawn.astype(out[name].dtype))
    for name, factor in factors.items():
        out[name] = (out[name] * factor).astype(out[name].dtype)
    return out
```

```python
from contextlib import ExitStack, contextmanager

import numpy as np

import concourse.bass as bass
from concourse import mybir

F32 = mybir.dt.float32
F32R = mybir.dt.float32r
BF16 = mybir.dt.bfloat16
ALU = mybir.AluOpType
ACT = mybir.ActivationFunctionType
AX_X = mybir.AxisListType.X

D = 128
NSEQ, S = 32, 256
TOK = NSEQ * S
T = 512
SEQ_T = T // S
NT = TOK // T
LEAD = 64

NST = 16
RANK = 8
NE = 8
HID = 32
EPS = 1e-5
LN_AND_EXP = "natural_log_exp_and_others"


PASSED = []


@contextmanager
def signals(nc, stage, *names):
    sems = [nc.alloc_semaphore(f"{stage}_{name}") for name in names]
    for sem in sems:
        nc.sync.sem_inc(sem, LEAD)
    nc.all_engine_barrier()
    yield sems
    nc.clear_and_free_semaphores(sems)
    nc.all_engine_barrier()


def cols(t, width=T):
    return bass.ds(t * width, width)


def tile_pairs(eng, step):
    with eng.Fori(0, NT // 2) as pair:
        for slot in range(2):
            step(pair * 2 + slot, slot)


def layer_norm(nc, stage, mem, src, dst, affine=None, twice=False, residual=None):
    with ExitStack() as ctx:
        sq = ctx.enter_context(nc.sbuf_tensor(stage + "_sq", [D, 2, T], F32))
        logv = ctx.enter_context(nc.sbuf_tensor(stage + "_logv", [D, 2, T], F32))
        rstd = ctx.enter_context(nc.sbuf_tensor(stage + "_rstd", [D, 2, T], F32))
        log1 = ctx.enter_context(nc.sbuf_tensor(stage + "_log1", [D, 2, T], F32)) if residual is not None else None
        rstd1 = ctx.enter_context(nc.sbuf_tensor(stage + "_rstd1", [D, 2, T], F32)) if residual is not None else None
        ps_mean = [mem.bank[0], mem.bank[1]]
        ps_var = [mem.bank[2], mem.bank[3]]
        (mean_ready, centered, squared, var_ready, log_done, rstd_ready, added, scaled) = ctx.enter_context(
            signals(nc, stage, "mean", "centered", "squared", "var", "log", "rstd", "added", "scaled"))
        block = ctx.enter_context(nc.Block())
        n_log = 2 if residual is not None else 1

        @block.tensor
        def _(pe):
            def mean(t, s):
                pe.wait_ge(centered, t - 1 + LEAD)
                nc.tensor.matmul(ps_mean[s], mem.avg, src[:, cols(t)], start=True, stop=True).then_inc(mean_ready, 1)

            def var(t, s):
                pe.wait_ge(squared, t + 1 + LEAD)
                pe.wait_ge(rstd_ready, n_log * (t - 1) + LEAD)
                nc.tensor.matmul(ps_var[s], mem.avg, sq[:, s, :], start=True, stop=True).then_inc(var_ready, 1)

            mean(0, 0)
            with pe.Fori(0, NT // 2 - 1) as pair:
                for s in range(2):
                    mean(pair * 2 + s + 1, 1 - s)
                    var(pair * 2 + s, s)
            mean(NT - 1, 1)
            var(NT - 2, 0)
            var(NT - 1, 1)

        @block.vector
        def _(dve):
            def center(t, s):
                dve.wait_ge(mean_ready, t + 1 + LEAD)
                nc.vector.tensor_tensor(dst[:, cols(t)], src[:, cols(t)], ps_mean[s], ALU.subtract).then_inc(centered, 1)

            def scale(t, s):
                dve.wait_ge(rstd_ready, n_log * (t + 1) + LEAD)
                dve.wait_ge(squared, t + 1 + LEAD)
                if residual is not None:
                    nc.vector.tensor_tensor(rstd1[:, s, :], dst[:, cols(t)], rstd1[:, s, :], ALU.mult).then_inc(scaled, 1)
                    dve.wait_ge(scaled, 2 * t + 1 + LEAD)
                    nc.vector.tensor_tensor(residual[:, cols(t)], residual[:, cols(t)], rstd1[:, s, :], ALU.add).then_inc(added, 1)
                if affine is None:
                    nc.vector.tensor_tensor(dst[:, cols(t)], dst[:, cols(t)], rstd[:, s, :], ALU.mult).then_inc(scaled, 1)
                else:
                    k = 2 if residual is not None else 1
                    nc.vector.scalar_tensor_tensor(dst[:, cols(t)], dst[:, cols(t)], affine[0], rstd[:, s, :],
                                                   ALU.mult, ALU.mult).then_inc(scaled, 1)
                    dve.wait_ge(scaled, k * t + k + LEAD)
                    nc.vector.tensor_scalar(dst[:, cols(t)], dst[:, cols(t)], affine[1], None, ALU.add)

            center(0, 0)
            with dve.Fori(0, NT // 2 - 1) as pair:
                for s in range(2):
                    center(pair * 2 + s + 1, 1 - s)
                    scale(pair * 2 + s, s)
            center(NT - 1, 1)
            scale(NT - 2, 0)
            scale(NT - 1, 1)

        @block.gpsimd
        def _(pool):
            def square(t, s):
                pool.wait_ge(var_ready, t - 1 + LEAD)
                pool.wait_ge(centered, t + 1 + LEAD)
                pool.sem_inc(PASSED[0], 1)
                nc.gpsimd.tensor_tensor(sq[:, s, :], dst[:, cols(t)], dst[:, cols(t)], ALU.mult).then_inc(squared, 1)
            tile_pairs(pool, square)

        @block.scalar
        def _(act):
            def rsqrt(t, s):
                act.wait_ge(scaled, ((t - 1) * (2 if residual is not None else 1)) + LEAD)
                if residual is not None:
                    act.wait_ge(added, t - 1 + LEAD)
                act.wait_ge(var_ready, t + 1 + LEAD)
                if twice:
                    nc.scalar.activation(logv[:, s, :], ps_var[s], ACT.Ln, bias=mem.eps2, scale=1.0 + EPS).then_inc(log_done, 1)
                else:
                    nc.scalar.activation(logv[:, s, :], ps_var[s], ACT.Ln, bias=mem.eps, scale=1.0).then_inc(log_done, 1)
                if residual is not None:
                    nc.scalar.activation(log1[:, s, :], ps_var[s], ACT.Ln, bias=mem.eps, scale=1.0).then_inc(log_done, 1)
                    act.wait_ge(log_done, 2 * t + 2 + LEAD)
                    nc.scalar.activation(rstd1[:, s, :], log1[:, s, :], ACT.Exp, scale=-0.5).then_inc(rstd_ready, 1)
                else:
                    act.wait_ge(log_done, t + 1 + LEAD)
                nc.scalar.activation(rstd[:, s, :], logv[:, s, :], ACT.Exp, scale=-0.5).then_inc(rstd_ready, 1)
            nc.scalar.preload_act_table_set(LN_AND_EXP)
            tile_pairs(act, rsqrt)


class Memory:
    pass
PAD = 3
GN = 2
NG = NST // GN
HALVES = 2
FRONT = 7
USES = FRONT + 1
DIRS = "fb"


def mamba_weights(nc, mem):
    w = mem.w
    with ExitStack() as ctx:
        (exp_done, products) = ctx.enter_context(signals(nc, "mw", "exp", "products"))
        block = ctx.enter_context(nc.Block())

        @block.scalar
        def _(act):
            for d, c in enumerate(DIRS):
                nc.scalar.activation(mem.A[:, d, :], w["A_log_" + c], ACT.Exp).then_inc(exp_done, 1)

        @block.vector
        def _(dve):
            dve.wait_ge(exp_done, 2 + LEAD)
            nc.vector.tensor_scalar(mem.A[:, :, :], mem.A[:, :, :], -1.0, None, ALU.mult)
            for d, c in enumerate(DIRS):
                in_xc = w["in_" + c][:, 0:256].unsqueeze(1).to_broadcast([D, 4, 256])
                nc.vector.tensor_tensor(mem.conv_in[:, d, :, :], w["taps_" + c].rearrange("p (k c) -> p k c", k=4), in_xc, ALU.mult)
            dve.wait_ge(products, 1 + LEAD)
            for d in range(2):
                nc.vector.tensor_copy(mem.out_proj[:, d, :, :], mem.bank[d][:, 0:256].rearrange("p (h o) -> p h o", h=2))

        @block.tensor
        def _(pe):
            for d, c in enumerate(DIRS):
                for h in range(HALVES):
                    last = nc.tensor.matmul(mem.bank[d][:, h * 128:(h + 1) * 128], w["out_" + c][:, h * 128:(h + 1) * 128],
                                            w["proj"][:, d * 128:(d + 1) * 128], start=True, stop=True)
            last.then_inc(products, 1)


def mamba(nc, mem, X, U):
    w = mem.w
    with ExitStack() as ctx:
        def sb(name, shape, dt=F32):
            return ctx.enter_context(nc.sbuf_tensor("mamba_" + name, shape, dt))
        xpad = sb("xpad", [D, 2, SEQ_T, S + 2 * PAD])
        u = sb("u", [D, 2, 2, T])
        z = sb("z", [D, 2, 2, T])
        delta = sb("delta", [D, 2, 2, T])
        du = sb("du", [D, 2, 2, T])
        pre = sb("pre", [D, 2, T])
        soft = sb("soft", [D, 2, T])
        xdbl = sb("xdbl", [D, T])
        rest = sb("rest", [D, T])
        second = sb("second", [D, T], BF16)
        parts = sb("parts", [D, 2, T], BF16)
        outp = sb("outp", [D, T])
        dA = sb("dA", [D, 2, 2, 2, GN, SEQ_T, S])
        bu = sb("bu", [D, 2, GN * T])
        hc = sb("hc", [D, 2, 2, GN, T])
        work = [mem.bank[0], mem.bank[1]]
        ysum = [mem.bank[2], mem.bank[3]]
        b_bc = mem.psum[:, 4:6, :]
        c_bc = mem.psum[:, 6:8, :]

        (xpad_ready, work_ready, work_read, split_step, parts_ready, soft_step, soft_ready, delta_step, du_ready,
         b_ready, c_ready, dA_ready, bu_ready, scanned, hc_ready, summed, y_step, y_ready, added, zeroed
         ) = ctx.enter_context(signals(
            nc, "mamba", "xpad", "work", "work_read", "split_step", "parts", "soft_step", "soft", "delta_step", "du",
            "b_bc", "c_bc", "dA", "bu", "scanned", "hc", "summed", "y_step", "y", "added", "zeroed"))
        block = ctx.enter_context(nc.Block())


        def front_use(t, d, k):
            if isinstance(t, int) and (t, d) == (0, 0):
                return k, k % 2
            return (2 * t + d) * USES - 1 + k, (k + 1) % 2

        def out_use(t, d):
            if isinstance(t, int) and (t, d) == (NT - 1, 1):
                return (2 * t + d) * USES + FRONT, 1
            return (2 * t + d) * USES + 2 * FRONT, 0

        def by_seq(ap):
            return ap.rearrange("p (b t) -> p b t", b=SEQ_T)

        @block.gpsimd
        def _(pool):
            nc.gpsimd.memset(xpad[:, :, :, :], 0.0).then_inc(zeroed, 1)
            nc.gpsimd.memset(dA[:, :, :, :, :, :, :], 0.0).then_inc(zeroed, 1)
            pool.wait_ge(zeroed, 2 + LEAD)
            pool.sem_inc(PASSED[0], 1)

            def load(t, s):
                pool.wait_ge(work_ready, (2 * t - 3) * USES - 1 + 4 + LEAD)
                pool.sem_inc(PASSED[0], 1)
                nc.gpsimd.tensor_copy(xpad[:, s, :, PAD:PAD + S], by_seq(U[:, cols(t)])).then_inc(xpad_ready, 1)

            def front(t, d):
                q = 2 * t + d
                pool.wait_ge(work_read, front_use(t, d, 4)[0] + 1 + LEAD)
                pool.sem_inc(PASSED[0], 1)
                pool.wait_ge(c_ready, NG * (q - 1) + LEAD)
                pool.sem_inc(PASSED[0], 1)
                nc.gpsimd.tensor_copy(parts[:, d, :], xdbl[:, :]).then_inc(split_step, 1)
                pool.wait_ge(split_step, 3 * q + 1 + LEAD)
                pool.sem_inc(PASSED[0], 1)
                nc.gpsimd.tensor_tensor(rest[64:128, :], xdbl[64:128, :], parts[64:128, d, :], ALU.subtract).then_inc(split_step, 1)
                pool.wait_ge(split_step, 3 * q + 2 + LEAD)
                pool.sem_inc(PASSED[0], 1)
                nc.gpsimd.tensor_copy(second[64:128, :], rest[64:128, :]).then_inc(split_step, 1)
                pool.wait_ge(split_step, 3 * q + 3 + LEAD)
                pool.sem_inc(PASSED[0], 1)
                nc.gpsimd.tensor_copy(parts[64:96, d, :], rest[64:96, :]).then_inc(parts_ready, 1)
                pool.wait_ge(parts_ready, 2 * q + 1 + LEAD)
                pool.sem_inc(PASSED[0], 1)
                nc.gpsimd.tensor_tensor(parts[96:128, d, :], rest[96:128, :], second[96:128, :], ALU.subtract).then_inc(parts_ready, 1)
                pool.wait_ge(soft_ready, q + 1 + LEAD)
                pool.sem_inc(PASSED[0], 1)
                pool.wait_ge(parts_ready, 2 * q + 2 + LEAD)
                pool.sem_inc(PASSED[0], 1)
                pool.wait_ge(work_ready, (q - 2) * USES + 2 * FRONT + 1 + LEAD)
                pool.sem_inc(PASSED[0], 1)
                pool.wait_ge(dA_ready, 2 * NG * (q - 1) + LEAD)
                pool.sem_inc(PASSED[0], 1)
                nc.gpsimd.tensor_scalar(pre[:, :, :], pre[:, :, :], 0.0, -3e38, ALU.max, ALU.max).then_inc(delta_step, 1)
                pool.wait_ge(delta_step, 2 * q + 1 + LEAD)
                pool.sem_inc(PASSED[0], 1)
                nc.gpsimd.tensor_tensor(delta[:, d, :, :], pre[:, :, :], soft[:, :, :], ALU.add).then_inc(delta_step, 1)
                pool.wait_ge(delta_step, 2 * q + 2 + LEAD)
                pool.sem_inc(PASSED[0], 1)
                nc.gpsimd.tensor_tensor(du[:, d, :, :], delta[:, d, :, :], u[:, d, :, :], ALU.mult).then_inc(du_ready, 1)

            def out(t, d):
                pool.wait_ge(work_read, out_use(t, d)[0] + 1 + LEAD)
                pool.sem_inc(PASSED[0], 1)
                nc.gpsimd.tensor_tensor(X[:, cols(t)], X[:, cols(t)], outp[:, :], ALU.add).then_inc(added, 1)

            load(0, 0)
            front(0, 0)
            with pool.Fori(0, NT // 2 - 1) as pair:
                for s in range(2):
                    t = pair * 2 + s
                    load(t + 1, 1 - s)
                    front(t, 1)
                    out(t, 0)
                    front(t + 1, 0)
                    out(t, 1)
            load(NT - 1, 1)
            for t in (NT - 2, NT - 1):
                front(t, 1)
                out(t, 0)
                if t < NT - 1:
                    front(t + 1, 0)
                out(t, 1)

        @block.tensor
        def _(pe):
            pe.wait_ge(zeroed, 2 + LEAD)

            def claim(use):
                pos, bank = use
                pe.wait_ge(work_read, pos - 1 + LEAD)
                return work[bank]

            def convolve(t, s, d):
                pe.wait_ge(xpad_ready, t + 1 + LEAD)
                for h in range(HALVES):
                    to = by_seq(claim(front_use(t, d, h)))
                    for k in range(4):
                        at = k if d == 0 else 2 * PAD - k
                        last = nc.tensor.matmul(to, mem.conv_in[:, d, k, h * 128:(h + 1) * 128], xpad[:, s, :, at:at + S],
                                                start=(k == 0), stop=(k == 3))
                    last.then_inc(work_ready, 1)
                for h in range(HALVES):
                    to = by_seq(claim(front_use(t, d, 2 + h)))
                    nc.tensor.matmul(to, w["in_" + DIRS[d]][:, 256 + h * 128:256 + (h + 1) * 128], xpad[:, s, :, PAD:PAD + S],
                                     start=True, stop=True).then_inc(work_ready, 1)

            def project(t, d):
                to = claim(front_use(t, d, 4))
                pe.wait_ge(work_read, front_use(t, d, 1)[0] + 1 + LEAD)
                for h in range(HALVES):
                    last = nc.tensor.matmul(to, w["xp_" + DIRS[d]][:, h * 128:(h + 1) * 128], u[:, d, h, :],
                                            start=(h == 0), stop=(h == 1))
                last.then_inc(work_ready, 1)
                pe.wait_ge(work_read, front_use(t, d, 4)[0] + 1 + LEAD)
                for h in range(HALVES):
                    to = claim(front_use(t, d, 5 + h))
                    nc.tensor.matmul(to, w["dtp_" + DIRS[d]][0:RANK, h * 128:(h + 1) * 128], xdbl[0:RANK, :],
                                     start=True, stop=True).then_inc(work_ready, 1)

            def spread(t, d, g):
                q = 2 * t + d
                if g == 0:
                    pe.wait_ge(parts_ready, 2 * q + 2 + LEAD)
                pe.wait_ge(bu_ready, 2 * (NG * q + g) + LEAD)
                for n in range(GN):
                    last = nc.tensor.matmul(b_bc[:, n, :], mem.sel[:, GN * g + n, :], parts[:, d, :], start=True, stop=True)
                last.then_inc(b_ready, 1)
                pe.wait_ge(hc_ready, 2 * (NG * q + g) + LEAD)
                for n in range(GN):
                    last = nc.tensor.matmul(c_bc[:, n, :], mem.sel[:, NST + GN * g + n, :], parts[:, d, :], start=True, stop=True)
                last.then_inc(c_ready, 1)

            def reduce(t, d, g):
                q = 2 * t + d
                for h in range(HALVES):
                    if g == 0:
                        pe.wait_ge(y_step, 2 * q + LEAD)
                    pe.wait_ge(hc_ready, 2 * (NG * q + g) + h + 1 + LEAD)
                    for n in range(GN):
                        last = nc.tensor.matmul(ysum[h], mem.ident, hc[:, h, g % 2, n, :],
                                                start=(g == 0 and n == 0), stop=(g == NG - 1 and n == GN - 1))
                    last.then_inc(summed, 1)

            def out(t, d):
                to = claim(out_use(t, d))
                for h in range(HALVES):
                    pe.wait_ge(y_ready, 2 * (2 * t + d) + h + 1 + LEAD)
                    last = nc.tensor.matmul(to, mem.out_proj[:, d, h, :], du[:, d, h, :], start=(h == 0), stop=(h == 1))
                last.then_inc(work_ready, 1)

            def unit(t, s, d):
                has_next = not (isinstance(t, int) and t == NT - 1 and d == 1)
                for g in range(NG):
                    spread(t, d, g)
                    if g >= 1:
                        reduce(t, d, g - 1)
                    if has_next and g == 1:
                        convolve(t + d, (s + d) % 2, 1 - d)
                    if has_next and g == 3:
                        project(t + d, 1 - d)
                reduce(t, d, NG - 1)
                out(t, d)

            convolve(0, 0, 0)
            project(0, 0)
            with pe.Fori(0, NT // 2 - 1) as pair:
                for s in range(2):
                    unit(pair * 2 + s, s, 0)
                    unit(pair * 2 + s, s, 1)
            for t in (NT - 2, NT - 1):
                unit(t, t % 2, 0)
                unit(t, t % 2, 1)

        @block.scalar
        def _(act):
            act.wait_ge(zeroed, 2 + LEAD)

            def work_at(use):
                pos, bank = use
                act.wait_ge(work_ready, pos + 1 + LEAD)
                return work[bank]

            def gates(t, d):
                act.wait_ge(y_ready, 2 * (2 * t + d) - 2 + LEAD)
                act.wait_ge(du_ready, 2 * t + d - 1 + LEAD)
                for h in range(HALVES):
                    nc.scalar.activation(u[:, d, h, :], work_at(front_use(t, d, h)), ACT.Silu,
                                         bias=w["conv_b_" + DIRS[d]][:, h:h + 1]).then_inc(work_read, 1)
                for h in range(HALVES):
                    nc.scalar.activation(z[:, d, h, :], work_at(front_use(t, d, 2 + h)), ACT.Silu).then_inc(work_read, 1)

            def softplus(t, d):
                q = 2 * t + d
                src = work_at(front_use(t, d, 4))
                act.wait_ge(parts_ready, 2 * q + LEAD)
                nc.scalar.activation(xdbl[:, :], src, ACT.Identity).then_inc(work_read, 1)
                act.wait_ge(du_ready, q + LEAD)
                for h in range(HALVES):
                    nc.scalar.activation(pre[:, h, :], work_at(front_use(t, d, 5 + h)), ACT.Identity,
                                         bias=w["dtp_b_" + DIRS[d]][:, h:h + 1]).then_inc(work_read, 1)
                act.wait_ge(work_read, front_use(t, d, 6)[0] + 1 + LEAD)
                nc.scalar.activation(soft[:, :, :], pre[:, :, :], ACT.Abs).then_inc(soft_step, 1)
                nc.scalar.preload_act_table_set(LN_AND_EXP)
                act.wait_ge(soft_step, 2 * q + 1 + LEAD)
                nc.scalar.activation(soft[:, :, :], soft[:, :, :], ACT.Exp, scale=-1.0).then_inc(soft_step, 1)
                act.wait_ge(soft_step, 2 * q + 2 + LEAD)
                nc.scalar.activation(soft[:, :, :], soft[:, :, :], ACT.Ln, bias=mem.one, scale=1.0).then_inc(soft_ready, 1)

            def decay(t, d, g):
                q = 2 * t + d
                lo, hi = (1, S) if d == 0 else (0, S - 1)
                if g == 0:
                    act.wait_ge(du_ready, q + 1 + LEAD)
                for h in range(HALVES):
                    act.wait_ge(scanned, 2 * (NG * q + g) + h - 3 + LEAD)
                    for n in range(GN):
                        last = nc.scalar.activation(dA[:, d, h, g % 2, n, :, lo:hi], by_seq(delta[:, d, h, :])[:, :, lo:hi], ACT.Exp,
                                                    scale=mem.A[:, d, h * NST + GN * g + n:h * NST + GN * g + n + 1])
                    last.then_inc(dA_ready, 1)

            def out(t, d):
                src = work_at(out_use(t, d))
                act.wait_ge(added, 2 * t + d + LEAD)
                nc.scalar.activation(outp[:, :], src, ACT.Identity,
                                     bias=w["proj_b"] if d == 0 else mem.zero).then_inc(work_read, 1)

            def unit(t, d):
                has_next = not (isinstance(t, int) and t == NT - 1 and d == 1)
                for g in range(NG):
                    decay(t, d, g)
                    if has_next and g == 1:
                        gates(t + d, 1 - d)
                    if has_next and g == 3:
                        softplus(t + d, 1 - d)
                out(t, d)

            gates(0, 0)
            softplus(0, 0)
            with act.Fori(0, NT // 2 - 1) as pair:
                for s in range(2):
                    unit(pair * 2 + s, 0)
                    unit(pair * 2 + s, 1)
            for t in (NT - 2, NT - 1):
                unit(t, 0)
                unit(t, 1)

        @block.vector
        def _(dve):
            dve.wait_ge(zeroed, 2 + LEAD)

            def unit(t, d):
                q = 2 * t + d
                run = slice(None) if d == 0 else slice(None, None, -1)
                for g in range(NG):
                    G = NG * q + g
                    par = g % 2
                    if g == 0:
                        dve.wait_ge(du_ready, q + 1 + LEAD)
                    dve.wait_ge(b_ready, G + 1 + LEAD)
                    for h in range(HALVES):
                        dve.wait_ge(hc_ready, 2 * G + h - 1 + LEAD)
                        nc.vector.tensor_tensor(bu[:, h, :].rearrange("p (n t) -> p n t", n=GN), b_bc,
                                                du[:, d, h, :].unsqueeze(1).to_broadcast([D, GN, T]), ALU.mult).then_inc(bu_ready, 1)
                    for h in range(HALVES):
                        dve.wait_ge(dA_ready, 2 * G + h + 1 + LEAD)
                        dve.wait_ge(bu_ready, 2 * G + h + 1 + LEAD)
                        state = bu[:, h, :]
                        decay = dA[:, d, h, par, :, :, :].rearrange("p n b t -> p (n b t)")
                        nc.vector.tensor_tensor_scan(state[:, run], decay[:, run], state[:, run], 0.0,
                                                     ALU.mult, ALU.add).then_inc(scanned, 1)
                    dve.wait_ge(c_ready, G + 1 + LEAD)
                    for h in range(HALVES):
                        dve.wait_ge(summed, 2 * G + h - 3 + LEAD)
                        dve.wait_ge(scanned, 2 * G + h + 1 + LEAD)
                        nc.vector.tensor_tensor(hc[:, h, par, :, :], bu[:, h, :].rearrange("p (n t) -> p n t", n=GN),
                                                c_bc, ALU.mult).then_inc(hc_ready, 1)
                for h in range(HALVES):
                    dve.wait_ge(summed, 2 * NG * (q + 1) - 1 + h + LEAD)
                    nc.vector.scalar_tensor_tensor(du[:, d, h, :], u[:, d, h, :], w["D_" + DIRS[d]][:, h:h + 1], ysum[h],
                                                   ALU.mult, ALU.add).then_inc(y_step, 1)
                for h in range(HALVES):
                    dve.wait_ge(y_step, 2 * q + h + 1 + LEAD)
                    nc.vector.tensor_tensor(du[:, d, h, :], du[:, d, h, :], z[:, d, h, :], ALU.mult).then_inc(y_ready, 1)

            with dve.Fori(0, NT // 2) as pair:
                for s in range(2):
                    unit(pair * 2 + s, 0)
                    unit(pair * 2 + s, 1)


SUB = T // 128
NB = TOK // 128


def top2_weights(nc, stage, mem, logits, comb):
    with ExitStack() as ctx:
        def sb(name, *shape):
            return ctx.enter_context(nc.sbuf_tensor(stage + "_" + name, [128, *shape], F32))
        beats = sb("beats", NB, NE, NE)
        ties = sb("ties", NB, NE, NE)
        rank = sb("rank", NB, NE)
        top = sb("top", NB)
        total = sb("total", NB)
        inverse = sb("inverse", NB)
        (top_ready, centered, gt_ready, eq_ready, tie_ready, beats_ready, rank_ready, chosen, powers, weighed, summed, inverted, done
         ) = ctx.enter_context(signals(nc, stage, "top", "centered", "gt", "eq", "tie", "beats", "rank", "chosen", "powers",
                                       "weighed", "summed", "inverted", "done"))
        block = ctx.enter_context(nc.Block())
        of_f = logits.unsqueeze(2).to_broadcast([128, NB, NE, NE])
        of_e = logits.unsqueeze(3).to_broadcast([128, NB, NE, NE])

        @block.vector
        def _(dve):
            nc.vector.tensor_reduce(top[:, :], logits, AX_X, ALU.max).then_inc(top_ready, 1)
            nc.vector.tensor_tensor(beats[:, :, :, :], of_f, of_e, ALU.is_gt).then_inc(gt_ready, 1)
            dve.wait_ge(top_ready, 1 + LEAD)
            nc.vector.tensor_tensor(comb, logits, top[:, :].unsqueeze(2).to_broadcast([128, NB, NE]), ALU.subtract).then_inc(centered, 1)
            nc.vector.tensor_tensor(ties[:, :, :, :], of_f, of_e, ALU.is_equal).then_inc(eq_ready, 1)
            dve.wait_ge(eq_ready, 1 + LEAD)
            earlier = mem.const["earlier"].rearrange("p (e f) -> p e f", e=NE).unsqueeze(1).to_broadcast([128, NB, NE, NE])
            nc.vector.tensor_tensor(ties[:, :, :, :], ties[:, :, :, :], earlier, ALU.mult).then_inc(tie_ready, 1)
            dve.wait_ge(tie_ready, 1 + LEAD)
            dve.wait_ge(gt_ready, 1 + LEAD)
            nc.vector.tensor_tensor(beats[:, :, :, :], beats[:, :, :, :], ties[:, :, :, :], ALU.add).then_inc(beats_ready, 1)
            dve.wait_ge(beats_ready, 1 + LEAD)
            nc.vector.tensor_reduce(rank[:, :, :], beats[:, :, :, :], AX_X, ALU.add).then_inc(rank_ready, 1)
            dve.wait_ge(rank_ready, 1 + LEAD)
            nc.vector.tensor_scalar(rank[:, :, :], rank[:, :, :], 1.5, None, ALU.is_lt).then_inc(chosen, 1)
            dve.wait_ge(chosen, 1 + LEAD)
            dve.wait_ge(powers, 1 + LEAD)
            nc.vector.tensor_tensor(comb, comb, rank[:, :, :], ALU.mult).then_inc(weighed, 1)
            dve.wait_ge(weighed, 1 + LEAD)
            nc.vector.tensor_reduce(total[:, :], comb, AX_X, ALU.add).then_inc(summed, 1)
            dve.wait_ge(summed, 1 + LEAD)
            nc.vector.reciprocal(inverse[:, :], total[:, :]).then_inc(inverted, 1)
            dve.wait_ge(inverted, 1 + LEAD)
            nc.vector.tensor_tensor(comb, comb, inverse[:, :].unsqueeze(2).to_broadcast([128, NB, NE]), ALU.mult).then_inc(done, 1)

        @block.scalar
        def _(act):
            act.wait_ge(centered, 1 + LEAD)
            nc.scalar.activation(comb, comb, ACT.Exp).then_inc(powers, 1)


def l0_weights(nc, mem):
    w = mem.w
    with ExitStack() as ctx:
        (biased, done) = ctx.enter_context(signals(nc, "l0w", "biased", "done"))
        block = ctx.enter_context(nc.Block())

        @block.tensor
        def _(pe):
            nc.tensor.matmul(mem.bank[0][:, 0:1], w["pw"], w["dw_bias"], start=True, stop=True).then_inc(biased, 1)

        @block.vector
        def _(dve):
            for k in range(3):
                nc.vector.tensor_scalar(mem.pw_taps[:, k, :], w["pw"], w["dw"][:, k:k + 1], None, ALU.mult)
            dve.wait_ge(biased, 1 + LEAD)
            nc.vector.tensor_tensor(mem.pw_bias[:, :], mem.bank[0][:, 0:1], w["pw_b"], ALU.add).then_inc(done, 1)


def l0_mixer(nc, stage, mem, U, logits):
    w = mem.w
    with ExitStack() as ctx:
        def sb(name, *shape):
            return ctx.enter_context(nc.sbuf_tensor(stage + "_" + name, [D, *shape], F32))
        upad = sb("upad", 2, SEQ_T, 2 + S)
        act_c = sb("c", 2, T)
        x1 = sb("x1", 2, T)
        (zeroed, padded, conv_ready, c_ready, x1_ready, stored, logits_ready, logits_read) = ctx.enter_context(signals(
            nc, stage, "zeroed", "padded", "conv", "c", "x1", "stored", "logits", "logits_read"))
        block = ctx.enter_context(nc.Block())

        @block.gpsimd
        def _(pool):
            nc.gpsimd.memset(upad[:, :, :, :], 0.0).then_inc(zeroed, 1)
            pool.wait_ge(zeroed, 1 + LEAD)

            def pad(t, s):
                pool.wait_ge(conv_ready, t - 1 + LEAD)
                pool.sem_inc(PASSED[0], 1)
                nc.gpsimd.tensor_copy(upad[:, s, :, 2:2 + S], U[:, cols(t)].rearrange("p (b t) -> p b t", b=SEQ_T)).then_inc(padded, 1)
            tile_pairs(pool, pad)

        @block.tensor
        def _(pe):
            def conv(t, s):
                pe.wait_ge(padded, t + 1 + LEAD)
                pe.wait_ge(c_ready, t - 1 + LEAD)
                for k in range(3):
                    last = nc.tensor.matmul(mem.bank[s].rearrange("p (b t) -> p b t", b=SEQ_T), mem.pw_taps[:, k, :],
                                            upad[:, s, :, k:k + S], start=(k == 0), stop=(k == 2))
                last.then_inc(conv_ready, 1)

            def route(t, s):
                pe.wait_ge(x1_ready, t + 1 + LEAD)
                pe.wait_ge(logits_read, t - 1 + LEAD)
                for j in range(SUB):
                    last = nc.tensor.matmul(mem.bank[2 + s][:, j * NE:(j + 1) * NE], x1[:, s, j * 128:(j + 1) * 128], w["router"],
                                            start=True, stop=True)
                last.then_inc(logits_ready, 1)

            conv(0, 0)
            with pe.Fori(0, NT // 2 - 1) as pair:
                for s in range(2):
                    conv(pair * 2 + s + 1, 1 - s)
                    route(pair * 2 + s, s)
            conv(NT - 1, 1)
            route(NT - 2, 0)
            route(NT - 1, 1)

        @block.scalar
        def _(act):
            def silu(t, s):
                act.wait_ge(x1_ready, t - 1 + LEAD)
                act.wait_ge(conv_ready, t + 1 + LEAD)
                nc.scalar.activation(act_c[:, s, :], mem.bank[s], ACT.Silu, bias=mem.pw_bias[:, :]).then_inc(c_ready, 1)

            def store(t, s):
                act.wait_ge(x1_ready, t + 1 + LEAD)
                act.sem_inc(PASSED[0], 1)
                nc.scalar.activation(U[:, cols(t)], x1[:, s, :], ACT.Identity).then_inc(stored, 1)

            silu(0, 0)
            with act.Fori(0, NT // 2 - 1) as pair:
                for s in range(2):
                    silu(pair * 2 + s + 1, 1 - s)
                    store(pair * 2 + s, s)
            silu(NT - 1, 1)
            store(NT - 2, 0)
            store(NT - 1, 1)

        @block.vector
        def _(dve):
            def add(t, s):
                dve.wait_ge(c_ready, t + 1 + LEAD)
                dve.wait_ge(logits_ready, t - 1 + LEAD)
                dve.wait_ge(stored, t - 1 + LEAD)
                nc.vector.tensor_tensor(x1[:, s, :], act_c[:, s, :], U[:, cols(t)], ALU.add).then_inc(x1_ready, 1)

            def take_logits(t, s):
                dve.wait_ge(logits_ready, t + 1 + LEAD)
                bias = w["router_b"].unsqueeze(1).to_broadcast([128, SUB, NE])
                nc.vector.tensor_tensor(logits[:, bass.ds(t * SUB, SUB), :], mem.bank[2 + s][:, 0:SUB * NE].rearrange("p (j e) -> p j e", j=SUB),
                                        bias, ALU.add).then_inc(logits_read, 1)

            add(0, 0)
            with dve.Fori(0, NT // 2 - 1) as pair:
                for s in range(2):
                    add(pair * 2 + s + 1, 1 - s)
                    take_logits(pair * 2 + s, s)
            add(NT - 1, 1)
            take_logits(NT - 2, 0)
            take_logits(NT - 1, 1)


def l0_experts(nc, stage, mem, U, comb):
    w = mem.w
    with ExitStack() as ctx:
        def sb(name, *shape):
            return ctx.enter_context(nc.sbuf_tensor(stage + "_" + name, [D, *shape], F32))
        tile_comb = sb("tile_comb", 2, SUB, NE)
        ye = sb("ye", 2, T)
        weighed = sb("weighed", 2, T)
        total = sb("total", 2, T)
        (comb_ready, ye_ready, expert_ready, spread_ready, weighed_ready, summed, out_ready, out_read) = ctx.enter_context(signals(
            nc, stage, "comb", "ye", "expert", "spread", "weighed", "summed", "out", "out_read"))
        block = ctx.enter_context(nc.Block())

        @block.gpsimd
        def _(pool):
            def step(t, s):
                pool.wait_ge(spread_ready, NE * (t - 1) + LEAD)
                pool.sem_inc(PASSED[0], 1)
                nc.gpsimd.tensor_copy(tile_comb[:, s, :, :], comb[:, bass.ds(t * SUB, SUB), :]).then_inc(comb_ready, 1)
                pool.wait_ge(out_ready, t - 1 + LEAD)
                pool.sem_inc(PASSED[0], 1)
                for e in range(NE):
                    pool.wait_ge(weighed_ready, NE * t + e + 1 + LEAD)
                    pool.sem_inc(PASSED[0], 1)
                    if e == 0:
                        nc.gpsimd.tensor_copy(total[:, s, :], weighed[:, 0, :]).then_inc(summed, 1)
                    else:
                        pool.wait_ge(summed, NE * t + e + LEAD)
                        pool.sem_inc(PASSED[0], 1)
                        nc.gpsimd.tensor_tensor(total[:, s, :], total[:, s, :], weighed[:, e % 2, :], ALU.add).then_inc(summed, 1)
            tile_pairs(pool, step)

        @block.tensor
        def _(pe):
            def experts(t, s, before=None):
                pe.wait_ge(comb_ready, t + 1 + LEAD)
                for e in range(NE):
                    pe.wait_ge(ye_ready, NE * t + e - 1 + LEAD)
                    nc.tensor.matmul(mem.bank[e % 2], w["experts"][:, e * D:(e + 1) * D], U[:, cols(t)], start=True, stop=True).then_inc(expert_ready, 1)
                    pe.wait_ge(weighed_ready, NE * t + e - 1 + LEAD)
                    for j in range(SUB):
                        last = nc.tensor.matmul(mem.bank[2 + e % 2][:, j * 128:(j + 1) * 128],
                                                tile_comb[:, s, j, e:e + 1].to_broadcast([128, 128]), mem.ident, start=True, stop=True)
                    last.then_inc(spread_ready, 1)
                    if e == 2 and before is not None:
                        project(before, 1 - s)

            def project(t, s):
                pe.wait_ge(summed, NE * (t + 1) + LEAD)
                pe.wait_ge(out_read, t - 1 + LEAD)
                nc.tensor.matmul(mem.bank[4 + s], w["out"], total[:, s, :], start=True, stop=True).then_inc(out_ready, 1)

            experts(0, 0)
            experts(1, 1, before=0)
            with pe.Fori(1, NT // 2) as pair:
                for s in range(2):
                    experts(pair * 2 + s, s, before=pair * 2 + s - 1)
            project(NT - 1, 1)

        @block.scalar
        def _(act):
            def step(t, s):
                for e in range(NE):
                    act.wait_ge(expert_ready, NE * t + e + 1 + LEAD)
                    act.wait_ge(weighed_ready, NE * t + e - 1 + LEAD)
                    nc.scalar.activation(ye[:, e % 2, :], mem.bank[e % 2], ACT.Silu, bias=w["expert_b"][:, e:e + 1]).then_inc(ye_ready, 1)
            tile_pairs(act, step)

        @block.vector
        def _(dve):
            def experts(t, s, before=None):
                for e in range(NE):
                    dve.wait_ge(ye_ready, NE * t + e + 1 + LEAD)
                    dve.wait_ge(spread_ready, NE * t + e + 1 + LEAD)
                    dve.wait_ge(summed, NE * t + e - 1 + LEAD)
                    nc.vector.tensor_tensor(weighed[:, e % 2, :], ye[:, e % 2, :], mem.bank[2 + e % 2], ALU.mult).then_inc(weighed_ready, 1)
                    if e == 4 and before is not None:
                        finish(before, 1 - s)

            def finish(t, s):
                dve.wait_ge(out_ready, t + 1 + LEAD)
                dve.wait_ge(expert_ready, NE * (t + 1) + LEAD)
                nc.vector.scalar_tensor_tensor(U[:, cols(t)], mem.bank[4 + s], w["out_b"], U[:, cols(t)], ALU.add, ALU.add).then_inc(out_read, 1)

            experts(0, 0)
            experts(1, 1, before=0)
            with dve.Fori(1, NT // 2) as pair:
                for s in range(2):
                    experts(pair * 2 + s, s, before=pair * 2 + s - 1)
            finish(NT - 1, 1)


def rms_norm(nc, stage, mem, U, weight):
    with ExitStack() as ctx:
        def sb(name, *shape):
            return ctx.enter_context(nc.sbuf_tensor(stage + "_" + name, [D, *shape], F32))
        sq, logv, rstd = sb("sq", 2, T), sb("logv", 2, T), sb("rstd", 2, T)
        (squared, var_ready, log_done, rstd_ready, scaled) = ctx.enter_context(signals(
            nc, stage, "squared", "var", "log", "rstd", "scaled"))
        block = ctx.enter_context(nc.Block())

        @block.gpsimd
        def _(pool):
            def square(t, s):
                pool.wait_ge(var_ready, t - 1 + LEAD)
                pool.sem_inc(PASSED[0], 1)
                nc.gpsimd.tensor_tensor(sq[:, s, :], U[:, cols(t)], U[:, cols(t)], ALU.mult).then_inc(squared, 1)
            tile_pairs(pool, square)

        @block.tensor
        def _(pe):
            def mean(t, s):
                pe.wait_ge(squared, t + 1 + LEAD)
                pe.wait_ge(log_done, t - 1 + LEAD)
                nc.tensor.matmul(mem.bank[s], mem.avg, sq[:, s, :], start=True, stop=True).then_inc(var_ready, 1)
            tile_pairs(pe, mean)

        @block.scalar
        def _(act):
            def rsqrt(t, s):
                act.wait_ge(var_ready, t + 1 + LEAD)
                act.wait_ge(scaled, t - 1 + LEAD)
                nc.scalar.activation(logv[:, s, :], mem.bank[s], ACT.Ln, bias=mem.const["eps6"], scale=1.0).then_inc(log_done, 1)
                act.wait_ge(log_done, t + 1 + LEAD)
                nc.scalar.activation(rstd[:, s, :], logv[:, s, :], ACT.Exp, scale=-0.5).then_inc(rstd_ready, 1)
            nc.scalar.preload_act_table_set(LN_AND_EXP)
            tile_pairs(act, rsqrt)

        @block.vector
        def _(dve):
            def scale(t, s):
                dve.wait_ge(rstd_ready, t + 1 + LEAD)
                nc.vector.scalar_tensor_tensor(U[:, cols(t)], U[:, cols(t)], weight, rstd[:, s, :], ALU.mult, ALU.mult).then_inc(scaled, 1)
            tile_pairs(dve, scale)


def l0_feed_forward(nc, stage, mem, X, U):
    w = mem.w
    with ExitStack() as ctx:
        g = ctx.enter_context(nc.sbuf_tensor(stage + "_g", [HID, 2, T], F32))
        branch = ctx.enter_context(nc.sbuf_tensor(stage + "_branch", [D, 2, T], F32))
        (down_ready, g_ready, up_ready, branch_ready, added) = ctx.enter_context(signals(
            nc, stage, "down", "g", "up", "branch", "added"))
        block = ctx.enter_context(nc.Block())

        @block.tensor
        def _(pe):
            def down(t, s):
                pe.wait_ge(g_ready, t - 1 + LEAD)
                nc.tensor.matmul(mem.bank[s][0:HID, :], w["down"], U[:, cols(t)], start=True, stop=True,
                                 ).then_inc(down_ready, 1)

            def up(t, s):
                pe.wait_ge(g_ready, t + 1 + LEAD)
                pe.wait_ge(branch_ready, t - 1 + LEAD)
                nc.tensor.matmul(mem.bank[2 + s], w["up"], g[:, s, :], start=True, stop=True).then_inc(up_ready, 1)

            down(0, 0)
            with pe.Fori(0, NT // 2 - 1) as pair:
                for s in range(2):
                    down(pair * 2 + s + 1, 1 - s)
                    up(pair * 2 + s, s)
            down(NT - 1, 1)
            up(NT - 2, 0)
            up(NT - 1, 1)

        @block.scalar
        def _(act):
            def gelu(t, s):
                act.wait_ge(down_ready, t + 1 + LEAD)
                act.wait_ge(up_ready, t - 1 + LEAD)
                nc.scalar.activation(g[:, s, :], mem.bank[s][0:HID, :], ACT.Gelu, bias=w["down_b"]).then_inc(g_ready, 1)
            tile_pairs(act, gelu)

        @block.vector
        def _(dve):
            def add(t, s):
                dve.wait_ge(up_ready, t + 1 + LEAD)
                dve.wait_ge(added, t - 1 + LEAD)
                nc.vector.scalar_tensor_tensor(branch[:, s, :], mem.bank[2 + s], w["up_b"], U[:, cols(t)], ALU.add, ALU.add).then_inc(branch_ready, 1)
                dve.wait_ge(branch_ready, t + 1 + LEAD)
                nc.vector.tensor_tensor(X[:, cols(t)], X[:, cols(t)], branch[:, s, :], ALU.add).then_inc(added, 1)
            tile_pairs(dve, add)


def l0_ffn(nc, stage, mem, X, U):
    with ExitStack() as ctx:
        logits = ctx.enter_context(nc.sbuf_tensor(stage + "_logits", [128, NB, NE], F32))
        comb = ctx.enter_context(nc.sbuf_tensor(stage + "_comb", [128, NB, NE], F32))
        layer_norm(nc, stage + "_ln", mem, X, U)
        l0_mixer(nc, stage + "_mix", mem, U, logits)
        top2_weights(nc, stage + "_top2", mem, logits[:, :, :], comb[:, :, :])
        l0_experts(nc, stage + "_moe", mem, U, comb)
        rms_norm(nc, stage + "_rms", mem, U, mem.w["norm_w"])
        l0_feed_forward(nc, stage + "_ff", mem, X, U)


STEPS = T // NSEQ


def rnn(nc, mem, U, H):
    w = mem.w
    with ExitStack() as ctx:
        (input_ready, pre_ready, h_ready) = ctx.enter_context(signals(nc, "rnn", "input", "pre", "h"))
        start = ctx.enter_context(nc.sbuf_tensor("rnn_start", [D, NSEQ], F32))
        h = ctx.enter_context(nc.sbuf_tensor("rnn_h", [D, 2, STEPS, NSEQ], F32))
        (kept,) = ctx.enter_context(signals(nc, "rnn_keep", "kept"))
        block = ctx.enter_context(nc.Block())
        by_time = U[:, :].rearrange("p (b t) -> p t b", b=NSEQ)
        NCH = S // STEPS

        @block.tensor
        def _(pe):
            def inputs(c, par):
                nc.tensor.matmul(mem.bank[par].rearrange("p (t b) -> p t b", b=NSEQ), w["rnn_B"],
                                 by_time[:, bass.ds(c * STEPS, STEPS), :], start=True, stop=False, skip_group_check=True)

            def chunk(c, par, more):
                for k in range(STEPS):
                    if k == STEPS // 2 and more:
                        pe.wait_ge(h_ready, STEPS * c + 1 + LEAD)
                        inputs(c + 1, 1 - par)
                    first = isinstance(c, int) and c == 0 and k == 0
                    if not first:
                        pe.wait_ge(h_ready, STEPS * c + k + LEAD)
                    before = start[:, :] if first else (h[:, par, k - 1, :] if k else h[:, 1 - par, STEPS - 1, :])
                    nc.tensor.matmul(mem.bank[par][:, k * NSEQ:(k + 1) * NSEQ], w["rnn_A"], before, start=False, stop=True,
                                     skip_group_check=True).then_inc(pre_ready, 1)

            pe.wait_ge(input_ready, 1 + LEAD)
            inputs(0, 0)
            chunk(0, 0, True)
            chunk(1, 1, True)
            with pe.Fori(1, NCH // 2 - 1) as pair:
                for par in range(2):
                    chunk(pair * 2 + par, par, True)
            chunk(NCH - 2, 0, True)
            chunk(NCH - 1, 1, False)

        @block.scalar
        def _(act):
            def chunk(c, par):
                for k in range(STEPS):
                    if k == 0:
                        act.wait_ge(kept, c - 1 + LEAD)
                    act.wait_ge(pre_ready, STEPS * c + k + 1 + LEAD)
                    nc.scalar.activation(h[:, par, k, :], mem.bank[par][:, k * NSEQ:(k + 1) * NSEQ], ACT.Tanh).then_inc(h_ready, 1)
            with act.Fori(0, NCH // 2) as pair:
                for par in range(2):
                    chunk(pair * 2 + par, par)

        @block.vector
        def _(dve):
            nc.vector.memset(start[:, :], 0.0).then_inc(input_ready, 1)
            h_by_time = H[:, :].rearrange("p (b t) -> p t b", b=NSEQ)
            with dve.Fori(0, NCH // 2) as pair:
                for par in range(2):
                    c = pair * 2 + par
                    dve.wait_ge(h_ready, STEPS * c + STEPS + LEAD)
                    nc.vector.tensor_scalar(h_by_time[:, bass.ds(c * STEPS, STEPS), :], h[:, par, :, :], 1.0, None, ALU.mult).then_inc(kept, 1)


def project_add(nc, stage, mem, weight, src, dst, bias=None):
    with ExitStack() as ctx:
        (ready, added) = ctx.enter_context(signals(nc, stage, "ready", "added"))
        block = ctx.enter_context(nc.Block())

        @block.tensor
        def _(pe):
            def step(t, s):
                pe.wait_ge(added, t - 1 + LEAD)
                nc.tensor.matmul(mem.bank[s], weight, src[:, cols(t)], start=True, stop=True).then_inc(ready, 1)
            tile_pairs(pe, step)

        @block.vector
        def _(dve):
            def step(t, s):
                dve.wait_ge(ready, t + 1 + LEAD)
                if bias is None:
                    nc.vector.tensor_tensor(dst[:, cols(t)], dst[:, cols(t)], mem.bank[s], ALU.add).then_inc(added, 1)
                else:
                    nc.vector.scalar_tensor_tensor(dst[:, cols(t)], mem.bank[s], bias, dst[:, cols(t)], ALU.add, ALU.add).then_inc(added, 1)
            tile_pairs(dve, step)


def add_all(nc, stage, mem, src, dst):
    with ExitStack() as ctx:
        (added,) = ctx.enter_context(signals(nc, stage, "added"))
        block = ctx.enter_context(nc.Block())

        @block.vector
        def _(dve):
            def step(t, s):
                nc.vector.tensor_tensor(dst[:, cols(t)], dst[:, cols(t)], src[:, cols(t)], ALU.add).then_inc(added, 1)
            tile_pairs(dve, step)


def recurrent(nc, mem, X, U):
    layer_norm(nc, "rnn_ln", mem, X, U)
    with nc.sbuf_tensor("H", [D, TOK], F32) as H:
        rnn(nc, mem, U, H)
        project_add(nc, "rnn_out", mem, mem.w["rnn_C"], H, U)
        layer_norm(nc, "rnn_ln2", mem, U, H, affine=(mem.w["rnn_gamma"], mem.w["rnn_beta"]))
        add_all(nc, "rnn_add", mem, H, X)


F = 512
CH = F // 128
LIMIT = 10.0


def l1_router(nc, stage, mem, U, logits):
    w = mem.w
    with ExitStack() as ctx:
        x = ctx.enter_context(nc.sbuf_tensor(stage + "_x", [D, 2, T], F32))
        (copied, logits_ready, logits_read) = ctx.enter_context(signals(nc, stage, "copied", "logits", "logits_read"))
        block = ctx.enter_context(nc.Block())

        @block.scalar
        def _(act):
            def step(t, s):
                act.wait_ge(logits_ready, t - 1 + LEAD)
                act.sem_inc(PASSED[0], 1)
                nc.scalar.activation(x[:, s, :], U[:, cols(t)], ACT.Identity).then_inc(copied, 1)
            tile_pairs(act, step)

        @block.tensor
        def _(pe):
            def step(t, s):
                pe.wait_ge(copied, t + 1 + LEAD)
                pe.wait_ge(logits_read, t - 1 + LEAD)
                for j in range(SUB):
                    last = nc.tensor.matmul(mem.bank[s][:, j * NE:(j + 1) * NE], x[:, s, j * 128:(j + 1) * 128], w["l1_router"],
                                            start=True, stop=True)
                last.then_inc(logits_ready, 1)
            tile_pairs(pe, step)

        @block.vector
        def _(dve):
            def step(t, s):
                dve.wait_ge(logits_ready, t + 1 + LEAD)
                dve.sem_inc(PASSED[0], 1)
                nc.vector.tensor_copy(logits[:, bass.ds(t * SUB, SUB), :], mem.bank[s][:, 0:SUB * NE].rearrange("p (j e) -> p j e", j=SUB)).then_inc(logits_read, 1)
            tile_pairs(dve, step)


def split_comb(nc, dve, comb, rest, parts, split):
    nc.vector.tensor_copy(parts[:, :, 0:NE], comb).then_inc(split, 1)
    dve.wait_ge(split, 1 + LEAD)
    nc.vector.tensor_tensor(rest, comb, parts[:, :, 0:NE], ALU.subtract).then_inc(split, 1)
    dve.wait_ge(split, 2 + LEAD)
    nc.vector.tensor_copy(parts[:, :, NE:2 * NE], rest).then_inc(split, 1)
    dve.wait_ge(split, 3 + LEAD)
    nc.vector.tensor_tensor(parts[:, :, 2 * NE:3 * NE], rest, parts[:, :, NE:2 * NE], ALU.subtract).then_inc(split, 1)


def tiles_with_next(eng, step):
    step(0, 0, False)
    with eng.Fori(0, NT // 2 - 1) as pair:
        step(pair * 2 + 1, 1, False)
        step(pair * 2 + 2, 0, False)
    step(NT - 1, 1, True)


def l1_experts(nc, stage, mem, X, U, comb):
    NCHUNK = NE * CH + 1
    with ExitStack() as ctx:
        def sb(name, *shape, dt=F32):
            return ctx.enter_context(nc.sbuf_tensor(stage + "_" + name, [D, *shape], dt))
        parts = sb("parts", NB, 3 * NE, dt=BF16)
        tile_parts = sb("tile_parts", SUB, 3 * NE, dt=BF16)
        rows = sb("rows", 2, T, dt=BF16)
        x = sb("x", 2, 2, T, dt=F32R)
        weighed = sb("weighed", T)
        xw = sb("xw", 2, 2, T, dt=F32R)
        act = sb("act", 3, T)
        hidden = sb("hidden", 2, 2, T, dt=F32R)
        (split, parts_copied, turned, rows_ready, spread_ready, weighed_ready, xw_high, xw_ready, x_high, x_ready, gate_ready, clipped,
         silu_ready, up_ready, multiplied, high_ready, low_ready, down_done, added) = ctx.enter_context(signals(
             nc, stage, "split", "parts_copied", "turned", "rows", "spread", "weighed", "xw_high", "xw", "x_high", "x", "gate", "clipped",
             "silu", "up", "multiplied", "high", "low", "down", "added"))
        block = ctx.enter_context(nc.Block())
        where = mem.moe_where

        def at(t, s, c):
            if c < 0:
                return t - 1, 1 - s, c + NCHUNK
            if c >= NCHUNK:
                return t + 1, 1 - s, c - NCHUNK
            return t, s, c

        def parity(s, c):
            return (s + c) % 2

        def number(t, c):
            return NCHUNK * t + c

        def next_expert(t, s, c):
            e = c // CH + 1
            return (t, s, e) if e < NE else (t + 1, 1 - s, 0)

        def weighs(c, last):
            return c % CH == 1 and c < NE * CH and not (last and c // CH + 1 == NE)

        def chunk_weights(c, kind):
            if c == NCHUNK - 1:
                lo = where["shared_" + kind][1]
            elif kind == "down":
                lo = where["l1_down"][1] + c * D
            else:
                lo = where["gate_up"][1] + c // CH * 2 * F + (F if kind == "up" else 0) + c % CH * 128
            return mem.w_high[:, lo:lo + 128], mem.w_low[:, lo:lo + 128]

        @block.gpsimd
        def _(pool):
            def split_x(t, s):
                pool.wait_ge(up_ready, NCHUNK * (t - 1) + LEAD)
                pool.sem_inc(PASSED[0], 1)
                nc.gpsimd.tensor_copy(x[:, s, 0, :], U[:, cols(t)]).then_inc(x_high, 1)
                pool.wait_ge(x_high, t + 1 + LEAD)
                pool.sem_inc(PASSED[0], 1)
                nc.gpsimd.tensor_tensor(x[:, s, 1, :], U[:, cols(t)], x[:, s, 0, :], ALU.subtract).then_inc(x_ready, 1)

            def copy_parts(t):
                pool.wait_ge(turned, t + LEAD)
                pool.sem_inc(PASSED[0], 1)
                nc.gpsimd.tensor_copy(tile_parts[:, :, :], parts[:, bass.ds(t * SUB, SUB), :]).then_inc(parts_copied, 1)

            def xw_low(t, e):
                pool.wait_ge(xw_high, NE * t + e + 1 + LEAD)
                pool.sem_inc(PASSED[0], 1)
                nc.gpsimd.tensor_tensor(xw[:, e % 2, 1, :], weighed[:, :], xw[:, e % 2, 0, :], ALU.subtract).then_inc(xw_ready, 1)

            def low(t, s, c):
                pool.wait_ge(high_ready, number(t, c) + 1 + LEAD)
                pool.sem_inc(PASSED[0], 1)
                nc.gpsimd.tensor_tensor(hidden[:, parity(s, c), 1, :], act[:, c % 3, :], hidden[:, parity(s, c), 0, :],
                                        ALU.subtract).then_inc(low_ready, 1)

            def tile(t, s, last):
                for c in range(NCHUNK):
                    low(t, s, c)
                    if weighs(c, last):
                        nt, ns, e = next_expert(t, s, c)
                        xw_low(nt, e)
                    if c == 14 and not last:
                        copy_parts(t + 1)
                    if c == 18 and not last:
                        split_x(t + 1, 1 - s)

            pool.wait_ge(split, 4 + LEAD)
            copy_parts(0)
            split_x(0, 0)
            xw_low(0, 0)
            tiles_with_next(pool, tile)

        @block.tensor
        def _(pe):
            def product(to, weights, x, start=True, stop=True):
                nc.tensor.matmul(to, weights[0], x[:, 0, :], start=start, stop=False)
                nc.tensor.matmul(to, weights[0], x[:, 1, :], start=False, stop=False)
                return nc.tensor.matmul(to, weights[1], x[:, 0, :], start=False, stop=stop)

            def turn(t, s):
                pe.wait_ge(parts_copied, t + 1 + LEAD)
                pe.wait_ge(rows_ready, t + LEAD)
                pe.sem_inc(PASSED[0], 1)
                for j in range(SUB):
                    last = nc.tensor.matmul(mem.bank[7][0:3 * NE, j * 128:(j + 1) * 128], tile_parts[:, j, :], mem.ident16, start=True, stop=True)
                last.then_inc(turned, 1)

            def spread(t, s, e):
                pe.wait_ge(rows_ready, t + 1 + LEAD)
                pe.wait_ge(weighed_ready, NE * t + e + LEAD)
                pe.sem_inc(PASSED[0], 1)
                nc.tensor.matmul(mem.bank[4], mem.one_hot[0:3 * NE, e:e + 1].to_broadcast([3 * NE, 128]), rows[0:3 * NE, s, :],
                                 start=True, stop=True).then_inc(spread_ready, 1)

            def gate(t, s, c):
                if c == 0:
                    pe.wait_ge(x_ready, t + 1 + LEAD)
                pe.wait_ge(clipped, number(t, c) - 1 + LEAD)
                product(mem.bank[parity(s, c)], chunk_weights(c, "gate"), x[:, s, :, :]).then_inc(gate_ready, 1)

            def up(t, s, c):
                if c % CH == 0 and c < NE * CH:
                    pe.wait_ge(xw_ready, NE * t + c // CH + 1 + LEAD)
                pe.wait_ge(multiplied, number(t, c) - 1 + LEAD)
                product(mem.bank[2 + parity(s, c)], chunk_weights(c, "up"),
                        xw[:, c // CH % 2, :, :] if c < NE * CH else x[:, s, :, :]).then_inc(up_ready, 1)

            def down(t, s, c):
                if c == 0:
                    pe.wait_ge(added, t - 1 + LEAD)
                pe.wait_ge(low_ready, number(t, c) + 1 + LEAD)
                product(mem.bank[5 + s], chunk_weights(c, "down"), hidden[:, parity(s, c), :, :],
                        start=(c == 0), stop=(c == NCHUNK - 1)).then_inc(down_done, 1)

            def tile(t, s, last):
                for c in range(NCHUNK):
                    if not (last and c == NCHUNK - 1):
                        gate(*at(t, s, c + 1))
                    up(t, s, c)
                    if weighs(c, last):
                        spread(*next_expert(t, s, c))
                    if c == 22 and not last:
                        turn(t + 1, 1 - s)
                    if c >= 2 or not isinstance(t, int) or t > 0:
                        down(*at(t, s, c - 2))

            turn(0, 0)
            spread(0, 0, 0)
            gate(0, 0, 0)
            tiles_with_next(pe, tile)
            down(NT - 1, 1, NCHUNK - 2)
            down(NT - 1, 1, NCHUNK - 1)

        @block.scalar
        def _(scalar):
            def take_rows(t, s):
                scalar.wait_ge(turned, t + 1 + LEAD)
                scalar.wait_ge(spread_ready, NE * (t - 1) + LEAD)
                nc.scalar.activation(rows[0:3 * NE, s, :], mem.bank[7][0:3 * NE, :], ACT.Identity).then_inc(rows_ready, 1)

            def take_xw_high(t, s, e):
                used = NCHUNK * t + CH * (e - 1) if e >= 2 else NCHUNK * (t - 1) + CH * (e + NE - 1)
                scalar.wait_ge(weighed_ready, NE * t + e + 1 + LEAD)
                scalar.wait_ge(up_ready, used + LEAD)
                nc.scalar.activation(xw[:, e % 2, 0, :], weighed[:, :], ACT.Identity).then_inc(xw_high, 1)

            def silu(t, s, c):
                scalar.wait_ge(clipped, number(t, c) + 1 + LEAD)
                nc.scalar.activation(act[:, c % 3, :], act[:, c % 3, :], ACT.Silu).then_inc(silu_ready, 1)

            def high(t, s, c):
                scalar.wait_ge(multiplied, number(t, c) + 1 + LEAD)
                scalar.wait_ge(down_done, number(t, c) - 1 + LEAD)
                nc.scalar.activation(hidden[:, parity(s, c), 0, :], act[:, c % 3, :], ACT.Identity).then_inc(high_ready, 1)

            def tile(t, s, last):
                for c in range(NCHUNK):
                    if not (last and c == NCHUNK - 1):
                        silu(*at(t, s, c + 1))
                    if weighs(c, last):
                        take_xw_high(*next_expert(t, s, c))
                    if c == 22 and not last:
                        take_rows(t + 1, 1 - s)
                    high(t, s, c)

            take_rows(0, 0)
            take_xw_high(0, 0, 0)
            silu(0, 0, 0)
            tiles_with_next(scalar, tile)

        @block.vector
        def _(dve):
            def weigh(t, s, e):
                dve.wait_ge(spread_ready, NE * t + e + 1 + LEAD)
                dve.wait_ge(xw_ready, NE * t + e + LEAD)
                nc.vector.tensor_tensor(weighed[:, :], U[:, cols(t)], mem.bank[4], ALU.mult).then_inc(weighed_ready, 1)

            def clip(t, s, c):
                dve.wait_ge(gate_ready, number(t, c) + 1 + LEAD)
                dve.wait_ge(low_ready, number(t, c) - 2 + LEAD)
                nc.vector.tensor_scalar(act[:, c % 3, :], mem.bank[parity(s, c)], -LIMIT, LIMIT, ALU.max, ALU.min).then_inc(clipped, 1)

            def multiply(t, s, c):
                dve.wait_ge(silu_ready, number(t, c) + 1 + LEAD)
                dve.wait_ge(up_ready, number(t, c) + 1 + LEAD)
                nc.vector.tensor_tensor(act[:, c % 3, :], act[:, c % 3, :], mem.bank[2 + parity(s, c)], ALU.mult).then_inc(multiplied, 1)

            def add(t, s):
                dve.wait_ge(down_done, NCHUNK * (t + 1) + LEAD)
                nc.vector.tensor_tensor(X[:, cols(t)], X[:, cols(t)], mem.bank[5 + s], ALU.add).then_inc(added, 1)

            def tile(t, s, last):
                for c in range(NCHUNK):
                    if not (last and c == NCHUNK - 1):
                        clip(*at(t, s, c + 1))
                    multiply(t, s, c)
                    if weighs(c, last):
                        weigh(*next_expert(t, s, c))
                    if c == 3 and (not isinstance(t, int) or t > 0):
                        add(t - 1, 1 - s)

            split_comb(nc, dve, comb[:, :, :], act[:, 0, :].rearrange("p (b e) -> p b e", e=NE), parts, split)
            dve.wait_ge(split, 4 + LEAD)
            weigh(0, 0, 0)
            clip(0, 0, 0)
            tiles_with_next(dve, tile)
            add(NT - 1, 1)


def load_split(nc, ctx, mem, stage, dram, where):
    n = dram.shape[1]
    pieces = 8
    size = n // pieces
    mem.moe_where = where
    mem.w_high = ctx.enter_context(nc.sbuf_tensor(stage + "_high", [D, n], F32R))
    mem.w_low = ctx.enter_context(nc.sbuf_tensor(stage + "_low", [D, n], F32R))
    with ExitStack() as inner:
        whole = inner.enter_context(nc.sbuf_tensor(stage + "_whole", [D, 2, size], F32))
        (even, odd, rounded, done) = inner.enter_context(signals(nc, stage + "_load", "even", "odd", "rounded", "done"))
        landed = (even, odd)
        block = inner.enter_context(nc.Block())

        @block.sync
        def _(sp):
            for i in range(pieces):
                if i >= 2:
                    sp.wait_ge(done, i - 1 + LEAD)
                sp.dma_start(whole[:, i % 2, :], dram[:, i * size:(i + 1) * size]).then_inc(landed[i % 2], 16)

        @block.scalar
        def _(act):
            for i in range(pieces):
                act.wait_ge(landed[i % 2], 16 * (i // 2 + 1) + LEAD)
                nc.scalar.activation(mem.w_high[:, i * size:(i + 1) * size], whole[:, i % 2, :], ACT.Identity).then_inc(rounded, 1)

        @block.vector
        def _(dve):
            for i in range(pieces):
                dve.wait_ge(rounded, i + 1 + LEAD)
                nc.vector.tensor_tensor(mem.w_low[:, i * size:(i + 1) * size], whole[:, i % 2, :], mem.w_high[:, i * size:(i + 1) * size],
                                        ALU.subtract).then_inc(done, 1)


def l1_ffn(nc, stage, mem, X, U, experts):
    with ExitStack() as ctx:
        comb = ctx.enter_context(nc.sbuf_tensor(stage + "_comb", [128, NB, NE], F32))
        layer_norm(nc, stage + "_ln", mem, X, U, affine=(mem.w["l1_gamma"], mem.w["l1_beta"]), twice=True)
        with nc.sbuf_tensor(stage + "_logits", [128, NB, NE], F32) as logits:
            l1_router(nc, stage + "_route", mem, U, logits)
            top2_weights(nc, stage + "_top2", mem, logits[:, :, :], comb[:, :, :])
        load_split(nc, ctx, mem, stage, *experts)
        l1_experts(nc, stage + "_moe", mem, X, U, comb)


HEADS, HD = 16, 8
LHEADS, LD = 4, 32
LAT = 64
POOLED = S // LAT
QB = 2
SCALE = float(HD) ** -0.5


def attend(nc, stage, mem, *, rows, groups, heads, widths, chunk, q, head_mask, keys, masks, values, dst, valid=None, mix=None):
    H = groups * heads
    SP = heads * max(widths)
    with ExitStack() as ctx:
        def sb(name, *shape):
            return ctx.enter_context(nc.sbuf_tensor(stage + "_" + name, [128, *shape], F32))
        qm = sb("qm", QB, H, 128)
        top = sb("top", 2, heads)
        probs = sb("probs", 2, SP)
        turned = sb("turned", 2, SP // chunk * 128)
        inverse = sb("inverse", 2, H)
        heads_out = sb("heads_out", 2, H * HD)
        (qm_ready, scores_ready, top_ready, centered, powers, turn_ready, turned_ready, summed, inverted, masked, heads_ready,
         out_ready, stored) = ctx.enter_context(signals(
            nc, stage, "qm", "scores", "top", "centered", "powers", "turn", "turned", "summed", "inverted", "masked", "heads",
            "out", "stored"))
        if mix is not None:
            mix.allocate(nc, ctx, stage)
        block = ctx.enter_context(nc.Block())
        N = QB * groups

        def scores_at(slot, width):
            return mem.psum[:, 2 * slot:2 * slot + 2, :].rearrange("p a t -> p (a t)")[:, 0:heads * width]

        turn_ps = mem.psum[:, 4:6, :].rearrange("p a t -> p (a t)")

        def sums_at(qb):
            return mem.bank[6][:, qb * 256:qb * 256 + H * (HD + 1)].rearrange("p (h d) -> p h d", h=H)

        out_ps = mem.bank[7][0:rows, 0:128]

        def index(b, g):
            return b * N + g

        def back(b, g, n):
            g -= n
            while g < 0:
                b, g = b - 1, g + N
            if isinstance(b, int) and (b < 0 or b >= NSEQ):
                return None
            return b, g

        def schedule(eng, step):
            first = -(-3 // N)
            for g in range(first * N):
                step(g // N, g % N)
            with eng.Fori(first, NSEQ) as b:
                for g in range(N):
                    step(b, g)
            for g in range(3):
                step(NSEQ + g // N, g % N)

        def n_slot(at):
            return at[1] % 2

        def is_last(at):
            return at is not None and at[1] % groups == groups - 1

        def unit(at):
            return at[0] * QB + at[1] // groups, at[1] // groups

        def tokens(at):
            return bass.ds(at[0] * S + (at[1] // groups) * 128, 128)

        def live(b):
            return not (isinstance(b, int) and b >= NSEQ)

        @block.gpsimd
        def _(pool):
            def blocks(b):
                for qb in range(QB):
                    u = b * QB + qb
                    pool.wait_ge(scores_ready, (u - 1) * groups + LEAD)
                    pool.sem_inc(PASSED[0], 1)
                    nc.gpsimd.tensor_tensor(qm[0:rows, qb, :, :], q[:, bass.ds(b * S + qb * 128, 128)].unsqueeze(1).to_broadcast([rows, H, 128]),
                                            head_mask.unsqueeze(2).to_broadcast([rows, H, 128]), ALU.mult).then_inc(qm_ready, 1)
                    if mix is not None:
                        mix.load(pool, b, qb, u)
            with pool.Fori(0, NSEQ) as b:
                blocks(b)

        @block.tensor
        def _(pe):
            def scores(b, g):
                qb, hg = g // groups, g % groups
                width = widths[qb]
                slot = index(0, g) % 2
                if hg == 0:
                    pe.wait_ge(qm_ready, b * QB + qb + 1 + LEAD)
                pe.wait_ge(centered, index(b, g) - 1 + LEAD)
                per_bank = min(heads, T // width)
                out = scores_at(slot, width).rearrange("p (h k) -> p h k", h=heads)
                for h0 in range(0, heads, per_bank):
                    for i, (k0, mask) in enumerate(masks[qb]):
                        nc.tensor.matmul(out[:, h0:h0 + per_bank, k0:k0 + chunk], mem.ident16,
                                         mask.unsqueeze(1).to_broadcast([128, per_bank, chunk]), start=(i == 0), stop=False, skip_group_check=True)
                    for h in range(h0, h0 + per_bank):
                        last = nc.tensor.matmul(out[:, h, :], qm[0:rows, qb, hg * heads + h, :], keys(b, width), start=False,
                                                stop=True, skip_group_check=True)
                last.then_inc(scores_ready, 1)

            def turn(at):
                n = index(*at)
                width = widths[at[1] // groups]
                pe.wait_ge(powers, n + 1 + LEAD)
                if chunk < 128:
                    pe.sem_inc(PASSED[0], 1)
                pe.wait_ge(turned_ready, n + LEAD)
                if chunk < 128:
                    pe.sem_inc(PASSED[0], 1)
                for h in range(heads):
                    for c in range(width // chunk):
                        i = h * (width // chunk) + c
                        last = nc.tensor.transpose(turn_ps[0:chunk, i * 128:(i + 1) * 128],
                                                   probs[:, n_slot(at), h * width + c * chunk:h * width + (c + 1) * chunk], mem.ident)
                last.then_inc(turn_ready, 1)

            def weigh(at):
                n = index(*at)
                b, g = at
                qb, hg = g // groups, g % groups
                nch = widths[qb] // chunk
                u, _ = unit(at)
                pe.wait_ge(turned_ready, n + 1 + LEAD)
                if chunk < 128:
                    pe.sem_inc(PASSED[0], 1)
                if hg == 0:
                    if mix is None:
                        pe.wait_ge(heads_ready, u + LEAD)
                        if chunk < 128:
                            pe.sem_inc(PASSED[0], 1)
                    else:
                        pe.wait_ge(mix.step, STEPS_OF_MIX * (u - 1) + 1 + LEAD)
                if mix is not None and is_last(at):
                    pe.wait_ge(stored, u + LEAD)
                    mix.product(pe, u, qb)
                for h in range(heads):
                    for c in range(nch):
                        i = h * nch + c
                        last = nc.tensor.matmul(sums_at(qb)[:, hg * heads + h, :], turned[0:chunk, n_slot(at), i * 128:(i + 1) * 128],
                                                values(b, c, hg * heads + h), start=(c == 0), stop=(c == nch - 1), skip_group_check=True)
                last.then_inc(summed, 1)

            def turn_out(at):
                u, qb = unit(at)
                pe.wait_ge(heads_ready, u + 1 + LEAD)
                pe.wait_ge(stored, u + LEAD)
                nc.tensor.transpose(out_ps, heads_out[:, qb, :], mem.ident).then_inc(out_ready, 1)

            def step(b, g):
                if live(b):
                    scores(b, g)
                if back(b, g, 1):
                    turn(back(b, g, 1))
                if back(b, g, 2):
                    weigh(back(b, g, 2))
                if is_last(back(b, g, 3)):
                    turn_out(back(b, g, 3))

            schedule(pe, step)

        @block.vector
        def _(dve):
            def center(b, g):
                n = index(b, g)
                width = widths[g // groups]
                ps = scores_at(g % 2, width).rearrange("p (h k) -> p h k", h=heads)
                dve.wait_ge(scores_ready, n + 1 + LEAD)
                nc.vector.tensor_reduce(top[:, g % 2, :], ps, AX_X, ALU.max).then_inc(top_ready, 1)
                dve.wait_ge(turn_ready, n - 1 + LEAD)
                dve.wait_ge(top_ready, n + 1 + LEAD)
                nc.vector.tensor_tensor(probs[:, g % 2, 0:heads * width].rearrange("p (h k) -> p h k", h=heads), ps,
                                        top[:, g % 2, :].unsqueeze(2).to_broadcast([128, heads, width]), ALU.subtract).then_inc(centered, 1)

            def finish(at):
                u, qb = unit(at)
                sums = sums_at(qb)
                dve.wait_ge(summed, u * groups + groups + LEAD)
                nc.vector.reciprocal(inverse[:, qb, :], sums[:, :, HD]).then_inc(inverted, 1)
                dve.wait_ge(inverted, u + 1 + LEAD)
                if valid is not None and qb == 0:
                    nc.vector.tensor_scalar(inverse[:, qb, :], inverse[:, qb, :], valid, None, ALU.mult).then_inc(masked, 1)
                    dve.wait_ge(masked, at[0] + 1 + LEAD)
                out = heads_out[:, qb, :].rearrange("p (h d) -> p h d", h=H)
                by_head = inverse[:, qb, :].unsqueeze(2).to_broadcast([128, H, HD])
                dve.wait_ge(out_ready, u - 1 + LEAD)
                if mix is None:
                    nc.vector.tensor_tensor(out, sums[:, :, 0:HD], by_head, ALU.mult).then_inc(heads_ready, 1)
                else:
                    mix.combine(dve, u, qb, lambda: nc.vector.tensor_tensor(out, sums[:, :, 0:HD], by_head, ALU.mult),
                                heads_out[:, qb, :], heads_ready)

            def step(b, g):
                if live(b):
                    center(b, g)
                if is_last(back(b, g, 2)):
                    finish(back(b, g, 2))

            schedule(dve, step)

        @block.scalar
        def _(act):
            def power(b, g):
                n = index(b, g)
                width = heads * widths[g // groups]
                act.wait_ge(centered, n + 1 + LEAD)
                nc.scalar.activation(probs[:, g % 2, 0:width], probs[:, g % 2, 0:width], ACT.Exp, scale=SCALE).then_inc(powers, 1)

            def take_turned(at):
                n = index(*at)
                width = heads * widths[at[1] // groups] // chunk * 128
                act.wait_ge(turn_ready, n + 1 + LEAD)
                act.wait_ge(summed, n - 1 + LEAD)
                nc.scalar.activation(turned[0:chunk, at[1] % 2, 0:width], turn_ps[0:chunk, 0:width], ACT.Identity).then_inc(turned_ready, 1)

            def store(at):
                u, qb = unit(at)
                act.wait_ge(out_ready, u + 1 + LEAD)
                act.sem_inc(PASSED[0], 1)
                nc.scalar.activation(dst[:, tokens(at)], out_ps, ACT.Identity).then_inc(stored, 1)

            def step(b, g):
                if live(b):
                    power(b, g)
                if back(b, g, 1):
                    take_turned(back(b, g, 1))
                if is_last(back(b, g, 2)) and mix is not None:
                    mix.gate(act, *unit(back(b, g, 2)))
                if is_last(back(b, g, 3)):
                    store(back(b, g, 3))

            schedule(act, step)


class GateMix:

    def __init__(self, mem, lat):
        self.mem, self.lat = mem, lat

    def allocate(self, nc, ctx, stage):
        def sb(name, *shape):
            return ctx.enter_context(nc.sbuf_tensor(stage + "_" + name, [128, *shape], F32))
        self.nc = nc
        self.lat_block = sb("lat_block", QB, 128)
        self.remote = sb("remote", D)
        self.dots = sb("dots", 2, D)
        self.z = sb("z", QB, HEADS)
        (self.lat_ready, self.product_ready, self.step, self.z_ready, self.g_ready) = ctx.enter_context(
            signals(nc, stage + "_mix", "lat", "product", "step", "z", "g"))
        self.ps = self.mem.bank[7][:, 256:384]

    def load(self, pool, b, qb, u):
        pool.wait_ge(self.product_ready, u - 1 + LEAD)
        pool.sem_inc(PASSED[0], 1)
        self.nc.gpsimd.tensor_copy(self.lat_block[0:LD, qb, :], self.lat[:, bass.ds(b * S + qb * 128, 128)]).then_inc(self.lat_ready, 1)

    def product(self, pe, u, qb):
        pe.wait_ge(self.lat_ready, u + 1 + LEAD)
        pe.wait_ge(self.step, STEPS_OF_MIX * u + LEAD)
        self.nc.tensor.matmul(self.ps, self.lat_block[0:LD, qb, :], self.mem.w["rout"], start=True, stop=True).then_inc(self.product_ready, 1)

    def combine(self, dve, u, qb, local, L, done):
        nc, w = self.nc, self.mem.w
        R, dots, z = self.remote[:, :], self.dots[:, :, :], self.z[:, qb, :]
        n = STEPS_OF_MIX * u
        dve.wait_ge(done, u + LEAD)
        local().then_inc(self.step, 1)
        dve.wait_ge(self.product_ready, u + 1 + LEAD)
        nc.vector.tensor_tensor(R, self.ps, w["rout_b"], ALU.add).then_inc(self.step, 1)
        dve.wait_ge(self.step, n + 1 + LEAD)
        nc.vector.tensor_tensor(dots[:, 0, :], L, w["gl"], ALU.mult).then_inc(self.step, 1)
        dve.wait_ge(self.step, n + 2 + LEAD)
        nc.vector.tensor_tensor(dots[:, 1, :], R, w["gr"], ALU.mult).then_inc(self.step, 1)
        nc.vector.tensor_tensor(L, L, R, ALU.subtract).then_inc(self.step, 1)
        dve.wait_ge(self.step, n + 4 + LEAD)
        nc.vector.tensor_reduce(z, dots.rearrange("p a (h d) -> p h a d", h=HEADS), mybir.AxisListType.XY, ALU.add).then_inc(self.z_ready, 1)
        dve.wait_ge(self.g_ready, u + 1 + LEAD)
        nc.vector.tensor_scalar(z, z, 1.0, None, ALU.add).then_inc(self.step, 1)
        dve.wait_ge(self.step, n + 6 + LEAD)
        nc.vector.reciprocal(z, z).then_inc(self.step, 1)
        dve.wait_ge(self.step, n + 7 + LEAD)
        nc.vector.tensor_tensor(L.rearrange("p (h d) -> p h d", h=HEADS), L.rearrange("p (h d) -> p h d", h=HEADS),
                                z.unsqueeze(2).to_broadcast([128, HEADS, HD]), ALU.mult).then_inc(self.step, 1)
        dve.wait_ge(self.step, n + 8 + LEAD)
        nc.vector.tensor_tensor(L, L, R, ALU.add).then_inc(done, 1)

    def gate(self, act, u, qb):
        act.wait_ge(self.z_ready, u + 1 + LEAD)
        self.nc.scalar.activation(self.z[:, qb, :], self.z[:, qb, :], ACT.Exp, scale=-1.0).then_inc(self.g_ready, 1)


STEPS_OF_MIX = 8


def split_heads(blocks):
    return blocks.rearrange("p j (h d) -> p j h d", h=HEADS)


def project_qkv(nc, stage, mem, U, K, V, rope):
    w = mem.w
    with ExitStack() as ctx:
        def sb(name, *shape):
            return ctx.enter_context(nc.sbuf_tensor(stage + "_" + name, [D, *shape], F32))
        x = sb("x", 2, T)
        part = sb("part", 2, 2, 2, T) if rope else None
        names = ["q", "k", "swap_q", "swap_k"] if rope else ["q", "k"]
        (copied, ones, qk_ready, v_ready, turned, qk_stored, v_stored) = ctx.enter_context(signals(
            nc, stage, "copied", "ones", "qk", "v", "turned", "qk_stored", "v_stored"))
        block = ctx.enter_context(nc.Block())

        def ps_of(i, s):
            return mem.bank[2 * i + s] if i < 2 else mem.bank[4 + i]

        @block.scalar
        def _(act):
            def copy(t, s):
                act.wait_ge(v_ready, t - 1 + LEAD)
                act.sem_inc(PASSED[0], 1)
                nc.scalar.activation(x[:, s, :], U[:, cols(t)], ACT.Identity).then_inc(copied, 1)

            def store(t, s):
                if not rope:
                    for i, to in enumerate((U, K)):
                        act.wait_ge(qk_ready, 2 * t + i + 1 + LEAD)
                        act.sem_inc(PASSED[0], 1)
                        nc.scalar.activation(to[:, cols(t)], ps_of(i, s), ACT.Identity, bias=w["qk_b"][:, i:i + 1]).then_inc(qk_stored, 1)

            copy(0, 0)
            with act.Fori(0, NT // 2 - 1) as pair:
                for s in range(2):
                    copy(pair * 2 + s + 1, 1 - s)
                    store(pair * 2 + s, s)
            copy(NT - 1, 1)
            store(NT - 2, 0)
            store(NT - 1, 1)

        @block.tensor
        def _(pe):
            def step(t, s):
                pe.wait_ge(copied, t + 1 + LEAD)
                for i, name in enumerate(names):
                    if rope:
                        pe.wait_ge(turned, (len(names) * (t - 1) + i + 1 if i < 2 else len(names) * (t - 1) + i + 1) + LEAD)
                    else:
                        pe.wait_ge(qk_stored, 2 * (t - 2) + i + 1 + LEAD)
                    nc.tensor.matmul(ps_of(i, s), w[name], x[:, s, :], start=True, stop=True).then_inc(qk_ready, 1)
                pe.wait_ge(v_stored, t - 1 + LEAD)
                for j in range(SUB):
                    last = nc.tensor.matmul(mem.bank[4 + s][:, j * D:(j + 1) * D], x[:, s, j * 128:(j + 1) * 128], w["v"], start=True, stop=True)
                last.then_inc(v_ready, 1)
            tile_pairs(pe, step)

        @block.gpsimd
        def _(pool):
            nc.gpsimd.memset(V[:, :, :, HD:HD + 1], 1.0).then_inc(ones, 1)
            if rope:
                def add(t, s):
                    for i, to in enumerate((U, K)):
                        pool.wait_ge(turned, 4 * t + 3 + i + LEAD)
                        pool.sem_inc(PASSED[0], 1)
                        nc.gpsimd.tensor_tensor(to[:, cols(t)], part[:, s, i, 0, :], part[:, s, i, 1, :], ALU.add).then_inc(qk_stored, 1)
                tile_pairs(pool, add)

        @block.vector
        def _(dve):
            def step(t, s):
                if rope:
                    for i in range(4):
                        dve.wait_ge(qk_ready, 4 * t + i + 1 + LEAD)
                        dve.wait_ge(qk_stored, 2 * (t - 2) + i % 2 + 1 + LEAD)
                        by_seq = lambda ap: ap.rearrange("p (b t) -> p b t", b=SEQ_T)
                        table = mem.w["cos" if i < 2 else "sin"].unsqueeze(1).to_broadcast([D, SEQ_T, S])
                        nc.vector.tensor_tensor(by_seq(part[:, s, i % 2, i // 2, :]), by_seq(ps_of(i, s)), table, ALU.mult).then_inc(turned, 1)
                dve.wait_ge(v_ready, t + 1 + LEAD)
                to = V[:, bass.ds(t * SUB, SUB), :, 0:HD]
                src = split_heads(mem.bank[4 + s].rearrange("p (j n) -> p j n", j=SUB))
                bias = split_heads(w["v_b"].unsqueeze(1).to_broadcast([128, SUB, D])) if not rope else None
                for j in range(SUB):
                    one = V[:, bass.ds(t * SUB + j, 1), :, 0:HD].rearrange("p a h d -> p (a h) d")
                    if rope:
                        last = nc.vector.tensor_scalar(one, src[:, j, :, :], 1.0, None, ALU.mult)
                    else:
                        last = nc.vector.tensor_tensor(one, src[:, j, :, :], w["v_b"].rearrange("p (h d) -> p h d", h=HEADS), ALU.add)
                last.then_inc(v_stored, 1)
            tile_pairs(dve, step)


def causal_attention(nc, mem, X, U, weights):
    layer_norm(nc, "cau_ln", mem, X, U)
    with weights("l1b") as held:
        K = held.enter_context(nc.sbuf_tensor("cau_K", [D, TOK], F32))
        V = held.enter_context(nc.sbuf_tensor("cau_V", [128, NB, HEADS, HD + 1], F32))
        project_qkv(nc, "cau_qkv", mem, U, K, V, rope=True)
        attend(nc, "cau", mem, rows=D, groups=4, heads=4, widths=(128, 256), chunk=128, q=U, head_mask=mem.w["head_mask"],
               keys=lambda b, width: K[:, bass.ds(b * S, width)],
               masks=[[(0, mem.masks[:, 0, :])], [(128, mem.masks[:, 0, :])]],
               values=lambda b, c, h: V[:, bass.ds(b * QB + c, 1), h, :].rearrange("p a d -> p (a d)"), dst=U)
        project_add(nc, "cau_out", mem, mem.w["o"], U, X)


def pool_latents(nc, mem, U, RQ, RK, RV):
    w = mem.w
    NLAT = NSEQ * LAT
    with ExitStack() as ctx:
        pooled = ctx.enter_context(nc.sbuf_tensor("lat_pooled", [D, NLAT], F32))
        (rq_ready, rq_stored, sums, means, rk_ready, rk_stored, rv_ready, rv_stored, ones) = ctx.enter_context(signals(
            nc, "latp", "rq", "rq_stored", "sums", "means", "rk", "rk_stored", "rv", "rv_stored", "ones"))
        block = ctx.enter_context(nc.Block())

        @block.tensor
        def _(pe):
            def step(t, s):
                pe.wait_ge(rq_stored, t - 1 + LEAD)
                nc.tensor.matmul(mem.bank[s][0:LD, :], w["rq"], U[:, cols(t)], start=True, stop=True).then_inc(rq_ready, 1)
            tile_pairs(pe, step)
            pe.wait_ge(means, 1 + LEAD)
            for i in range(NLAT // T):
                nc.tensor.matmul(mem.bank[2 + i % 4][0:LD, :], w["rk"], pooled[:, i * T:(i + 1) * T], start=True, stop=True).then_inc(rk_ready, 1)
            for b in range(NSEQ):
                if b % 16 == 0:
                    bank = mem.bank[6 + b // 16]
                last = nc.tensor.matmul(bank[0:LAT, (b % 16) * LD:(b % 16 + 1) * LD], pooled[:, b * LAT:(b + 1) * LAT], w["rv"], start=True, stop=True)
            last.then_inc(rv_ready, 1)

        @block.scalar
        def _(act):
            def step(t, s):
                act.wait_ge(rq_ready, t + 1 + LEAD)
                act.sem_inc(PASSED[0], 1)
                nc.scalar.activation(RQ[:, cols(t)], mem.bank[s][0:LD, :], ACT.Identity, bias=w["rq_b"]).then_inc(rq_stored, 1)
            tile_pairs(act, step)
            for i in range(NLAT // T):
                act.wait_ge(rk_ready, i + 1 + LEAD)
                nc.scalar.activation(RK[:, i * T:(i + 1) * T], mem.bank[2 + i % 4][0:LD, :], ACT.Identity, bias=w["rk_b"]).then_inc(rk_stored, 1)

        @block.vector
        def _(dve):
            nc.vector.memset(RV[:, :, :, HD:HD + 1], 1.0).then_inc(ones, 1)
            nc.vector.tensor_reduce(pooled[:, :], U[:, :].rearrange("p (n c) -> p n c", c=POOLED), AX_X, ALU.add).then_inc(sums, 1)
            dve.wait_ge(sums, 1 + LEAD)
            nc.vector.tensor_scalar(pooled[:, :], pooled[:, :], 1.0 / POOLED, None, ALU.mult).then_inc(means, 1)
            dve.wait_ge(rv_ready, 1 + LEAD)
            bias = w["rv_b"].rearrange("p (h d) -> p h d", h=LHEADS)[0:LAT]
            for b in range(NSEQ):
                nc.vector.tensor_tensor(RV[:, b, :, 0:HD], mem.bank[6 + b // 16][0:LAT, (b % 16) * LD:(b % 16 + 1) * LD].rearrange("p (h d) -> p h d", h=LHEADS),
                                        bias, ALU.add)


def local_latent_attention(nc, mem, X, U, weights):
    layer_norm(nc, "loc_ln", mem, X, U)
    with weights("l1a") as held:
        lat = held.enter_context(nc.sbuf_tensor("lat_out", [LD, TOK], F32))
        with ExitStack() as inner:
            RK = inner.enter_context(nc.sbuf_tensor("RK", [LD, NSEQ * LAT], F32))
            RV = inner.enter_context(nc.sbuf_tensor("RV", [LAT, NSEQ, LHEADS, HD + 1], F32))
            pool_latents(nc, mem, U, lat, RK, RV)
            attend(nc, "lat", mem, rows=LD, groups=1, heads=LHEADS, widths=(LAT, LAT), chunk=LAT, q=lat, head_mask=mem.w["head_mask"][0:LD, 0:LHEADS],
                   keys=lambda b, width: RK[:, bass.ds(b * LAT, LAT)],
                   masks=[[(0, mem.masks[:, 3, 0:LAT])], [(0, mem.masks[:, 3, LAT:2 * LAT])]],
                   values=lambda b, c, h: RV[:, bass.ds(b, 1), h, :].rearrange("p a d -> p (a d)"), dst=lat,
                   valid=mem.w["sees_latent"])
        K = held.enter_context(nc.sbuf_tensor("loc_K", [D, TOK], F32))
        V = held.enter_context(nc.sbuf_tensor("loc_V", [128, NB, HEADS, HD + 1], F32))
        project_qkv(nc, "loc_qkv", mem, U, K, V, rope=False)
        attend(nc, "loc", mem, rows=D, groups=4, heads=4, widths=(128, 256), chunk=128, q=U, head_mask=mem.w["head_mask"],
               keys=lambda b, width: K[:, bass.ds(b * S, width)],
               masks=[[(0, mem.masks[:, 1, :])], [(0, mem.masks[:, 2, :]), (128, mem.masks[:, 1, :])]],
               values=lambda b, c, h: V[:, bass.ds(b * QB + c, 1), h, :].rearrange("p a d -> p (a d)"), dst=U,
               valid=mem.w["sees_key"], mix=GateMix(mem, lat))
        project_add(nc, "loc_out", mem, mem.w["o"], U, X, bias=mem.w["o_b"])


def rows_in_halves(a):
    return np.concatenate([a[0:128], a[128:256]], axis=1)


def pack_mamba(i):
    out = {}
    for c in DIRS:
        g = lambda name: i[f"L0_attn_a_{name}_{c}"]
        out["in_" + c] = g("in_w").T
        out["conv_b_" + c] = rows_in_halves(g("conv_b")[:, None])
        xp = g("xp_w").T
        bc = xp[:, RANK:]
        xp = np.concatenate([xp[:, 0:RANK], np.zeros((256, 32 - RANK), np.float32), bc, bc, bc], axis=1)
        out["xp_" + c] = rows_in_halves(xp)
        out["dtp_" + c] = g("dtp_w").T
        out["dtp_b_" + c] = rows_in_halves(g("dtp_b")[:, None])
        out["A_log_" + c] = rows_in_halves(g("A_log"))
        out["D_" + c] = rows_in_halves(g("D")[:, None])
        out["out_" + c] = g("out_w")
    out["proj"] = rows_in_halves(i["L0_attn_a_proj_w"].T)
    out["proj_b"] = i["L0_attn_a_proj_b"][:, None]
    out["gamma_a"] = i["L0_attn_a_ln_gamma"][:, None]
    out["beta_a"] = i["L0_attn_a_ln_beta"][:, None]
    return out


def col(a):
    return a[:, None]


def pack_l0(i):
    f, r = (lambda name: i["L0_ffn_" + name]), (lambda name: i["L0_attn_b_" + name])
    return {
        "pw": f("pw_w").T, "dw": f("dw_kernel")[:, 0, :], "dw_bias": col(f("dw_bias")), "pw_b": col(f("pw_b")),
        "router": f("router_w").T, "router_b": np.repeat(f("router_b")[None, :], D, axis=0),
        "experts": f("expert_w").transpose(2, 0, 1).reshape(D, NE * D), "expert_b": f("expert_b").T,
        "out": f("out_w").T, "out_b": col(f("out_b")), "norm_w": col(f("norm_w")),
        "down": f("ff_down_w").T, "down_b": col(f("ff_down_b")), "up": f("ff_up_w").T, "up_b": col(f("ff_up_b")),
        "rnn_A": r("A").T, "rnn_B": r("B").T, "rnn_C": r("C").T, "rnn_gamma": col(r("gamma")), "rnn_beta": col(r("beta")),
    }


def pack_l1_norm(i):
    f = lambda name: i["L1_ffn_" + name]
    return {"l1_gamma": col(f("ln_gamma")), "l1_beta": col(f("ln_beta")), "l1_router": f("router_w")}


def pack_l1_moe(i):
    f = lambda name: i["L1_ffn_" + name]
    return {
        "gate_up": f("gate_up_w").transpose(1, 0, 2).reshape(D, NE * 2 * F),
        "l1_down": f("down_w").reshape(NE * CH, 128, D).transpose(1, 0, 2).reshape(128, NE * CH * D),
        "shared_gate": f("shared_gate_up_w")[:, 0:128], "shared_up": f("shared_gate_up_w")[:, 128:256],
        "shared_down": f("shared_down_w"),
    }


def shared_attention():
    p = np.arange(D)
    return {"head_mask": (p[:, None] // HD == np.arange(HEADS)[None, :]).astype(np.float32)}


def pack_l1a(i):
    f = lambda name: i["L1_attn_a_" + name]
    on_all = lambda v: np.repeat(v[None, :], D, axis=0)
    p = np.arange(D)[:, None]
    return {
        "q": f("qkv_w")[:, 0:D], "k": f("qkv_w")[:, D:2 * D], "v": f("qkv_w")[:, 2 * D:],
        "qk_b": f("qkv_b")[0:2 * D].reshape(2, D).T, "v_b": on_all(f("qkv_b")[2 * D:]),
        "rq": f("rq_w"), "rq_b": col(f("rq_b")), "rk": f("rkv_w")[:, 0:LD], "rk_b": col(f("rkv_b")[0:LD]),
        "rv": f("rkv_w")[:, LD:], "rv_b": on_all(f("rkv_b")[LD:]), "rout": f("rout_w"), "rout_b": on_all(f("rout_b")),
        "o": f("out_w"), "o_b": col(f("out_b")),
        "gl": on_all(np.tile(f("gl_w")[:, 0], HEADS)), "gr": on_all(np.tile(f("gr_w")[:, 0], HEADS)),
        "sees_key": (p >= 1).astype(np.float32), "sees_latent": (p >= POOLED).astype(np.float32),
        **shared_attention(),
    }


def pack_l1b(i):
    f = lambda name: i["L1_attn_b_" + name].T
    pairs = np.arange(D).reshape(-1, 2)[:, ::-1].ravel()
    half = HD // 2
    inv_freq = np.float32(10000.0) ** (-np.arange(half, dtype=np.float32) * np.float32(2.0) / np.float32(HD))
    angle = np.arange(S, dtype=np.float32)[None, :] * inv_freq[(np.arange(D) % HD) // 2][:, None]
    sign = np.where(np.arange(D) % 2 == 0, -1.0, 1.0)[:, None]
    return {
        "q": f("Wq"), "k": f("Wk"), "v": f("Wv"), "o": f("Wo"), "swap_q": f("Wq")[:, pairs], "swap_k": f("Wk")[:, pairs],
        "cos": np.cos(angle).astype(np.float32), "sin": (sign * np.sin(angle)).astype(np.float32), **shared_attention(),
    }


def attention_masks():
    q, k = np.arange(128)[:, None], np.arange(128)[None, :]
    latent = np.concatenate([np.arange(LAT)[None, :] < (q + qb * 128) // POOLED for qb in range(QB)], axis=1)
    seen = np.stack([k <= q, k < q, (k >= q) & (k >= 1), latent], axis=1)
    return np.where(seen, 0.0, -1e30).astype(np.float32)


def constants():
    full = lambda v: np.full((D, 1), v, np.float32)
    e = np.arange(NE)
    earlier = (e[None, :] < e[:, None]).astype(np.float32)
    return {"ident": np.eye(D, dtype=np.float32), "avg": np.full((D, D), 1.0 / D, np.float32),
            "eps": full(EPS), "eps2": full(EPS * EPS), "eps6": full(1e-6), "one": full(1.0), "zero": full(0.0),
            "earlier": np.repeat(earlier.reshape(1, NE * NE), D, axis=0)}


def pack_taps(i):
    return {"taps_" + c: np.repeat(i["L0_attn_a_conv_w_" + c][:, 0, :].T.reshape(1, 4 * 256), D, axis=0) for c in DIRS}


def one_hot_rows():
    sel = np.zeros((D, 2 * NST, D), np.float32)
    for n in range(2 * NST):
        for part in (32, 64, 96):
            sel[part + n, n, :] = 1.0
    return sel


def one_hot_experts():
    sel = np.zeros((D, D), np.float32)
    for k in range(3):
        for e in range(NE):
            sel[k * NE + e, e] = 1.0
    return sel


def pack(parts):
    where, at = {}, 0
    for name, a in parts.items():
        where[name] = (a.shape[0], at, at + a.shape[1])
        at += a.shape[1]
    whole = np.zeros((D, at), np.float32)
    for name, a in parts.items():
        rows, lo, hi = where[name]
        whole[0:rows, lo:hi] = a
    return whole, where


def load_weights(nc, ctx, name, dram, where):
    held = ctx.enter_context(nc.sbuf_tensor(name, [D, dram.shape[1]], F32))
    return held, {k: held[0:rows, lo:hi] for k, (rows, lo, hi) in where.items()}


def program(nc, x_in, consts, consts16, sel, packs, out, stages):
    with ExitStack() as ctx:
        mem = Memory()
        PASSED[:] = [nc.alloc_semaphore("waits_passed")]
        mem.psum = ctx.enter_context(nc.psum_tensor("psum", [D, 8, T], F32))
        mem.bank = [mem.psum[:, b, :] for b in range(8)]
        X = ctx.enter_context(nc.sbuf_tensor("X", [D, TOK], F32))
        U = ctx.enter_context(nc.sbuf_tensor("U", [D, TOK], F32))
        held, const = load_weights(nc, ctx, "consts", consts[0], consts[1])
        mem.ident, mem.avg = const["ident"], const["avg"]
        mem.eps, mem.eps2, mem.one = const["eps"], const["eps2"], const["one"]
        mem.zero, mem.w, mem.const = const["zero"], {}, const

        uses = []

        @contextmanager
        def weights(group, *more):
            uses.append(group)
            with ExitStack() as inner:
                dram, where = packs[group]
                mem.w_outer = mem.w
                held_w, mem.w = load_weights(nc, inner, "weights_%s%d" % (group, len(uses)), dram, where)
                mem.w.update(const)
                (landed,) = inner.enter_context(signals(nc, "load_%s%d" % (group, len(uses)), "landed"))
                with nc.Block() as block:
                    @block.sync
                    def _(sp):
                        sp.dma_start(held_w[:, :], dram).then_inc(landed, 16)
                        for to, src in more:
                            sp.dma_start(to, src).then_inc(landed, 16)
                        sp.wait_ge(landed, 16 * (1 + len(more)) + LEAD)
                yield inner

        held16 = ctx.enter_context(nc.sbuf_tensor("consts16", [D, 6, D], BF16))
        mem.ident16, mem.masks, mem.one_hot = held16[:, 0, :], held16[:, 1:5, :], held16[:, 5, :]
        (loaded,) = ctx.enter_context(signals(nc, "load", "loaded"))
        with nc.Block() as block:
            @block.sync
            def _(sp):
                sp.dma_start(held[:, :], consts[0]).then_inc(loaded, 16)
                sp.dma_start(X[:, :], x_in).then_inc(loaded, 16)
                sp.dma_start(held16[:, :, :], consts16).then_inc(loaded, 16)
                sp.wait_ge(loaded, 48 + LEAD)

        if "a" in stages:
            with ExitStack() as stage:
                mem.sel = stage.enter_context(nc.sbuf_tensor("sel", [D, 2 * NST, D], BF16))
                mem.A = stage.enter_context(nc.sbuf_tensor("A", [D, 2, 2 * NST], F32))
                mem.conv_in = stage.enter_context(nc.sbuf_tensor("conv_in", [D, 2, 4, 256], F32))
                mem.out_proj = stage.enter_context(nc.sbuf_tensor("out_proj", [D, 2, 2, D], F32))
                with weights("mamba", (mem.sel[:, :, :], sel)):
                    with weights("taps"):
                        mem.w.update(mem.w_outer)
                        mamba_weights(nc, mem)
                    mem.w = mem.w_outer
                    layer_norm(nc, "ln_a", mem, X, U, affine=(mem.w["gamma_a"], mem.w["beta_a"]), twice=True, residual=X)
                    mamba(nc, mem, X, U)
        with weights("l0") as held_l0:
            mem.pw_taps = held_l0.enter_context(nc.sbuf_tensor("pw_taps", [D, 3, D], F32))
            mem.pw_bias = held_l0.enter_context(nc.sbuf_tensor("pw_bias", [D, 1], F32))
            l0_weights(nc, mem)
            if "b" in stages:
                l0_ffn(nc, "ffn1", mem, X, U)
            if "c" in stages:
                recurrent(nc, mem, X, U)
            if "d" in stages:
                l0_ffn(nc, "ffn2", mem, X, U)
        if "e" in stages:
            local_latent_attention(nc, mem, X, U, weights)
        if "f" in stages:
            with weights("l1_norm"):
                l1_ffn(nc, "ffn3", mem, X, U, packs["l1_moe"])
        if "g" in stages:
            causal_attention(nc, mem, X, U, weights)
        if "h" in stages:
            with weights("l1_norm"):
                l1_ffn(nc, "ffn4", mem, X, U, packs["l1_moe"])
        (stored,) = ctx.enter_context(signals(nc, "store", "stored"))
        with nc.Block() as block:
            @block.sync
            def _(sp):
                sp.dma_start(out, X[:, :]).then_inc(stored, 16)
                sp.wait_ge(stored, 16 + LEAD)


def kernel(**inputs):
    import concourse.bacc as bacc
    import ml_dtypes
    from concourse.bass_utils import run_bass_kernel_spmd

    i = {name: np.asarray(a) for name, a in inputs.items()}
    nc = bacc.Bacc("TRN2", target_bir_lowering=False, num_devices=1)
    arrays = {}

    def given(name, a):
        a = np.ascontiguousarray(a)
        arrays[name] = a
        return nc.dram_tensor(name, a.shape, mybir.dt.from_np(a.dtype), kind="ExternalInput").ap()

    def packed(name, parts):
        whole, where = pack(parts)
        return given("in_" + name, whole), where

    x_in = given("in_x", i["L0_attn_a_x"].reshape(TOK, D).T)
    consts = packed("consts", constants())
    consts16 = given("in_consts16", np.concatenate([np.eye(D)[:, None, :], attention_masks(), one_hot_experts()[:, None, :]], axis=1).astype(ml_dtypes.bfloat16))
    sel = given("in_sel", one_hot_rows().astype(ml_dtypes.bfloat16))
    packs = {
        "mamba": packed("mamba", pack_mamba(i)), "taps": packed("taps", pack_taps(i)), "l0": packed("l0", pack_l0(i)),
        "l1_norm": packed("l1_norm", pack_l1_norm(i)),
        "l1_moe": packed("l1_moe", pack_l1_moe(i)), "l1a": packed("l1a", pack_l1a(i)), "l1b": packed("l1b", pack_l1b(i)),
    }
    out = nc.dram_tensor("out", (D, TOK), F32, kind="ExternalOutput").ap()
    program(nc, x_in, consts, consts16, sel, packs, out, 'abcdefgh')
    r = run_bass_kernel_spmd(nc, [arrays], core_ids=[0])
    return np.ascontiguousarray(r.results[0]["out"].T).reshape(NSEQ, S, D)
```

```python
from contextlib import ExitStack, contextmanager

import numpy as np

import concourse.bass as bass
from concourse import mybir

F32 = mybir.dt.float32
F32R = mybir.dt.float32r
BF16 = mybir.dt.bfloat16
ALU = mybir.AluOpType
ACT = mybir.ActivationFunctionType
AX_X = mybir.AxisListType.X

D = 128
NSEQ, S = 32, 256
TOK = NSEQ * S
T = 512
SEQ_T = T // S
NT = TOK // T
LEAD = 64

NST = 16
RANK = 8
NE = 8
HID = 32
EPS = 1e-5
LN_AND_EXP = "natural_log_exp_and_others"


PASSED = []


@contextmanager
def signals(nc, stage, *names):
    sems = [nc.alloc_semaphore(f"{stage}_{name}") for name in names]
    for sem in sems:
        nc.sync.sem_inc(sem, LEAD)
    nc.all_engine_barrier()
    yield sems
    nc.clear_and_free_semaphores(sems)
    nc.all_engine_barrier()


def cols(t, width=T):
    return bass.ds(t * width, width)


def tile_pairs(eng, step):
    with eng.Fori(0, NT // 2) as pair:
        for slot in range(2):
            step(pair * 2 + slot, slot)


def layer_norm(nc, stage, mem, src, dst, affine=None, twice=False, residual=None):
    with ExitStack() as ctx:
        sq = ctx.enter_context(nc.sbuf_tensor(stage + "_sq", [D, 2, T], F32))
        logv = ctx.enter_context(nc.sbuf_tensor(stage + "_logv", [D, 2, T], F32))
        rstd = ctx.enter_context(nc.sbuf_tensor(stage + "_rstd", [D, 2, T], F32))
        log1 = ctx.enter_context(nc.sbuf_tensor(stage + "_log1", [D, 2, T], F32)) if residual is not None else None
        rstd1 = ctx.enter_context(nc.sbuf_tensor(stage + "_rstd1", [D, 2, T], F32)) if residual is not None else None
        ps_mean = [mem.bank[0], mem.bank[1]]
        ps_var = [mem.bank[2], mem.bank[3]]
        (mean_ready, centered, squared, var_ready, log_done, rstd_ready, added, scaled) = ctx.enter_context(
            signals(nc, stage, "mean", "centered", "squared", "var", "log", "rstd", "added", "scaled"))
        block = ctx.enter_context(nc.Block())
        n_log = 2 if residual is not None else 1

        @block.tensor
        def _(pe):
            def mean(t, s):
                pe.wait_ge(centered, t - 1 + LEAD)
                nc.tensor.matmul(ps_mean[s], mem.avg, src[:, cols(t)], start=True, stop=True).then_inc(mean_ready, 1)

            def var(t, s):
                pe.wait_ge(squared, t + 1 + LEAD)
                pe.wait_ge(rstd_ready, n_log * (t - 1) + LEAD)
                nc.tensor.matmul(ps_var[s], mem.avg, sq[:, s, :], start=True, stop=True).then_inc(var_ready, 1)

            mean(0, 0)
            mean(1, 1)
            with pe.Fori(0, NT // 2 - 1) as pair:
                for s in range(2):
                    mean(pair * 2 + s + 2, s)
                    var(pair * 2 + s, s)
            var(NT - 2, 0)
            var(NT - 1, 1)

        @block.vector
        def _(dve):
            def center(t, s):
                dve.wait_ge(mean_ready, t + 1 + LEAD)
                nc.vector.tensor_tensor(dst[:, cols(t)], src[:, cols(t)], ps_mean[s], ALU.subtract).then_inc(centered, 1)

            def scale(t, s):
                dve.wait_ge(rstd_ready, n_log * (t + 1) + LEAD)
                dve.wait_ge(squared, t + 1 + LEAD)
                if residual is not None:
                    nc.vector.tensor_tensor(rstd1[:, s, :], dst[:, cols(t)], rstd1[:, s, :], ALU.mult).then_inc(scaled, 1)
                    dve.wait_ge(scaled, 2 * t + 1 + LEAD)
                    nc.vector.tensor_tensor(residual[:, cols(t)], residual[:, cols(t)], rstd1[:, s, :], ALU.add).then_inc(added, 1)
                if affine is None:
                    nc.vector.tensor_tensor(dst[:, cols(t)], dst[:, cols(t)], rstd[:, s, :], ALU.mult).then_inc(scaled, 1)
                else:
                    k = 2 if residual is not None else 1
                    nc.vector.scalar_tensor_tensor(dst[:, cols(t)], dst[:, cols(t)], affine[0], rstd[:, s, :],
                                                   ALU.mult, ALU.mult).then_inc(scaled, 1)
                    dve.wait_ge(scaled, k * t + k + LEAD)
                    nc.vector.tensor_scalar(dst[:, cols(t)], dst[:, cols(t)], affine[1], None, ALU.add)

            center(0, 0)
            center(1, 1)
            with dve.Fori(0, NT // 2 - 1) as pair:
                for s in range(2):
                    center(pair * 2 + s + 2, s)
                    scale(pair * 2 + s, s)
            scale(NT - 2, 0)
            scale(NT - 1, 1)

        @block.gpsimd
        def _(pool):
            def square(t, s):
                pool.wait_ge(var_ready, t - 1 + LEAD)
                pool.wait_ge(centered, t + 1 + LEAD)
                pool.sem_inc(PASSED[0], 1)
                nc.gpsimd.tensor_tensor(sq[:, s, :], dst[:, cols(t)], dst[:, cols(t)], ALU.mult).then_inc(squared, 1)
            tile_pairs(pool, square)

        @block.scalar
        def _(act):
            def rsqrt(t, s):
                act.wait_ge(scaled, ((t - 1) * (2 if residual is not None else 1)) + LEAD)
                if residual is not None:
                    act.wait_ge(added, t - 1 + LEAD)
                act.wait_ge(var_ready, t + 1 + LEAD)
                if twice:
                    nc.scalar.activation(logv[:, s, :], ps_var[s], ACT.Ln, bias=mem.eps2, scale=1.0 + EPS).then_inc(log_done, 1)
                else:
                    nc.scalar.activation(logv[:, s, :], ps_var[s], ACT.Ln, bias=mem.eps, scale=1.0).then_inc(log_done, 1)
                if residual is not None:
                    nc.scalar.activation(log1[:, s, :], ps_var[s], ACT.Ln, bias=mem.eps, scale=1.0).then_inc(log_done, 1)
                    act.wait_ge(log_done, 2 * t + 2 + LEAD)
                    nc.scalar.activation(rstd1[:, s, :], log1[:, s, :], ACT.Exp, scale=-0.5).then_inc(rstd_ready, 1)
                else:
                    act.wait_ge(log_done, t + 1 + LEAD)
                nc.scalar.activation(rstd[:, s, :], logv[:, s, :], ACT.Exp, scale=-0.5).then_inc(rstd_ready, 1)
            nc.scalar.preload_act_table_set(LN_AND_EXP)
            tile_pairs(act, rsqrt)


class Memory:
    pass
PAD = 3
GN = 2
NG = NST // GN
HALVES = 2
FRONT = 7
USES = FRONT + 1
DIRS = "fb"


def mamba_weights(nc, mem):
    w = mem.w
    with ExitStack() as ctx:
        (exp_done, products) = ctx.enter_context(signals(nc, "mw", "exp", "products"))
        block = ctx.enter_context(nc.Block())

        @block.scalar
        def _(act):
            for d, c in enumerate(DIRS):
                nc.scalar.activation(mem.A[:, d, :], w["A_log_" + c], ACT.Exp).then_inc(exp_done, 1)

        @block.vector
        def _(dve):
            dve.wait_ge(exp_done, 2 + LEAD)
            nc.vector.tensor_scalar(mem.A[:, :, :], mem.A[:, :, :], -1.0, None, ALU.mult)
            for d, c in enumerate(DIRS):
                in_xc = w["in_" + c][:, 0:256].unsqueeze(1).to_broadcast([D, 4, 256])
                nc.vector.tensor_tensor(mem.conv_in[:, d, :, :], w["taps_" + c].rearrange("p (k c) -> p k c", k=4), in_xc, ALU.mult)
            dve.wait_ge(products, 1 + LEAD)
            for d in range(2):
                nc.vector.tensor_copy(mem.out_proj[:, d, :, :], mem.bank[d][:, 0:256].rearrange("p (h o) -> p h o", h=2))

        @block.tensor
        def _(pe):
            for d, c in enumerate(DIRS):
                for h in range(HALVES):
                    last = nc.tensor.matmul(mem.bank[d][:, h * 128:(h + 1) * 128], w["out_" + c][:, h * 128:(h + 1) * 128],
                                            w["proj"][:, d * 128:(d + 1) * 128], start=True, stop=True)
            last.then_inc(products, 1)


def mamba(nc, mem, X, U):
    w = mem.w
    with ExitStack() as ctx:
        def sb(name, shape, dt=F32):
            return ctx.enter_context(nc.sbuf_tensor("mamba_" + name, shape, dt))
        xpad = sb("xpad", [D, 2, SEQ_T, S + 2 * PAD])
        u = sb("u", [D, 2, 2, T])
        z = sb("z", [D, 2, 2, T])
        delta = sb("delta", [D, 2, 2, T])
        du = sb("du", [D, 2, 2, T])
        pre = sb("pre", [D, 2, T])
        soft = sb("soft", [D, 2, T])
        xdbl = sb("xdbl", [D, T])
        rest = sb("rest", [D, T])
        first = sb("first", [D, T], BF16)
        second = sb("second", [D, T], BF16)
        parts = sb("parts", [D, 2, T], BF16)
        outp = sb("outp", [D, T])
        dA = sb("dA", [D, 2, 2, 2, GN, SEQ_T, S])
        bu = sb("bu", [D, 2, GN * T])
        hc = sb("hc", [D, 2, 2, GN, T])
        work = [mem.bank[0], mem.bank[1]]
        ysum = [mem.bank[2], mem.bank[3]]
        b_bc = mem.psum[:, 4:6, :]
        c_bc = mem.psum[:, 6:8, :]

        (xpad_ready, work_ready, work_read, first_ready, rest_ready, second_ready, parts_ready, soft_step, soft_ready, delta_step, du_ready,
         b_ready, c_ready, dA_ready, bu_ready, scanned, hc_ready, paired, summed, y_step, y_ready, added, zeroed
         ) = ctx.enter_context(signals(
            nc, "mamba", "xpad", "work", "work_read", "first", "rest", "second", "parts", "soft_step", "soft", "delta_step", "du",
            "b_bc", "c_bc", "dA", "bu", "scanned", "hc", "paired", "summed", "y_step", "y", "added", "zeroed"))
        block = ctx.enter_context(nc.Block())


        def front_use(t, d, k):
            if isinstance(t, int) and (t, d) == (0, 0):
                return k, k % 2
            return (2 * t + d) * USES - 1 + k, (k + 1) % 2

        def out_use(t, d):
            if isinstance(t, int) and (t, d) == (NT - 1, 1):
                return (2 * t + d) * USES + FRONT, 1
            return (2 * t + d) * USES + 2 * FRONT, 0

        def by_seq(ap):
            return ap.rearrange("p (b t) -> p b t", b=SEQ_T)

        def is_first(t, d):
            return isinstance(t, int) and (t, d) == (0, 0)

        def has_next(t, d):
            return not (isinstance(t, int) and (t, d) == (NT - 1, 1))

        def before(t, d):
            return (t, 0) if d == 1 else (t - 1, 1)

        def all_units(eng, unit):
            unit(0, 0, 0)
            unit(0, 0, 1)
            with eng.Fori(0, NT // 2 - 1) as pair:
                for t, s in ((pair * 2 + 1, 1), (pair * 2 + 2, 0)):
                    unit(t, s, 0)
                    unit(t, s, 1)
            unit(NT - 1, 1, 0)
            unit(NT - 1, 1, 1)

        @block.gpsimd
        def _(pool):
            nc.gpsimd.memset(xpad[:, :, :, :], 0.0).then_inc(zeroed, 1)
            nc.gpsimd.memset(dA[:, :, :, :, :, :, :], 0.0).then_inc(zeroed, 1)
            pool.wait_ge(zeroed, 2 + LEAD)
            pool.sem_inc(PASSED[0], 1)

            def load(t, s):
                pool.wait_ge(work_ready, (2 * t - 3) * USES - 1 + 4 + LEAD)
                pool.sem_inc(PASSED[0], 1)
                nc.gpsimd.tensor_copy(xpad[:, s, :, PAD:PAD + S], by_seq(U[:, cols(t)])).then_inc(xpad_ready, 1)

            def split_rest(t, d):
                q = 2 * t + d
                pool.wait_ge(first_ready, q + 1 + LEAD)
                pool.sem_inc(PASSED[0], 1)
                pool.wait_ge(work_read, front_use(t, d, 4)[0] + 1 + LEAD)
                pool.sem_inc(PASSED[0], 1)
                nc.gpsimd.tensor_tensor(rest[:, :], xdbl[:, :], first[:, :], ALU.subtract).then_inc(rest_ready, 1)

            def split_last(t, d):
                q = 2 * t + d
                pool.wait_ge(second_ready, q + 1 + LEAD)
                pool.sem_inc(PASSED[0], 1)
                pool.wait_ge(rest_ready, q + 1 + LEAD)
                pool.sem_inc(PASSED[0], 1)
                pool.wait_ge(c_ready, NG * (q - 1) + LEAD)
                pool.sem_inc(PASSED[0], 1)
                nc.gpsimd.tensor_tensor(parts[:, d, :], rest[:, :], second[:, :], ALU.subtract).then_inc(parts_ready, 1)

            def step_size(t, d):
                q = 2 * t + d
                pool.wait_ge(soft_ready, q + 1 + LEAD)
                pool.sem_inc(PASSED[0], 1)
                pool.wait_ge(soft_step, 3 * q + 3 + LEAD)
                pool.sem_inc(PASSED[0], 1)
                pool.wait_ge(work_ready, (q - 2) * USES + 2 * FRONT + 1 + LEAD)
                pool.sem_inc(PASSED[0], 1)
                pool.wait_ge(dA_ready, 2 * NG * (q - 1) + LEAD)
                pool.sem_inc(PASSED[0], 1)
                nc.gpsimd.tensor_tensor(delta[:, d, :, :], pre[:, :, :], soft[:, :, :], ALU.add).then_inc(delta_step, 1)
                pool.wait_ge(delta_step, q + 1 + LEAD)
                pool.sem_inc(PASSED[0], 1)
                nc.gpsimd.tensor_tensor(du[:, d, :, :], delta[:, d, :, :], u[:, d, :, :], ALU.mult).then_inc(du_ready, 1)

            def gate(t, d):
                for h in range(HALVES):
                    pool.wait_ge(y_step, 2 * (2 * t + d) + h + 1 + LEAD)
                    pool.sem_inc(PASSED[0], 1)
                    nc.gpsimd.tensor_tensor(du[:, d, h, :], du[:, d, h, :], z[:, d, h, :], ALU.mult).then_inc(y_ready, 1)

            def pair_up(t, d, g):
                for h in range(HALVES):
                    pool.wait_ge(hc_ready, 2 * (NG * (2 * t + d) + g) + h + 1 + LEAD)
                    pool.sem_inc(PASSED[0], 1)
                    nc.gpsimd.tensor_tensor(hc[:, h, g % 2, 0, :], hc[:, h, g % 2, 0, :], hc[:, h, g % 2, 1, :], ALU.add).then_inc(paired, 1)

            def out(t, d):
                pool.wait_ge(work_read, out_use(t, d)[0] + 1 + LEAD)
                pool.sem_inc(PASSED[0], 1)
                nc.gpsimd.tensor_tensor(X[:, cols(t)], X[:, cols(t)], outp[:, :], ALU.add).then_inc(added, 1)

            def unit(t, s, d):
                for g in range(NG):
                    if g == 6 and has_next(t, d):
                        step_size(t + d, 1 - d)
                    if g == 0 and not is_first(t, d):
                        gate(*before(t, d))
                    pair_up(t, d, g)
                    if g == 0 and d == 0 and has_next(t, 1):
                        load(t + 1, 1 - s)
                    if g == 2 and not is_first(t, d):
                        out(*before(t, d))
                    if g == 4 and has_next(t, d):
                        split_rest(t + d, 1 - d)
                    if g == 5 and has_next(t, d):
                        split_last(t + d, 1 - d)

            load(0, 0)
            split_rest(0, 0)
            split_last(0, 0)
            step_size(0, 0)
            all_units(pool, unit)
            gate(NT - 1, 1)
            out(NT - 1, 1)

        @block.tensor
        def _(pe):
            pe.wait_ge(zeroed, 2 + LEAD)

            def claim(use):
                pos, bank = use
                pe.wait_ge(work_read, pos - 1 + LEAD)
                return work[bank]

            def convolve(t, s, d, h):
                if h == 0:
                    pe.wait_ge(xpad_ready, t + 1 + LEAD)
                to = by_seq(claim(front_use(t, d, h)))
                for k in range(4):
                    at = k if d == 0 else 2 * PAD - k
                    last = nc.tensor.matmul(to, mem.conv_in[:, d, k, h * 128:(h + 1) * 128], xpad[:, s, :, at:at + S],
                                            start=(k == 0), stop=(k == 3))
                last.then_inc(work_ready, 1)

            def project_gate(t, s, d):
                for h in range(HALVES):
                    to = by_seq(claim(front_use(t, d, 2 + h)))
                    nc.tensor.matmul(to, w["in_" + DIRS[d]][:, 256 + h * 128:256 + (h + 1) * 128], xpad[:, s, :, PAD:PAD + S],
                                     start=True, stop=True).then_inc(work_ready, 1)

            def project_u(t, d):
                to = claim(front_use(t, d, 4))
                pe.wait_ge(work_read, front_use(t, d, 1)[0] + 1 + LEAD)
                for h in range(HALVES):
                    last = nc.tensor.matmul(to, w["xp_" + DIRS[d]][:, h * 128:(h + 1) * 128], u[:, d, h, :],
                                            start=(h == 0), stop=(h == 1))
                last.then_inc(work_ready, 1)

            def project_dt(t, d):
                pe.wait_ge(work_read, front_use(t, d, 4)[0] + 1 + LEAD)
                for h in range(HALVES):
                    to = claim(front_use(t, d, 5 + h))
                    nc.tensor.matmul(to, w["dtp_" + DIRS[d]][0:RANK, h * 128:(h + 1) * 128], xdbl[0:RANK, :],
                                     start=True, stop=True).then_inc(work_ready, 1)

            def spread_b(t, d, g):
                q = 2 * t + d
                if g == 0:
                    pe.wait_ge(parts_ready, q + 1 + LEAD)
                pe.wait_ge(bu_ready, 2 * (NG * q + g) + LEAD)
                for n in range(GN):
                    last = nc.tensor.matmul(b_bc[:, n, :], mem.sel[:, GN * g + n:GN * g + n + 1].to_broadcast([D, D]), parts[:, d, :], start=True, stop=True)
                last.then_inc(b_ready, 1)

            def spread_c(t, d, g):
                pe.wait_ge(hc_ready, 2 * (NG * (2 * t + d) + g) + LEAD)
                for n in range(GN):
                    last = nc.tensor.matmul(c_bc[:, n, :], mem.sel[:, NST + GN * g + n:NST + GN * g + n + 1].to_broadcast([D, D]), parts[:, d, :], start=True, stop=True)
                last.then_inc(c_ready, 1)

            def reduce(t, d, g):
                q = 2 * t + d
                for h in range(HALVES):
                    if g == 0:
                        pe.wait_ge(y_step, 2 * q + LEAD)
                    pe.wait_ge(paired, 2 * (NG * q + g) + h + 1 + LEAD)
                    nc.tensor.matmul(ysum[h], mem.ident, hc[:, h, g % 2, 0, :], start=(g == 0), stop=(g == NG - 1)).then_inc(summed, 1)

            def out(t, d):
                to = claim(out_use(t, d))
                for h in range(HALVES):
                    pe.wait_ge(y_ready, 2 * (2 * t + d) + h + 1 + LEAD)
                    last = nc.tensor.matmul(to, mem.out_proj[:, d, h, :], du[:, d, h, :], start=(h == 0), stop=(h == 1))
                last.then_inc(work_ready, 1)

            def unit(t, s, d):
                front = (t + d, 1 - d)
                for g in range(NG):
                    spread_c(t, d, g)
                    if g == 1 and not is_first(t, d):
                        out(*before(t, d))
                    if has_next(t, d):
                        if g == 1:
                            convolve(front[0], (s + d) % 2, front[1], 0)
                        if g == 2:
                            convolve(front[0], (s + d) % 2, front[1], 1)
                        if g == 3:
                            project_gate(front[0], (s + d) % 2, front[1])
                        if g == 4:
                            project_u(*front)
                        if g == 5:
                            project_dt(*front)
                    if g + 1 < NG:
                        spread_b(t, d, g + 1)
                    elif has_next(t, d):
                        spread_b(*front, 0)
                    if g >= 1:
                        reduce(t, d, g - 1)
                    elif not is_first(t, d):
                        reduce(*before(t, d), NG - 1)

            for h in range(HALVES):
                convolve(0, 0, 0, h)
            project_gate(0, 0, 0)
            project_u(0, 0)
            project_dt(0, 0)
            spread_b(0, 0, 0)
            all_units(pe, unit)
            reduce(NT - 1, 1, NG - 1)
            out(NT - 1, 1)

        @block.scalar
        def _(act):
            act.wait_ge(zeroed, 2 + LEAD)

            def work_at(use):
                pos, bank = use
                act.wait_ge(work_ready, pos + 1 + LEAD)
                return work[bank]

            def gates(t, d):
                act.wait_ge(y_ready, 2 * (2 * t + d) - 2 + LEAD)
                act.wait_ge(du_ready, 2 * t + d - 1 + LEAD)
                for h in range(HALVES):
                    nc.scalar.activation(u[:, d, h, :], work_at(front_use(t, d, h)), ACT.Silu,
                                         bias=w["conv_b_" + DIRS[d]][:, h:h + 1]).then_inc(work_read, 1)
                for h in range(HALVES):
                    nc.scalar.activation(z[:, d, h, :], work_at(front_use(t, d, 2 + h)), ACT.Silu).then_inc(work_read, 1)

            def take_xdbl(t, d):
                q = 2 * t + d
                src = work_at(front_use(t, d, 4))
                act.wait_ge(parts_ready, q + LEAD)
                nc.scalar.activation(first[:, :], src, ACT.Identity, scale=w["from_64"]).then_inc(first_ready, 1)
                nc.scalar.activation(xdbl[:, :], src, ACT.Identity).then_inc(work_read, 1)

            def round_rest(t, d):
                act.wait_ge(rest_ready, 2 * t + d + 1 + LEAD)
                nc.scalar.activation(second[:, :], rest[:, :], ACT.Identity, scale=w["from_96"]).then_inc(second_ready, 1)

            def take_pre(t, d):
                q = 2 * t + d
                act.wait_ge(du_ready, q + LEAD)
                for h in range(HALVES):
                    nc.scalar.activation(pre[:, h, :], work_at(front_use(t, d, 5 + h)), ACT.Identity,
                                         bias=w["dtp_b_" + DIRS[d]][:, h:h + 1]).then_inc(work_read, 1)

            def softplus(t, d):
                q = 2 * t + d
                act.wait_ge(work_read, front_use(t, d, 6)[0] + 1 + LEAD)
                nc.scalar.activation(soft[:, :, :], pre[:, :, :], ACT.Abs).then_inc(soft_step, 1)
                nc.scalar.preload_act_table_set(LN_AND_EXP)
                act.wait_ge(soft_step, 3 * q + 1 + LEAD)
                nc.scalar.activation(soft[:, :, :], soft[:, :, :], ACT.Exp, scale=-1.0).then_inc(soft_step, 1)
                act.wait_ge(soft_step, 3 * q + 2 + LEAD)
                nc.scalar.activation(soft[:, :, :], soft[:, :, :], ACT.Ln, bias=mem.one, scale=1.0).then_inc(soft_step, 1)
                nc.scalar.activation(pre[:, :, :], pre[:, :, :], ACT.Relu).then_inc(soft_ready, 1)

            def decay(t, d, g):
                q = 2 * t + d
                lo, hi = (1, S) if d == 0 else (0, S - 1)
                if g == 0:
                    act.wait_ge(du_ready, q + 1 + LEAD)
                for h in range(HALVES):
                    act.wait_ge(scanned, 2 * (NG * q + g) + h - 3 + LEAD)
                    for n in range(GN):
                        last = nc.scalar.activation(dA[:, d, h, g % 2, n, :, lo:hi], by_seq(delta[:, d, h, :])[:, :, lo:hi], ACT.Exp,
                                                    scale=mem.A[:, d, h * NST + GN * g + n:h * NST + GN * g + n + 1])
                    last.then_inc(dA_ready, 1)

            def out(t, d):
                src = work_at(out_use(t, d))
                act.wait_ge(added, 2 * t + d + LEAD)
                nc.scalar.activation(outp[:, :], src, ACT.Identity,
                                     bias=w["proj_b"] if d == 0 else mem.zero).then_inc(work_read, 1)

            def unit(t, s, d):
                for g in range(NG):
                    decay(t, d, g)
                    if g == 2 and not is_first(t, d):
                        out(*before(t, d))
                    if has_next(t, d):
                        if g == 3:
                            gates(t + d, 1 - d)
                        if g == 4:
                            take_xdbl(t + d, 1 - d)
                        if g == 5:
                            round_rest(t + d, 1 - d)
                            take_pre(t + d, 1 - d)
                        if g == 6:
                            softplus(t + d, 1 - d)

            gates(0, 0)
            take_xdbl(0, 0)
            round_rest(0, 0)
            take_pre(0, 0)
            softplus(0, 0)
            all_units(act, unit)
            out(NT - 1, 1)

        @block.vector
        def _(dve):
            dve.wait_ge(zeroed, 2 + LEAD)

            def gated(t, d):
                q = 2 * t + d
                for h in range(HALVES):
                    dve.wait_ge(summed, 2 * NG * (q + 1) - 1 + h + LEAD)
                    nc.vector.scalar_tensor_tensor(du[:, d, h, :], u[:, d, h, :], w["D_" + DIRS[d]][:, h:h + 1], ysum[h],
                                                   ALU.mult, ALU.add).then_inc(y_step, 1)

            def unit(t, s, d):
                q = 2 * t + d
                run = slice(None) if d == 0 else slice(None, None, -1)
                for g in range(NG):
                    G = NG * q + g
                    par = g % 2
                    if g == 0:
                        dve.wait_ge(du_ready, q + 1 + LEAD)
                    dve.wait_ge(b_ready, G + 1 + LEAD)
                    for h in range(HALVES):
                        dve.wait_ge(hc_ready, 2 * G + h - 1 + LEAD)
                        nc.vector.tensor_tensor(bu[:, h, :].rearrange("p (n t) -> p n t", n=GN), b_bc,
                                                du[:, d, h, :].unsqueeze(1).to_broadcast([D, GN, T]), ALU.mult).then_inc(bu_ready, 1)
                    for h in range(HALVES):
                        dve.wait_ge(dA_ready, 2 * G + h + 1 + LEAD)
                        dve.wait_ge(bu_ready, 2 * G + h + 1 + LEAD)
                        state = bu[:, h, :]
                        decay = dA[:, d, h, par, :, :, :].rearrange("p n b t -> p (n b t)")
                        nc.vector.tensor_tensor_scan(state[:, run], decay[:, run], state[:, run], 0.0,
                                                     ALU.mult, ALU.add).then_inc(scanned, 1)
                    if g == 0 and not is_first(t, d):
                        gated(*before(t, d))
                    dve.wait_ge(c_ready, G + 1 + LEAD)
                    for h in range(HALVES):
                        dve.wait_ge(summed, 2 * G + h - 3 + LEAD)
                        dve.wait_ge(scanned, 2 * G + h + 1 + LEAD)
                        nc.vector.tensor_tensor(hc[:, h, par, :, :], bu[:, h, :].rearrange("p (n t) -> p n t", n=GN),
                                                c_bc, ALU.mult).then_inc(hc_ready, 1)

            all_units(dve, unit)
            gated(NT - 1, 1)


SUB = T // 128
NB = TOK // 128


def top2_weights(nc, stage, mem, logits, comb):
    with ExitStack() as ctx:
        def sb(name, *shape):
            return ctx.enter_context(nc.sbuf_tensor(stage + "_" + name, [128, *shape], F32))
        beats = sb("beats", NB, NE, NE)
        ties = sb("ties", NB, NE, NE)
        rank = sb("rank", NB, NE)
        top = sb("top", NB)
        total = sb("total", NB)
        inverse = sb("inverse", NB)
        (top_ready, centered, gt_ready, eq_ready, tie_ready, beats_ready, rank_ready, chosen, powers, weighed, summed, inverted, done
         ) = ctx.enter_context(signals(nc, stage, "top", "centered", "gt", "eq", "tie", "beats", "rank", "chosen", "powers",
                                       "weighed", "summed", "inverted", "done"))
        block = ctx.enter_context(nc.Block())
        of_f = logits.unsqueeze(2).to_broadcast([128, NB, NE, NE])
        of_e = logits.unsqueeze(3).to_broadcast([128, NB, NE, NE])

        @block.vector
        def _(dve):
            nc.vector.tensor_reduce(top[:, :], logits, AX_X, ALU.max).then_inc(top_ready, 1)
            nc.vector.tensor_tensor(beats[:, :, :, :], of_f, of_e, ALU.is_gt).then_inc(gt_ready, 1)
            dve.wait_ge(top_ready, 1 + LEAD)
            nc.vector.tensor_tensor(comb, logits, top[:, :].unsqueeze(2).to_broadcast([128, NB, NE]), ALU.subtract).then_inc(centered, 1)
            nc.vector.tensor_tensor(ties[:, :, :, :], of_f, of_e, ALU.is_equal).then_inc(eq_ready, 1)
            dve.wait_ge(eq_ready, 1 + LEAD)
            earlier = mem.const["earlier"].rearrange("p (e f) -> p e f", e=NE).unsqueeze(1).to_broadcast([128, NB, NE, NE])
            nc.vector.tensor_tensor(ties[:, :, :, :], ties[:, :, :, :], earlier, ALU.mult).then_inc(tie_ready, 1)
            dve.wait_ge(tie_ready, 1 + LEAD)
            dve.wait_ge(gt_ready, 1 + LEAD)
            nc.vector.tensor_tensor(beats[:, :, :, :], beats[:, :, :, :], ties[:, :, :, :], ALU.add).then_inc(beats_ready, 1)
            dve.wait_ge(beats_ready, 1 + LEAD)
            nc.vector.tensor_reduce(rank[:, :, :], beats[:, :, :, :], AX_X, ALU.add).then_inc(rank_ready, 1)
            dve.wait_ge(rank_ready, 1 + LEAD)
            nc.vector.tensor_scalar(rank[:, :, :], rank[:, :, :], 1.5, None, ALU.is_lt).then_inc(chosen, 1)
            dve.wait_ge(chosen, 1 + LEAD)
            dve.wait_ge(powers, 1 + LEAD)
            nc.vector.tensor_tensor(comb, comb, rank[:, :, :], ALU.mult).then_inc(weighed, 1)
            dve.wait_ge(weighed, 1 + LEAD)
            nc.vector.tensor_reduce(total[:, :], comb, AX_X, ALU.add).then_inc(summed, 1)
            dve.wait_ge(summed, 1 + LEAD)
            nc.vector.reciprocal(inverse[:, :], total[:, :]).then_inc(inverted, 1)
            dve.wait_ge(inverted, 1 + LEAD)
            nc.vector.tensor_tensor(comb, comb, inverse[:, :].unsqueeze(2).to_broadcast([128, NB, NE]), ALU.mult).then_inc(done, 1)

        @block.scalar
        def _(act):
            act.wait_ge(centered, 1 + LEAD)
            nc.scalar.activation(comb, comb, ACT.Exp).then_inc(powers, 1)


def l0_weights(nc, mem):
    w = mem.w
    with ExitStack() as ctx:
        (biased, rounded, done) = ctx.enter_context(signals(nc, "l0w", "biased", "rounded", "done"))
        block = ctx.enter_context(nc.Block())

        @block.tensor
        def _(pe):
            nc.tensor.matmul(mem.bank[0][:, 0:1], w["pw"], w["dw_bias"], start=True, stop=True).then_inc(biased, 1)

        @block.vector
        def _(dve):
            nc.vector.tensor_copy(mem.expert_high[:, :], w["experts"]).then_inc(rounded, 1)
            dve.wait_ge(rounded, 1 + LEAD)
            nc.vector.tensor_tensor(mem.expert_low[:, :], w["experts"], mem.expert_high[:, :], ALU.subtract)
            for k in range(3):
                nc.vector.tensor_scalar(mem.pw_taps[:, k, :], w["pw"], w["dw"][:, k:k + 1], None, ALU.mult)
            dve.wait_ge(biased, 1 + LEAD)
            nc.vector.tensor_tensor(mem.pw_bias[:, :], mem.bank[0][:, 0:1], w["pw_b"], ALU.add).then_inc(done, 1)


def l0_mixer(nc, stage, mem, U, logits):
    w = mem.w
    with ExitStack() as ctx:
        def sb(name, *shape):
            return ctx.enter_context(nc.sbuf_tensor(stage + "_" + name, [D, *shape], F32))
        upad = sb("upad", 2, SEQ_T, 2 + S)
        act_c = sb("c", 2, T)
        x1 = sb("x1", 2, T)
        (zeroed, padded, conv_ready, c_ready, x1_ready, stored, logits_ready, logits_read) = ctx.enter_context(signals(
            nc, stage, "zeroed", "padded", "conv", "c", "x1", "stored", "logits", "logits_read"))
        block = ctx.enter_context(nc.Block())

        @block.gpsimd
        def _(pool):
            nc.gpsimd.memset(upad[:, :, :, :], 0.0).then_inc(zeroed, 1)
            pool.wait_ge(zeroed, 1 + LEAD)

            def pad(t, s):
                pool.wait_ge(conv_ready, t - 1 + LEAD)
                pool.sem_inc(PASSED[0], 1)
                nc.gpsimd.tensor_copy(upad[:, s, :, 2:2 + S], U[:, cols(t)].rearrange("p (b t) -> p b t", b=SEQ_T)).then_inc(padded, 1)
            tile_pairs(pool, pad)

        @block.tensor
        def _(pe):
            def conv(t, s):
                pe.wait_ge(padded, t + 1 + LEAD)
                pe.wait_ge(c_ready, t - 1 + LEAD)
                for k in range(3):
                    last = nc.tensor.matmul(mem.bank[s].rearrange("p (b t) -> p b t", b=SEQ_T), mem.pw_taps[:, k, :],
                                            upad[:, s, :, k:k + S], start=(k == 0), stop=(k == 2))
                last.then_inc(conv_ready, 1)

            def route(t, s):
                pe.wait_ge(x1_ready, t + 1 + LEAD)
                pe.wait_ge(logits_read, t - 1 + LEAD)
                for j in range(SUB):
                    last = nc.tensor.matmul(mem.bank[2 + s][:, j * NE:(j + 1) * NE], x1[:, s, j * 128:(j + 1) * 128], w["router"],
                                            start=True, stop=True)
                last.then_inc(logits_ready, 1)

            conv(0, 0)
            with pe.Fori(0, NT // 2 - 1) as pair:
                for s in range(2):
                    conv(pair * 2 + s + 1, 1 - s)
                    route(pair * 2 + s, s)
            conv(NT - 1, 1)
            route(NT - 2, 0)
            route(NT - 1, 1)

        @block.scalar
        def _(act):
            def silu(t, s):
                act.wait_ge(x1_ready, t - 1 + LEAD)
                act.wait_ge(conv_ready, t + 1 + LEAD)
                nc.scalar.activation(act_c[:, s, :], mem.bank[s], ACT.Silu, bias=mem.pw_bias[:, :]).then_inc(c_ready, 1)

            def store(t, s):
                act.wait_ge(x1_ready, t + 1 + LEAD)
                act.sem_inc(PASSED[0], 1)
                nc.scalar.activation(U[:, cols(t)], x1[:, s, :], ACT.Identity).then_inc(stored, 1)

            silu(0, 0)
            with act.Fori(0, NT // 2 - 1) as pair:
                for s in range(2):
                    silu(pair * 2 + s + 1, 1 - s)
                    store(pair * 2 + s, s)
            silu(NT - 1, 1)
            store(NT - 2, 0)
            store(NT - 1, 1)

        @block.vector
        def _(dve):
            def add(t, s):
                dve.wait_ge(c_ready, t + 1 + LEAD)
                dve.wait_ge(logits_ready, t - 1 + LEAD)
                dve.wait_ge(stored, t - 1 + LEAD)
                nc.vector.tensor_tensor(x1[:, s, :], act_c[:, s, :], U[:, cols(t)], ALU.add).then_inc(x1_ready, 1)

            def take_logits(t, s):
                dve.wait_ge(logits_ready, t + 1 + LEAD)
                bias = w["router_b"].unsqueeze(1).to_broadcast([128, SUB, NE])
                nc.vector.tensor_tensor(logits[:, bass.ds(t * SUB, SUB), :], mem.bank[2 + s][:, 0:SUB * NE].rearrange("p (j e) -> p j e", j=SUB),
                                        bias, ALU.add).then_inc(logits_read, 1)

            add(0, 0)
            with dve.Fori(0, NT // 2 - 1) as pair:
                for s in range(2):
                    add(pair * 2 + s + 1, 1 - s)
                    take_logits(pair * 2 + s, s)
            add(NT - 1, 1)
            take_logits(NT - 2, 0)
            take_logits(NT - 1, 1)


def split_comb(nc, dve, comb, rest, parts, split):
    nc.vector.tensor_copy(parts[:, :, 0:NE], comb).then_inc(split, 1)
    dve.wait_ge(split, 1 + LEAD)
    nc.vector.tensor_tensor(rest, comb, parts[:, :, 0:NE], ALU.subtract).then_inc(split, 1)
    dve.wait_ge(split, 2 + LEAD)
    nc.vector.tensor_copy(parts[:, :, NE:2 * NE], rest).then_inc(split, 1)
    dve.wait_ge(split, 3 + LEAD)
    nc.vector.tensor_tensor(parts[:, :, 2 * NE:3 * NE], rest, parts[:, :, NE:2 * NE], ALU.subtract).then_inc(split, 1)


def tiles_with_next(eng, step):
    step(0, 0, False)
    with eng.Fori(0, NT // 2 - 1) as pair:
        step(pair * 2 + 1, 1, False)
        step(pair * 2 + 2, 0, False)
    step(NT - 1, 1, True)


def l0_experts(nc, stage, mem, U, comb):
    w = mem.w
    PAIRS = NE // 2
    with ExitStack() as ctx:
        def sb(name, *shape, dt=F32):
            return ctx.enter_context(nc.sbuf_tensor(stage + "_" + name, [D, *shape], dt))
        rest = sb("rest", NB, NE)
        parts = sb("parts", NB, 3 * NE, dt=BF16)
        tile_parts = sb("tile_parts", SUB, 3 * NE, dt=BF16)
        rows = sb("rows", 2, T, dt=BF16)
        x = sb("x", 2, 2, T, dt=F32R)
        ye = sb("ye", 2, T)
        weighed = sb("weighed", NE, T)
        total = sb("total", 2, T)
        (split, parts_copied, turned, rows_ready, x_high, x_ready, ye_ready, expert_ready, spread_ready, weighed_ready, paired, summed,
         out_ready, out_read) = ctx.enter_context(signals(
             nc, stage, "split", "parts_copied", "turned", "rows", "x_high", "x", "ye", "expert", "spread", "weighed", "paired",
             "summed", "out", "out_read"))
        block = ctx.enter_context(nc.Block())
        SUMS = PAIRS - 1

        @block.gpsimd
        def _(pool):
            def copy_parts(t):
                pool.wait_ge(turned, t + LEAD)
                pool.sem_inc(PASSED[0], 1)
                nc.gpsimd.tensor_copy(tile_parts[:, :, :], parts[:, bass.ds(t * SUB, SUB), :]).then_inc(parts_copied, 1)

            def x_low(t, s):
                pool.wait_ge(x_high, t + 1 + LEAD)
                pool.sem_inc(PASSED[0], 1)
                nc.gpsimd.tensor_tensor(x[:, s, 1, :], U[:, cols(t)], x[:, s, 0, :], ALU.subtract).then_inc(x_ready, 1)

            def tile(t, s, last):
                for p in range(PAIRS):
                    pool.wait_ge(weighed_ready, NE * t + 2 * p + 2 + LEAD)
                    pool.sem_inc(PASSED[0], 1)
                    nc.gpsimd.tensor_tensor(weighed[:, 2 * p, :], weighed[:, 2 * p, :], weighed[:, 2 * p + 1, :], ALU.add).then_inc(paired, 1)
                    if p == 0 and not last:
                        copy_parts(t + 1)
                    if p == 1 and not last:
                        x_low(t + 1, 1 - s)

            pool.wait_ge(split, 4 + LEAD)
            copy_parts(0)
            x_low(0, 0)
            tiles_with_next(pool, tile)

        @block.tensor
        def _(pe):
            def turn(t, s):
                pe.wait_ge(parts_copied, t + 1 + LEAD)
                pe.wait_ge(rows_ready, t + LEAD)
                pe.sem_inc(PASSED[0], 1)
                for j in range(SUB):
                    last = nc.tensor.matmul(mem.bank[6][0:3 * NE, j * 128:(j + 1) * 128], tile_parts[:, j, :], mem.ident16, start=True, stop=True)
                last.then_inc(turned, 1)

            def expert(t, s, e):
                if e == 0:
                    pe.wait_ge(x_ready, t + 1 + LEAD)
                pe.wait_ge(ye_ready, NE * t + e - 1 + LEAD)
                high, low = mem.expert_high[:, e * D:(e + 1) * D], mem.expert_low[:, e * D:(e + 1) * D]
                nc.tensor.matmul(mem.bank[e % 2], high, x[:, s, 0, :], start=True, stop=False)
                nc.tensor.matmul(mem.bank[e % 2], high, x[:, s, 1, :], start=False, stop=False)
                nc.tensor.matmul(mem.bank[e % 2], low, x[:, s, 0, :], start=False, stop=True).then_inc(expert_ready, 1)

            def spread(t, s, e):
                pe.wait_ge(rows_ready, t + 1 + LEAD)
                pe.wait_ge(weighed_ready, NE * t + e - 1 + LEAD)
                pe.sem_inc(PASSED[0], 1)
                nc.tensor.matmul(mem.bank[2 + e % 2], mem.one_hot[0:3 * NE, e:e + 1].to_broadcast([3 * NE, 128]), rows[0:3 * NE, s, :],
                                 start=True, stop=True).then_inc(spread_ready, 1)

            def project(t, s):
                pe.wait_ge(summed, SUMS * (t + 1) + LEAD)
                pe.wait_ge(out_read, t - 1 + LEAD)
                nc.tensor.matmul(mem.bank[4 + s], w["out"], total[:, s, :], start=True, stop=True).then_inc(out_ready, 1)

            def tile(t, s, last):
                for e in range(NE):
                    expert(t, s, e)
                    spread(t, s, e)
                    if e == 4 and (not isinstance(t, int) or t > 0):
                        project(t - 1, 1 - s)
                    if e == 5 and not last:
                        turn(t + 1, 1 - s)

            turn(0, 0)
            tiles_with_next(pe, tile)
            project(NT - 1, 1)

        @block.scalar
        def _(act):
            def take_rows(t, s):
                act.wait_ge(turned, t + 1 + LEAD)
                act.wait_ge(spread_ready, NE * (t - 1) + LEAD)
                nc.scalar.activation(rows[0:3 * NE, s, :], mem.bank[6][0:3 * NE, :], ACT.Identity).then_inc(rows_ready, 1)

            def take_x_high(t, s):
                act.wait_ge(expert_ready, NE * (t - 1) + LEAD)
                act.sem_inc(PASSED[0], 1)
                nc.scalar.activation(x[:, s, 0, :], U[:, cols(t)], ACT.Identity).then_inc(x_high, 1)

            def tile(t, s, last):
                for e in range(NE):
                    act.wait_ge(expert_ready, NE * t + e + 1 + LEAD)
                    act.wait_ge(weighed_ready, NE * t + e - 1 + LEAD)
                    nc.scalar.activation(ye[:, e % 2, :], mem.bank[e % 2], ACT.Silu, bias=w["expert_b"][:, e:e + 1]).then_inc(ye_ready, 1)
                    if e == 1 and not last:
                        take_x_high(t + 1, 1 - s)
                    if e == 5 and not last:
                        take_rows(t + 1, 1 - s)

            take_x_high(0, 0)
            take_rows(0, 0)
            tiles_with_next(act, tile)

        @block.vector
        def _(dve):
            def weigh(t, e):
                dve.wait_ge(ye_ready, NE * t + e + 1 + LEAD)
                dve.wait_ge(spread_ready, NE * t + e + 1 + LEAD)
                nc.vector.tensor_tensor(weighed[:, e, :], ye[:, e % 2, :], mem.bank[2 + e % 2], ALU.mult).then_inc(weighed_ready, 1)

            def add_pair(t, s, p):
                if p == 1:
                    dve.wait_ge(out_ready, t - 1 + LEAD)
                else:
                    dve.wait_ge(summed, SUMS * t + p - 1 + LEAD)
                dve.wait_ge(paired, PAIRS * t + p + 1 + LEAD)
                nc.vector.tensor_tensor(total[:, s, :], weighed[:, 0, :] if p == 1 else total[:, s, :], weighed[:, 2 * p, :],
                                        ALU.add).then_inc(summed, 1)

            def finish(t, s):
                dve.wait_ge(out_ready, t + 1 + LEAD)
                dve.wait_ge(x_ready, t + 1 + LEAD)
                nc.vector.scalar_tensor_tensor(U[:, cols(t)], mem.bank[4 + s], w["out_b"], U[:, cols(t)], ALU.add, ALU.add).then_inc(out_read, 1)

            def tile(t, s, last):
                follows = not isinstance(t, int) or t > 0
                for e in range(NE):
                    if e == 5:
                        add_pair(t, s, 1)
                    if e == 7:
                        add_pair(t, s, 2)
                    weigh(t, e)
                    if e == 1 and follows:
                        add_pair(t - 1, 1 - s, 3)
                    if e == 6 and follows:
                        finish(t - 1, 1 - s)

            split_comb(nc, dve, comb[:, :, :], rest[:, :, :], parts, split)
            tiles_with_next(dve, tile)
            add_pair(NT - 1, 1, 3)
            finish(NT - 1, 1)


def rms_norm(nc, stage, mem, U, weight):
    with ExitStack() as ctx:
        def sb(name, *shape):
            return ctx.enter_context(nc.sbuf_tensor(stage + "_" + name, [D, *shape], F32))
        sq, logv, rstd = sb("sq", 2, T), sb("logv", 2, T), sb("rstd", 2, T)
        (squared, var_ready, log_done, rstd_ready, scaled) = ctx.enter_context(signals(
            nc, stage, "squared", "var", "log", "rstd", "scaled"))
        block = ctx.enter_context(nc.Block())

        @block.gpsimd
        def _(pool):
            def square(t, s):
                pool.wait_ge(var_ready, t - 1 + LEAD)
                pool.sem_inc(PASSED[0], 1)
                nc.gpsimd.tensor_tensor(sq[:, s, :], U[:, cols(t)], U[:, cols(t)], ALU.mult).then_inc(squared, 1)
            tile_pairs(pool, square)

        @block.tensor
        def _(pe):
            def mean(t, s):
                pe.wait_ge(squared, t + 1 + LEAD)
                pe.wait_ge(log_done, t - 1 + LEAD)
                nc.tensor.matmul(mem.bank[s], mem.avg, sq[:, s, :], start=True, stop=True).then_inc(var_ready, 1)
            tile_pairs(pe, mean)

        @block.scalar
        def _(act):
            def rsqrt(t, s):
                act.wait_ge(var_ready, t + 1 + LEAD)
                act.wait_ge(scaled, t - 1 + LEAD)
                nc.scalar.activation(logv[:, s, :], mem.bank[s], ACT.Ln, bias=mem.const["eps6"], scale=1.0).then_inc(log_done, 1)
                act.wait_ge(log_done, t + 1 + LEAD)
                nc.scalar.activation(rstd[:, s, :], logv[:, s, :], ACT.Exp, scale=-0.5).then_inc(rstd_ready, 1)
            nc.scalar.preload_act_table_set(LN_AND_EXP)
            tile_pairs(act, rsqrt)

        @block.vector
        def _(dve):
            def scale(t, s):
                dve.wait_ge(rstd_ready, t + 1 + LEAD)
                nc.vector.scalar_tensor_tensor(U[:, cols(t)], U[:, cols(t)], weight, rstd[:, s, :], ALU.mult, ALU.mult).then_inc(scaled, 1)
            tile_pairs(dve, scale)


def l0_feed_forward(nc, stage, mem, X, U):
    w = mem.w
    with ExitStack() as ctx:
        g = ctx.enter_context(nc.sbuf_tensor(stage + "_g", [HID, 2, T], F32))
        branch = ctx.enter_context(nc.sbuf_tensor(stage + "_branch", [D, 2, T], F32))
        (down_ready, g_ready, up_ready, branch_ready, added) = ctx.enter_context(signals(
            nc, stage, "down", "g", "up", "branch", "added"))
        block = ctx.enter_context(nc.Block())

        @block.tensor
        def _(pe):
            def down(t, s):
                pe.wait_ge(g_ready, t - 1 + LEAD)
                nc.tensor.matmul(mem.bank[s][0:HID, :], w["down"], U[:, cols(t)], start=True, stop=True,
                                 ).then_inc(down_ready, 1)

            def up(t, s):
                pe.wait_ge(g_ready, t + 1 + LEAD)
                pe.wait_ge(branch_ready, t - 1 + LEAD)
                nc.tensor.matmul(mem.bank[2 + s], w["up"], g[:, s, :], start=True, stop=True).then_inc(up_ready, 1)

            down(0, 0)
            with pe.Fori(0, NT // 2 - 1) as pair:
                for s in range(2):
                    down(pair * 2 + s + 1, 1 - s)
                    up(pair * 2 + s, s)
            down(NT - 1, 1)
            up(NT - 2, 0)
            up(NT - 1, 1)

        @block.scalar
        def _(act):
            def gelu(t, s):
                act.wait_ge(down_ready, t + 1 + LEAD)
                act.wait_ge(up_ready, t - 1 + LEAD)
                nc.scalar.activation(g[:, s, :], mem.bank[s][0:HID, :], ACT.Gelu, bias=w["down_b"]).then_inc(g_ready, 1)
            tile_pairs(act, gelu)

        @block.vector
        def _(dve):
            def add(t, s):
                dve.wait_ge(up_ready, t + 1 + LEAD)
                dve.wait_ge(added, t - 1 + LEAD)
                nc.vector.scalar_tensor_tensor(branch[:, s, :], mem.bank[2 + s], w["up_b"], U[:, cols(t)], ALU.add, ALU.add).then_inc(branch_ready, 1)
                dve.wait_ge(branch_ready, t + 1 + LEAD)
                nc.vector.tensor_tensor(X[:, cols(t)], X[:, cols(t)], branch[:, s, :], ALU.add).then_inc(added, 1)
            tile_pairs(dve, add)


def l0_ffn(nc, stage, mem, X, U):
    with ExitStack() as ctx:
        logits = ctx.enter_context(nc.sbuf_tensor(stage + "_logits", [128, NB, NE], F32))
        comb = ctx.enter_context(nc.sbuf_tensor(stage + "_comb", [128, NB, NE], F32))
        layer_norm(nc, stage + "_ln", mem, X, U)
        l0_mixer(nc, stage + "_mix", mem, U, logits)
        top2_weights(nc, stage + "_top2", mem, logits[:, :, :], comb[:, :, :])
        l0_experts(nc, stage + "_moe", mem, U, comb)
        rms_norm(nc, stage + "_rms", mem, U, mem.w["norm_w"])
        l0_feed_forward(nc, stage + "_ff", mem, X, U)


STEPS = T // NSEQ


def rnn(nc, mem, U, H):
    w = mem.w
    with ExitStack() as ctx:
        (input_ready, pre_ready, h_ready) = ctx.enter_context(signals(nc, "rnn", "input", "pre", "h"))
        start = ctx.enter_context(nc.sbuf_tensor("rnn_start", [D, NSEQ], F32))
        h = ctx.enter_context(nc.sbuf_tensor("rnn_h", [D, 2, STEPS, NSEQ], F32))
        (kept,) = ctx.enter_context(signals(nc, "rnn_keep", "kept"))
        block = ctx.enter_context(nc.Block())
        by_time = U[:, :].rearrange("p (b t) -> p t b", b=NSEQ)
        NCH = S // STEPS

        @block.tensor
        def _(pe):
            def inputs(c, par):
                nc.tensor.matmul(mem.bank[par].rearrange("p (t b) -> p t b", b=NSEQ), w["rnn_B"],
                                 by_time[:, bass.ds(c * STEPS, STEPS), :], start=True, stop=False, skip_group_check=True)

            def chunk(c, par, more):
                for k in range(STEPS):
                    if k == STEPS // 2 and more:
                        pe.wait_ge(h_ready, STEPS * c + 1 + LEAD)
                        inputs(c + 1, 1 - par)
                    first = isinstance(c, int) and c == 0 and k == 0
                    if not first:
                        pe.wait_ge(h_ready, STEPS * c + k + LEAD)
                    before = start[:, :] if first else (h[:, par, k - 1, :] if k else h[:, 1 - par, STEPS - 1, :])
                    nc.tensor.matmul(mem.bank[par][:, k * NSEQ:(k + 1) * NSEQ], w["rnn_A"], before, start=False, stop=True,
                                     skip_group_check=True).then_inc(pre_ready, 1)

            pe.wait_ge(input_ready, 1 + LEAD)
            inputs(0, 0)
            chunk(0, 0, True)
            chunk(1, 1, True)
            with pe.Fori(1, NCH // 2 - 1) as pair:
                for par in range(2):
                    chunk(pair * 2 + par, par, True)
            chunk(NCH - 2, 0, True)
            chunk(NCH - 1, 1, False)

        @block.scalar
        def _(act):
            def chunk(c, par):
                for k in range(STEPS):
                    if k == 0:
                        act.wait_ge(kept, c - 1 + LEAD)
                    act.wait_ge(pre_ready, STEPS * c + k + 1 + LEAD)
                    nc.scalar.activation(h[:, par, k, :], mem.bank[par][:, k * NSEQ:(k + 1) * NSEQ], ACT.Tanh).then_inc(h_ready, 1)
            with act.Fori(0, NCH // 2) as pair:
                for par in range(2):
                    chunk(pair * 2 + par, par)

        @block.vector
        def _(dve):
            nc.vector.memset(start[:, :], 0.0).then_inc(input_ready, 1)
            h_by_time = H[:, :].rearrange("p (b t) -> p t b", b=NSEQ)
            with dve.Fori(0, NCH // 2) as pair:
                for par in range(2):
                    c = pair * 2 + par
                    dve.wait_ge(h_ready, STEPS * c + STEPS + LEAD)
                    nc.vector.tensor_scalar(h_by_time[:, bass.ds(c * STEPS, STEPS), :], h[:, par, :, :], 1.0, None, ALU.mult).then_inc(kept, 1)


def project_add(nc, stage, mem, weight, src, dst, bias=None):
    with ExitStack() as ctx:
        (ready, added) = ctx.enter_context(signals(nc, stage, "ready", "added"))
        block = ctx.enter_context(nc.Block())

        @block.tensor
        def _(pe):
            def step(t, s):
                pe.wait_ge(added, t - 1 + LEAD)
                nc.tensor.matmul(mem.bank[s], weight, src[:, cols(t)], start=True, stop=True).then_inc(ready, 1)
            tile_pairs(pe, step)

        @block.vector
        def _(dve):
            def step(t, s):
                dve.wait_ge(ready, t + 1 + LEAD)
                if bias is None:
                    nc.vector.tensor_tensor(dst[:, cols(t)], dst[:, cols(t)], mem.bank[s], ALU.add).then_inc(added, 1)
                else:
                    nc.vector.scalar_tensor_tensor(dst[:, cols(t)], mem.bank[s], bias, dst[:, cols(t)], ALU.add, ALU.add).then_inc(added, 1)
            tile_pairs(dve, step)


def add_all(nc, stage, mem, src, dst):
    with ExitStack() as ctx:
        (added,) = ctx.enter_context(signals(nc, stage, "added"))
        block = ctx.enter_context(nc.Block())

        @block.vector
        def _(dve):
            def step(t, s):
                nc.vector.tensor_tensor(dst[:, cols(t)], dst[:, cols(t)], src[:, cols(t)], ALU.add).then_inc(added, 1)
            tile_pairs(dve, step)


def recurrent(nc, mem, X, U):
    layer_norm(nc, "rnn_ln", mem, X, U)
    with nc.sbuf_tensor("H", [D, TOK], F32) as H:
        rnn(nc, mem, U, H)
        project_add(nc, "rnn_out", mem, mem.w["rnn_C"], H, U)
        layer_norm(nc, "rnn_ln2", mem, U, H, affine=(mem.w["rnn_gamma"], mem.w["rnn_beta"]))
        add_all(nc, "rnn_add", mem, H, X)


F = 512
CH = F // 128
LIMIT = 10.0


def l1_router(nc, stage, mem, U, logits):
    w = mem.w
    with ExitStack() as ctx:
        x = ctx.enter_context(nc.sbuf_tensor(stage + "_x", [D, 2, T], F32))
        (copied, logits_ready, logits_read) = ctx.enter_context(signals(nc, stage, "copied", "logits", "logits_read"))
        block = ctx.enter_context(nc.Block())

        @block.scalar
        def _(act):
            def step(t, s):
                act.wait_ge(logits_ready, t - 1 + LEAD)
                act.sem_inc(PASSED[0], 1)
                nc.scalar.activation(x[:, s, :], U[:, cols(t)], ACT.Identity).then_inc(copied, 1)
            tile_pairs(act, step)

        @block.tensor
        def _(pe):
            def step(t, s):
                pe.wait_ge(copied, t + 1 + LEAD)
                pe.wait_ge(logits_read, t - 1 + LEAD)
                for j in range(SUB):
                    last = nc.tensor.matmul(mem.bank[s][:, j * NE:(j + 1) * NE], x[:, s, j * 128:(j + 1) * 128], w["l1_router"],
                                            start=True, stop=True)
                last.then_inc(logits_ready, 1)
            tile_pairs(pe, step)

        @block.vector
        def _(dve):
            def step(t, s):
                dve.wait_ge(logits_ready, t + 1 + LEAD)
                dve.sem_inc(PASSED[0], 1)
                nc.vector.tensor_copy(logits[:, bass.ds(t * SUB, SUB), :], mem.bank[s][:, 0:SUB * NE].rearrange("p (j e) -> p j e", j=SUB)).then_inc(logits_read, 1)
            tile_pairs(dve, step)


def l1_experts(nc, stage, mem, X, U, comb, out=None):
    NCHUNK = NE * CH + 1
    with ExitStack() as ctx:
        def sb(name, *shape, dt=F32):
            return ctx.enter_context(nc.sbuf_tensor(stage + "_" + name, [D, *shape], dt))
        parts = sb("parts", NB, 3 * NE, dt=BF16)
        tile_parts = sb("tile_parts", SUB, 3 * NE, dt=BF16)
        rows = sb("rows", 2, T, dt=BF16)
        x = sb("x", 2, 2, T, dt=F32R)
        weighed = sb("weighed", T)
        xw = sb("xw", 2, 2, T, dt=F32R)
        act = sb("act", 3, T)
        hidden = sb("hidden", 2, 2, T, dt=F32R)
        (split, parts_copied, turned, rows_ready, spread_ready, weighed_ready, xw_high, xw_ready, x_high, x_ready, gate_ready, clipped,
         silu_ready, up_ready, multiplied, high_ready, low_ready, down_done, added, in_dram) = ctx.enter_context(signals(
             nc, stage, "split", "parts_copied", "turned", "rows", "spread", "weighed", "xw_high", "xw", "x_high", "x", "gate", "clipped",
             "silu", "up", "multiplied", "high", "low", "down", "added", "in_dram"))
        block = ctx.enter_context(nc.Block())
        where = mem.moe_where

        def at(t, s, c):
            if c < 0:
                return t - 1, 1 - s, c + NCHUNK
            if c >= NCHUNK:
                return t + 1, 1 - s, c - NCHUNK
            return t, s, c

        def parity(s, c):
            return (s + c) % 2

        def number(t, c):
            return NCHUNK * t + c

        def next_expert(t, s, c):
            e = c // CH + 1
            return (t, s, e) if e < NE else (t + 1, 1 - s, 0)

        def weighs(c, last):
            return c % CH == 1 and c < NE * CH and not (last and c // CH + 1 == NE)

        def chunk_weights(c, kind):
            if c == NCHUNK - 1:
                lo = where["shared_" + kind][1]
            elif kind == "down":
                lo = where["l1_down"][1] + c * D
            else:
                lo = where["gate_up"][1] + c // CH * 2 * F + (F if kind == "up" else 0) + c % CH * 128
            return mem.w_high[:, lo:lo + 128], mem.w_low[:, lo:lo + 128]

        if out is not None:
            @block.sync
            def _(sp):
                for pair in range(NT // 2):
                    sp.wait_ge(added, 2 * (pair + 1) + LEAD)
                    sp.dma_start(out[:, cols(pair, 2 * T)], X[:, cols(pair, 2 * T)]).then_inc(in_dram, 16)
                sp.wait_ge(in_dram, 16 * (NT // 2) + LEAD)

        @block.gpsimd
        def _(pool):
            def split_x(t, s):
                pool.wait_ge(up_ready, NCHUNK * (t - 1) + LEAD)
                pool.sem_inc(PASSED[0], 1)
                nc.gpsimd.tensor_copy(x[:, s, 0, :], U[:, cols(t)]).then_inc(x_high, 1)
                pool.wait_ge(x_high, t + 1 + LEAD)
                pool.sem_inc(PASSED[0], 1)
                nc.gpsimd.tensor_tensor(x[:, s, 1, :], U[:, cols(t)], x[:, s, 0, :], ALU.subtract).then_inc(x_ready, 1)

            def copy_parts(t):
                pool.wait_ge(turned, t + LEAD)
                pool.sem_inc(PASSED[0], 1)
                nc.gpsimd.tensor_copy(tile_parts[:, :, :], parts[:, bass.ds(t * SUB, SUB), :]).then_inc(parts_copied, 1)

            def xw_low(t, e):
                pool.wait_ge(xw_high, NE * t + e + 1 + LEAD)
                pool.sem_inc(PASSED[0], 1)
                nc.gpsimd.tensor_tensor(xw[:, e % 2, 1, :], weighed[:, :], xw[:, e % 2, 0, :], ALU.subtract).then_inc(xw_ready, 1)

            def low(t, s, c):
                pool.wait_ge(high_ready, number(t, c) + 1 + LEAD)
                pool.sem_inc(PASSED[0], 1)
                nc.gpsimd.tensor_tensor(hidden[:, parity(s, c), 1, :], act[:, c % 3, :], hidden[:, parity(s, c), 0, :],
                                        ALU.subtract).then_inc(low_ready, 1)

            def tile(t, s, last):
                for c in range(NCHUNK):
                    low(t, s, c)
                    if weighs(c, last):
                        nt, ns, e = next_expert(t, s, c)
                        xw_low(nt, e)
                    if c == 14 and not last:
                        copy_parts(t + 1)
                    if c == 18 and not last:
                        split_x(t + 1, 1 - s)

            pool.wait_ge(split, 4 + LEAD)
            copy_parts(0)
            split_x(0, 0)
            xw_low(0, 0)
            tiles_with_next(pool, tile)

        @block.tensor
        def _(pe):
            def product(to, weights, x, start=True, stop=True):
                nc.tensor.matmul(to, weights[0], x[:, 0, :], start=start, stop=False)
                nc.tensor.matmul(to, weights[0], x[:, 1, :], start=False, stop=False)
                return nc.tensor.matmul(to, weights[1], x[:, 0, :], start=False, stop=stop)

            def turn(t, s):
                pe.wait_ge(parts_copied, t + 1 + LEAD)
                pe.wait_ge(rows_ready, t + LEAD)
                pe.sem_inc(PASSED[0], 1)
                for j in range(SUB):
                    last = nc.tensor.matmul(mem.bank[7][0:3 * NE, j * 128:(j + 1) * 128], tile_parts[:, j, :], mem.ident16, start=True, stop=True)
                last.then_inc(turned, 1)

            def spread(t, s, e):
                pe.wait_ge(rows_ready, t + 1 + LEAD)
                pe.wait_ge(weighed_ready, NE * t + e + LEAD)
                pe.sem_inc(PASSED[0], 1)
                nc.tensor.matmul(mem.bank[4], mem.one_hot[0:3 * NE, e:e + 1].to_broadcast([3 * NE, 128]), rows[0:3 * NE, s, :],
                                 start=True, stop=True).then_inc(spread_ready, 1)

            def gate(t, s, c):
                if c == 0:
                    pe.wait_ge(x_ready, t + 1 + LEAD)
                pe.wait_ge(clipped, number(t, c) - 1 + LEAD)
                product(mem.bank[parity(s, c)], chunk_weights(c, "gate"), x[:, s, :, :]).then_inc(gate_ready, 1)

            def up(t, s, c):
                if c % CH == 0 and c < NE * CH:
                    pe.wait_ge(xw_ready, NE * t + c // CH + 1 + LEAD)
                pe.wait_ge(multiplied, number(t, c) - 1 + LEAD)
                product(mem.bank[2 + parity(s, c)], chunk_weights(c, "up"),
                        xw[:, c // CH % 2, :, :] if c < NE * CH else x[:, s, :, :]).then_inc(up_ready, 1)

            def down(t, s, c):
                if c == 0:
                    pe.wait_ge(added, t - 1 + LEAD)
                pe.wait_ge(low_ready, number(t, c) + 1 + LEAD)
                product(mem.bank[5 + s], chunk_weights(c, "down"), hidden[:, parity(s, c), :, :],
                        start=(c == 0), stop=(c == NCHUNK - 1)).then_inc(down_done, 1)

            def tile(t, s, last):
                for c in range(NCHUNK):
                    if not (last and c == NCHUNK - 1):
                        gate(*at(t, s, c + 1))
                    up(t, s, c)
                    if weighs(c, last):
                        spread(*next_expert(t, s, c))
                    if c == 22 and not last:
                        turn(t + 1, 1 - s)
                    if c >= 2 or not isinstance(t, int) or t > 0:
                        down(*at(t, s, c - 2))

            turn(0, 0)
            spread(0, 0, 0)
            gate(0, 0, 0)
            tiles_with_next(pe, tile)
            down(NT - 1, 1, NCHUNK - 2)
            down(NT - 1, 1, NCHUNK - 1)

        @block.scalar
        def _(scalar):
            def take_rows(t, s):
                scalar.wait_ge(turned, t + 1 + LEAD)
                scalar.wait_ge(spread_ready, NE * (t - 1) + LEAD)
                nc.scalar.activation(rows[0:3 * NE, s, :], mem.bank[7][0:3 * NE, :], ACT.Identity).then_inc(rows_ready, 1)

            def take_xw_high(t, s, e):
                used = NCHUNK * t + CH * (e - 1) if e >= 2 else NCHUNK * (t - 1) + CH * (e + NE - 1)
                scalar.wait_ge(weighed_ready, NE * t + e + 1 + LEAD)
                scalar.wait_ge(up_ready, used + LEAD)
                nc.scalar.activation(xw[:, e % 2, 0, :], weighed[:, :], ACT.Identity).then_inc(xw_high, 1)

            def silu(t, s, c):
                scalar.wait_ge(clipped, number(t, c) + 1 + LEAD)
                nc.scalar.activation(act[:, c % 3, :], act[:, c % 3, :], ACT.Silu).then_inc(silu_ready, 1)

            def high(t, s, c):
                scalar.wait_ge(multiplied, number(t, c) + 1 + LEAD)
                scalar.wait_ge(down_done, number(t, c) - 1 + LEAD)
                nc.scalar.activation(hidden[:, parity(s, c), 0, :], act[:, c % 3, :], ACT.Identity).then_inc(high_ready, 1)

            def tile(t, s, last):
                for c in range(NCHUNK):
                    if not (last and c == NCHUNK - 1):
                        silu(*at(t, s, c + 1))
                    if weighs(c, last):
                        take_xw_high(*next_expert(t, s, c))
                    if c == 22 and not last:
                        take_rows(t + 1, 1 - s)
                    high(t, s, c)

            take_rows(0, 0)
            take_xw_high(0, 0, 0)
            silu(0, 0, 0)
            tiles_with_next(scalar, tile)

        @block.vector
        def _(dve):
            def weigh(t, s, e):
                dve.wait_ge(spread_ready, NE * t + e + 1 + LEAD)
                dve.wait_ge(xw_ready, NE * t + e + LEAD)
                nc.vector.tensor_tensor(weighed[:, :], U[:, cols(t)], mem.bank[4], ALU.mult).then_inc(weighed_ready, 1)

            def clip(t, s, c):
                dve.wait_ge(gate_ready, number(t, c) + 1 + LEAD)
                dve.wait_ge(low_ready, number(t, c) - 2 + LEAD)
                nc.vector.tensor_scalar(act[:, c % 3, :], mem.bank[parity(s, c)], -LIMIT, LIMIT, ALU.max, ALU.min).then_inc(clipped, 1)

            def multiply(t, s, c):
                dve.wait_ge(silu_ready, number(t, c) + 1 + LEAD)
                dve.wait_ge(up_ready, number(t, c) + 1 + LEAD)
                nc.vector.tensor_tensor(act[:, c % 3, :], act[:, c % 3, :], mem.bank[2 + parity(s, c)], ALU.mult).then_inc(multiplied, 1)

            def add(t, s):
                dve.wait_ge(down_done, NCHUNK * (t + 1) + LEAD)
                nc.vector.tensor_tensor(X[:, cols(t)], X[:, cols(t)], mem.bank[5 + s], ALU.add).then_inc(added, 1)

            def tile(t, s, last):
                for c in range(NCHUNK):
                    if not (last and c == NCHUNK - 1):
                        clip(*at(t, s, c + 1))
                    multiply(t, s, c)
                    if weighs(c, last):
                        weigh(*next_expert(t, s, c))
                    if c == 3 and (not isinstance(t, int) or t > 0):
                        add(t - 1, 1 - s)

            split_comb(nc, dve, comb[:, :, :], act[:, 0, :].rearrange("p (b e) -> p b e", e=NE), parts, split)
            dve.wait_ge(split, 4 + LEAD)
            weigh(0, 0, 0)
            clip(0, 0, 0)
            tiles_with_next(dve, tile)
            add(NT - 1, 1)


def load_split(nc, ctx, mem, stage, dram, where):
    n = dram.shape[1]
    pieces = 8
    size = n // pieces
    mem.moe_where = where
    mem.w_high = ctx.enter_context(nc.sbuf_tensor(stage + "_high", [D, n], F32R))
    mem.w_low = ctx.enter_context(nc.sbuf_tensor(stage + "_low", [D, n], F32R))
    with ExitStack() as inner:
        SLOTS = 4
        whole = inner.enter_context(nc.sbuf_tensor(stage + "_whole", [D, SLOTS, size], F32))
        (landed_0, landed_1, landed_2, landed_3, rounded, done) = inner.enter_context(signals(
            nc, stage + "_load", "landed_0", "landed_1", "landed_2", "landed_3", "rounded", "done"))
        landed = (landed_0, landed_1, landed_2, landed_3)
        block = inner.enter_context(nc.Block())

        @block.sync
        def _(sp):
            for i in range(pieces):
                if i >= SLOTS:
                    sp.wait_ge(done, i - SLOTS + 1 + LEAD)
                sp.dma_start(whole[:, i % SLOTS, :], dram[:, i * size:(i + 1) * size]).then_inc(landed[i % SLOTS], 16)

        @block.scalar
        def _(act):
            for i in range(pieces):
                act.wait_ge(landed[i % SLOTS], 16 * (i // SLOTS + 1) + LEAD)
                nc.scalar.activation(mem.w_high[:, i * size:(i + 1) * size], whole[:, i % SLOTS, :], ACT.Identity).then_inc(rounded, 1)

        @block.vector
        def _(dve):
            for i in range(pieces):
                dve.wait_ge(rounded, i + 1 + LEAD)
                nc.vector.tensor_tensor(mem.w_low[:, i * size:(i + 1) * size], whole[:, i % SLOTS, :], mem.w_high[:, i * size:(i + 1) * size],
                                        ALU.subtract).then_inc(done, 1)


def l1_ffn(nc, stage, mem, X, U, experts, out=None):
    with ExitStack() as ctx:
        comb = ctx.enter_context(nc.sbuf_tensor(stage + "_comb", [128, NB, NE], F32))
        layer_norm(nc, stage + "_ln", mem, X, U, affine=(mem.w["l1_gamma"], mem.w["l1_beta"]), twice=True)
        with nc.sbuf_tensor(stage + "_logits", [128, NB, NE], F32) as logits:
            l1_router(nc, stage + "_route", mem, U, logits)
            top2_weights(nc, stage + "_top2", mem, logits[:, :, :], comb[:, :, :])
        load_split(nc, ctx, mem, stage, *experts)
        l1_experts(nc, stage + "_moe", mem, X, U, comb, out)


HEADS, HD = 16, 8
LHEADS, LD = 4, 32
LAT = 64
POOLED = S // LAT
QB = 2
SCALE = float(HD) ** -0.5


def attend(nc, stage, mem, *, rows, groups, heads, widths, chunk, q, head_mask, keys, masks, values, dst, valid=None, mix=None):
    H = groups * heads
    SP = heads * max(widths)
    with ExitStack() as ctx:
        def sb(name, *shape):
            return ctx.enter_context(nc.sbuf_tensor(stage + "_" + name, [128, *shape], F32))
        qm = sb("qm", QB, H, 128)
        top = sb("top", 2, heads)
        probs = sb("probs", 2, SP)
        turned = sb("turned", 2, SP // chunk * 128)
        inverse = sb("inverse", 2, H)
        heads_out = sb("heads_out", 2, H * HD)
        (qm_ready, scores_ready, top_ready, centered, powers, turn_ready, turned_ready, summed, inverted, masked, heads_ready,
         out_ready, stored) = ctx.enter_context(signals(
            nc, stage, "qm", "scores", "top", "centered", "powers", "turn", "turned", "summed", "inverted", "masked", "heads",
            "out", "stored"))
        if mix is not None:
            mix.allocate(nc, ctx, stage)
        block = ctx.enter_context(nc.Block())
        N = QB * groups
        REACH = 4

        def scores_at(slot, width):
            return mem.psum[:, 2 * slot:2 * slot + 2, :].rearrange("p a t -> p (a t)")[:, 0:heads * width]

        turn_ps = mem.psum[:, 4:6, :].rearrange("p a t -> p (a t)")

        def sums_at(qb):
            return mem.bank[6][:, qb * 256:qb * 256 + H * (HD + 1)].rearrange("p (h d) -> p h d", h=H)

        out_ps = mem.bank[7][0:rows, 0:128]

        def index(b, g):
            return b * N + g

        def back(b, g, n):
            g -= n
            while g < 0:
                b, g = b - 1, g + N
            if isinstance(b, int) and (b < 0 or b >= NSEQ):
                return None
            return b, g

        def schedule(eng, step):
            first = -(-REACH // N)
            for g in range(first * N):
                step(g // N, g % N)
            with eng.Fori(first, NSEQ) as b:
                for g in range(N):
                    step(b, g)
            for g in range(REACH):
                step(NSEQ + g // N, g % N)

        def n_slot(at):
            return at[1] % 2

        def is_last(at):
            return at is not None and at[1] % groups == groups - 1

        def unit(at):
            return at[0] * QB + at[1] // groups, at[1] // groups

        def tokens(at):
            return bass.ds(at[0] * S + (at[1] // groups) * 128, 128)

        def live(b):
            return not (isinstance(b, int) and b >= NSEQ)

        @block.gpsimd
        def _(pool):
            def blocks(b):
                for qb in range(QB):
                    u = b * QB + qb
                    pool.wait_ge(scores_ready, (u - 1) * groups + LEAD)
                    pool.sem_inc(PASSED[0], 1)
                    nc.gpsimd.tensor_tensor(qm[0:rows, qb, :, :], q[:, bass.ds(b * S + qb * 128, 128)].unsqueeze(1).to_broadcast([rows, H, 128]),
                                            head_mask.unsqueeze(2).to_broadcast([rows, H, 128]), ALU.mult).then_inc(qm_ready, 1)
                    if mix is not None:
                        mix.load(pool, b, qb, u)
            with pool.Fori(0, NSEQ) as b:
                blocks(b)

        @block.tensor
        def _(pe):
            def scores(b, g):
                qb, hg = g // groups, g % groups
                width = widths[qb]
                slot = index(0, g) % 2
                if hg == 0:
                    pe.wait_ge(qm_ready, b * QB + qb + 1 + LEAD)
                pe.wait_ge(centered, index(b, g) - 1 + LEAD)
                per_bank = min(heads, T // width)
                out = scores_at(slot, width).rearrange("p (h k) -> p h k", h=heads)
                for h0 in range(0, heads, per_bank):
                    for i, (k0, mask) in enumerate(masks[qb]):
                        nc.tensor.matmul(out[:, h0:h0 + per_bank, k0:k0 + chunk], mem.ident16,
                                         mask.unsqueeze(1).to_broadcast([128, per_bank, chunk]), start=(i == 0), stop=False, skip_group_check=True)
                    for h in range(h0, h0 + per_bank):
                        last = nc.tensor.matmul(out[:, h, :], qm[0:rows, qb, hg * heads + h, :], keys(b, width), start=False,
                                                stop=True, skip_group_check=True)
                last.then_inc(scores_ready, 1)

            def turn(at):
                n = index(*at)
                width = widths[at[1] // groups]
                pe.wait_ge(powers, n + 1 + LEAD)
                if chunk < 128:
                    pe.sem_inc(PASSED[0], 1)
                pe.wait_ge(turned_ready, n + LEAD)
                if chunk < 128:
                    pe.sem_inc(PASSED[0], 1)
                for h in range(heads):
                    for c in range(width // chunk):
                        i = h * (width // chunk) + c
                        last = nc.tensor.transpose(turn_ps[0:chunk, i * 128:(i + 1) * 128],
                                                   probs[:, n_slot(at), h * width + c * chunk:h * width + (c + 1) * chunk], mem.ident)
                last.then_inc(turn_ready, 1)

            def weigh(at):
                n = index(*at)
                b, g = at
                qb, hg = g // groups, g % groups
                nch = widths[qb] // chunk
                u, _ = unit(at)
                pe.wait_ge(turned_ready, n + 1 + LEAD)
                if chunk < 128:
                    pe.sem_inc(PASSED[0], 1)
                if hg == 0:
                    if mix is None:
                        pe.wait_ge(heads_ready, u + LEAD)
                        if chunk < 128:
                            pe.sem_inc(PASSED[0], 1)
                    else:
                        pe.wait_ge(mix.step, STEPS_OF_MIX * (u - 1) + 1 + LEAD)
                if mix is not None and is_last(at):
                    pe.wait_ge(stored, u + LEAD)
                    mix.product(pe, u, qb)
                for h in range(heads):
                    for c in range(nch):
                        i = h * nch + c
                        last = nc.tensor.matmul(sums_at(qb)[:, hg * heads + h, :], turned[0:chunk, n_slot(at), i * 128:(i + 1) * 128],
                                                values(b, c, hg * heads + h), start=(c == 0), stop=(c == nch - 1), skip_group_check=True)
                last.then_inc(summed, 1)

            def turn_out(at):
                u, qb = unit(at)
                pe.wait_ge(heads_ready, u + 1 + LEAD)
                pe.wait_ge(stored, u + LEAD)
                nc.tensor.transpose(out_ps, heads_out[:, qb, :], mem.ident).then_inc(out_ready, 1)

            def step(b, g):
                if live(b):
                    scores(b, g)
                if back(b, g, 2):
                    turn(back(b, g, 2))
                if back(b, g, 3):
                    weigh(back(b, g, 3))
                if is_last(back(b, g, 4)):
                    turn_out(back(b, g, 4))

            schedule(pe, step)

        @block.vector
        def _(dve):
            def center(b, g):
                n = index(b, g)
                width = widths[g // groups]
                ps = scores_at(g % 2, width).rearrange("p (h k) -> p h k", h=heads)
                dve.wait_ge(scores_ready, n + 1 + LEAD)
                nc.vector.tensor_reduce(top[:, g % 2, :], ps, AX_X, ALU.max).then_inc(top_ready, 1)
                dve.wait_ge(turn_ready, n - 1 + LEAD)
                dve.wait_ge(top_ready, n + 1 + LEAD)
                nc.vector.tensor_tensor(probs[:, g % 2, 0:heads * width].rearrange("p (h k) -> p h k", h=heads), ps,
                                        top[:, g % 2, :].unsqueeze(2).to_broadcast([128, heads, width]), ALU.subtract).then_inc(centered, 1)

            def finish(at):
                u, qb = unit(at)
                sums = sums_at(qb)
                dve.wait_ge(summed, u * groups + groups + LEAD)
                nc.vector.reciprocal(inverse[:, qb, :], sums[:, :, HD]).then_inc(inverted, 1)
                dve.wait_ge(inverted, u + 1 + LEAD)
                if valid is not None and qb == 0:
                    nc.vector.tensor_scalar(inverse[:, qb, :], inverse[:, qb, :], valid, None, ALU.mult).then_inc(masked, 1)
                    dve.wait_ge(masked, at[0] + 1 + LEAD)
                out = heads_out[:, qb, :].rearrange("p (h d) -> p h d", h=H)
                by_head = inverse[:, qb, :].unsqueeze(2).to_broadcast([128, H, HD])
                dve.wait_ge(out_ready, u - 1 + LEAD)
                if mix is None:
                    nc.vector.tensor_tensor(out, sums[:, :, 0:HD], by_head, ALU.mult).then_inc(heads_ready, 1)
                else:
                    mix.combine(dve, u, qb, lambda: nc.vector.tensor_tensor(out, sums[:, :, 0:HD], by_head, ALU.mult),
                                heads_out[:, qb, :], heads_ready)

            def step(b, g):
                if live(b):
                    center(b, g)
                if is_last(back(b, g, 3)):
                    finish(back(b, g, 3))

            schedule(dve, step)

        @block.scalar
        def _(act):
            def power(b, g):
                n = index(b, g)
                width = heads * widths[g // groups]
                act.wait_ge(centered, n + 1 + LEAD)
                nc.scalar.activation(probs[:, g % 2, 0:width], probs[:, g % 2, 0:width], ACT.Exp, scale=SCALE).then_inc(powers, 1)

            def take_turned(at):
                n = index(*at)
                width = heads * widths[at[1] // groups] // chunk * 128
                act.wait_ge(turn_ready, n + 1 + LEAD)
                act.wait_ge(summed, n - 1 + LEAD)
                nc.scalar.activation(turned[0:chunk, at[1] % 2, 0:width], turn_ps[0:chunk, 0:width], ACT.Identity).then_inc(turned_ready, 1)

            def store(at):
                u, qb = unit(at)
                act.wait_ge(out_ready, u + 1 + LEAD)
                act.sem_inc(PASSED[0], 1)
                nc.scalar.activation(dst[:, tokens(at)], out_ps, ACT.Identity).then_inc(stored, 1)

            def step(b, g):
                if back(b, g, 2):
                    take_turned(back(b, g, 2))
                if live(b):
                    power(b, g)
                if is_last(back(b, g, 3)) and mix is not None:
                    mix.gate(act, *unit(back(b, g, 3)))
                if is_last(back(b, g, 4)):
                    store(back(b, g, 4))

            schedule(act, step)


class GateMix:

    def __init__(self, mem, lat):
        self.mem, self.lat = mem, lat

    def allocate(self, nc, ctx, stage):
        def sb(name, *shape):
            return ctx.enter_context(nc.sbuf_tensor(stage + "_" + name, [128, *shape], F32))
        self.nc = nc
        self.lat_block = sb("lat_block", QB, 128)
        self.remote = sb("remote", D)
        self.dots = sb("dots", 2, D)
        self.z = sb("z", QB, HEADS)
        (self.lat_ready, self.product_ready, self.step, self.z_ready, self.g_ready) = ctx.enter_context(
            signals(nc, stage + "_mix", "lat", "product", "step", "z", "g"))
        self.ps = self.mem.bank[7][:, 256:384]

    def load(self, pool, b, qb, u):
        pool.wait_ge(self.product_ready, u - 1 + LEAD)
        pool.sem_inc(PASSED[0], 1)
        self.nc.gpsimd.tensor_copy(self.lat_block[0:LD, qb, :], self.lat[:, bass.ds(b * S + qb * 128, 128)]).then_inc(self.lat_ready, 1)

    def product(self, pe, u, qb):
        pe.wait_ge(self.lat_ready, u + 1 + LEAD)
        pe.wait_ge(self.step, STEPS_OF_MIX * u + LEAD)
        self.nc.tensor.matmul(self.ps, self.lat_block[0:LD, qb, :], self.mem.w["rout"], start=True, stop=True).then_inc(self.product_ready, 1)

    def combine(self, dve, u, qb, local, L, done):
        nc, w = self.nc, self.mem.w
        R, dots, z = self.remote[:, :], self.dots[:, :, :], self.z[:, qb, :]
        n = STEPS_OF_MIX * u
        dve.wait_ge(done, u + LEAD)
        local().then_inc(self.step, 1)
        dve.wait_ge(self.product_ready, u + 1 + LEAD)
        nc.vector.tensor_tensor(R, self.ps, w["rout_b"], ALU.add).then_inc(self.step, 1)
        dve.wait_ge(self.step, n + 1 + LEAD)
        nc.vector.tensor_tensor(dots[:, 0, :], L, w["gl"], ALU.mult).then_inc(self.step, 1)
        dve.wait_ge(self.step, n + 2 + LEAD)
        nc.vector.tensor_tensor(dots[:, 1, :], R, w["gr"], ALU.mult).then_inc(self.step, 1)
        nc.vector.tensor_tensor(L, L, R, ALU.subtract).then_inc(self.step, 1)
        dve.wait_ge(self.step, n + 4 + LEAD)
        nc.vector.tensor_reduce(z, dots.rearrange("p a (h d) -> p h a d", h=HEADS), mybir.AxisListType.XY, ALU.add).then_inc(self.z_ready, 1)
        dve.wait_ge(self.g_ready, u + 1 + LEAD)
        nc.vector.tensor_scalar(z, z, 1.0, None, ALU.add).then_inc(self.step, 1)
        dve.wait_ge(self.step, n + 6 + LEAD)
        nc.vector.reciprocal(z, z).then_inc(self.step, 1)
        dve.wait_ge(self.step, n + 7 + LEAD)
        nc.vector.tensor_tensor(L.rearrange("p (h d) -> p h d", h=HEADS), L.rearrange("p (h d) -> p h d", h=HEADS),
                                z.unsqueeze(2).to_broadcast([128, HEADS, HD]), ALU.mult).then_inc(self.step, 1)
        dve.wait_ge(self.step, n + 8 + LEAD)
        nc.vector.tensor_tensor(L, L, R, ALU.add).then_inc(done, 1)

    def gate(self, act, u, qb):
        act.wait_ge(self.z_ready, u + 1 + LEAD)
        self.nc.scalar.activation(self.z[:, qb, :], self.z[:, qb, :], ACT.Exp, scale=-1.0).then_inc(self.g_ready, 1)


STEPS_OF_MIX = 8


def split_heads(blocks):
    return blocks.rearrange("p j (h d) -> p j h d", h=HEADS)


def project_qkv(nc, stage, mem, U, K, V, rope):
    w = mem.w
    with ExitStack() as ctx:
        def sb(name, *shape):
            return ctx.enter_context(nc.sbuf_tensor(stage + "_" + name, [D, *shape], F32))
        x = sb("x", 2, T)
        part = sb("part", 2, 2, 2, T) if rope else None
        names = ["q", "k", "swap_q", "swap_k"] if rope else ["q", "k"]
        (copied, ones, qk_ready, v_ready, turned, qk_stored, v_stored) = ctx.enter_context(signals(
            nc, stage, "copied", "ones", "qk", "v", "turned", "qk_stored", "v_stored"))
        block = ctx.enter_context(nc.Block())

        def ps_of(i, s):
            return mem.bank[2 * i + s] if i < 2 else mem.bank[4 + i]

        @block.scalar
        def _(act):
            def copy(t, s):
                act.wait_ge(v_ready, t - 1 + LEAD)
                act.sem_inc(PASSED[0], 1)
                nc.scalar.activation(x[:, s, :], U[:, cols(t)], ACT.Identity).then_inc(copied, 1)

            def store(t, s):
                if not rope:
                    for i, to in enumerate((U, K)):
                        act.wait_ge(qk_ready, 2 * t + i + 1 + LEAD)
                        act.sem_inc(PASSED[0], 1)
                        nc.scalar.activation(to[:, cols(t)], ps_of(i, s), ACT.Identity, bias=w["qk_b"][:, i:i + 1]).then_inc(qk_stored, 1)

            copy(0, 0)
            with act.Fori(0, NT // 2 - 1) as pair:
                for s in range(2):
                    copy(pair * 2 + s + 1, 1 - s)
                    store(pair * 2 + s, s)
            copy(NT - 1, 1)
            store(NT - 2, 0)
            store(NT - 1, 1)

        @block.tensor
        def _(pe):
            def step(t, s):
                pe.wait_ge(copied, t + 1 + LEAD)
                for i, name in enumerate(names):
                    if rope:
                        pe.wait_ge(turned, (len(names) * (t - 1) + i + 1 if i < 2 else len(names) * (t - 1) + i + 1) + LEAD)
                    else:
                        pe.wait_ge(qk_stored, 2 * (t - 2) + i + 1 + LEAD)
                    nc.tensor.matmul(ps_of(i, s), w[name], x[:, s, :], start=True, stop=True).then_inc(qk_ready, 1)
                pe.wait_ge(v_stored, t - 1 + LEAD)
                for j in range(SUB):
                    last = nc.tensor.matmul(mem.bank[4 + s][:, j * D:(j + 1) * D], x[:, s, j * 128:(j + 1) * 128], w["v"], start=True, stop=True)
                last.then_inc(v_ready, 1)
            tile_pairs(pe, step)

        @block.gpsimd
        def _(pool):
            nc.gpsimd.memset(V[:, :, :, HD:HD + 1], 1.0).then_inc(ones, 1)
            if rope:
                def add(t, s):
                    for i, to in enumerate((U, K)):
                        pool.wait_ge(turned, 4 * t + 3 + i + LEAD)
                        pool.sem_inc(PASSED[0], 1)
                        nc.gpsimd.tensor_tensor(to[:, cols(t)], part[:, s, i, 0, :], part[:, s, i, 1, :], ALU.add).then_inc(qk_stored, 1)
                tile_pairs(pool, add)

        @block.vector
        def _(dve):
            def step(t, s):
                if rope:
                    for i in range(4):
                        dve.wait_ge(qk_ready, 4 * t + i + 1 + LEAD)
                        dve.wait_ge(qk_stored, 2 * (t - 2) + i % 2 + 1 + LEAD)
                        by_seq = lambda ap: ap.rearrange("p (b t) -> p b t", b=SEQ_T)
                        table = mem.w["cos" if i < 2 else "sin"].unsqueeze(1).to_broadcast([D, SEQ_T, S])
                        nc.vector.tensor_tensor(by_seq(part[:, s, i % 2, i // 2, :]), by_seq(ps_of(i, s)), table, ALU.mult).then_inc(turned, 1)
                dve.wait_ge(v_ready, t + 1 + LEAD)
                to = V[:, bass.ds(t * SUB, SUB), :, 0:HD]
                src = split_heads(mem.bank[4 + s].rearrange("p (j n) -> p j n", j=SUB))
                bias = split_heads(w["v_b"].unsqueeze(1).to_broadcast([128, SUB, D])) if not rope else None
                for j in range(SUB):
                    one = V[:, bass.ds(t * SUB + j, 1), :, 0:HD].rearrange("p a h d -> p (a h) d")
                    if rope:
                        last = nc.vector.tensor_scalar(one, src[:, j, :, :], 1.0, None, ALU.mult)
                    else:
                        last = nc.vector.tensor_tensor(one, src[:, j, :, :], w["v_b"].rearrange("p (h d) -> p h d", h=HEADS), ALU.add)
                last.then_inc(v_stored, 1)
            tile_pairs(dve, step)


def causal_attention(nc, mem, X, U, weights):
    layer_norm(nc, "cau_ln", mem, X, U)
    with weights("l1b") as held:
        K = held.enter_context(nc.sbuf_tensor("cau_K", [D, TOK], F32))
        V = held.enter_context(nc.sbuf_tensor("cau_V", [128, NB, HEADS, HD + 1], F32))
        project_qkv(nc, "cau_qkv", mem, U, K, V, rope=True)
        attend(nc, "cau", mem, rows=D, groups=4, heads=4, widths=(128, 256), chunk=128, q=U, head_mask=mem.w["head_mask"],
               keys=lambda b, width: K[:, bass.ds(b * S, width)],
               masks=[[(0, mem.masks[:, 0, :])], [(128, mem.masks[:, 0, :])]],
               values=lambda b, c, h: V[:, bass.ds(b * QB + c, 1), h, :].rearrange("p a d -> p (a d)"), dst=U)
        project_add(nc, "cau_out", mem, mem.w["o"], U, X)


def pool_latents(nc, mem, U, RQ, RK, RV):
    w = mem.w
    NLAT = NSEQ * LAT
    with ExitStack() as ctx:
        pooled = ctx.enter_context(nc.sbuf_tensor("lat_pooled", [D, NLAT], F32))
        (rq_ready, rq_stored, sums, means, rk_ready, rk_stored, rv_ready, rv_stored, ones) = ctx.enter_context(signals(
            nc, "latp", "rq", "rq_stored", "sums", "means", "rk", "rk_stored", "rv", "rv_stored", "ones"))
        block = ctx.enter_context(nc.Block())

        @block.tensor
        def _(pe):
            def step(t, s):
                pe.wait_ge(rq_stored, t - 1 + LEAD)
                nc.tensor.matmul(mem.bank[s][0:LD, :], w["rq"], U[:, cols(t)], start=True, stop=True).then_inc(rq_ready, 1)
            tile_pairs(pe, step)
            pe.wait_ge(means, 1 + LEAD)
            for i in range(NLAT // T):
                nc.tensor.matmul(mem.bank[2 + i % 4][0:LD, :], w["rk"], pooled[:, i * T:(i + 1) * T], start=True, stop=True).then_inc(rk_ready, 1)
            for b in range(NSEQ):
                if b % 16 == 0:
                    bank = mem.bank[6 + b // 16]
                last = nc.tensor.matmul(bank[0:LAT, (b % 16) * LD:(b % 16 + 1) * LD], pooled[:, b * LAT:(b + 1) * LAT], w["rv"], start=True, stop=True)
            last.then_inc(rv_ready, 1)

        @block.scalar
        def _(act):
            def step(t, s):
                act.wait_ge(rq_ready, t + 1 + LEAD)
                act.sem_inc(PASSED[0], 1)
                nc.scalar.activation(RQ[:, cols(t)], mem.bank[s][0:LD, :], ACT.Identity, bias=w["rq_b"]).then_inc(rq_stored, 1)
            tile_pairs(act, step)
            for i in range(NLAT // T):
                act.wait_ge(rk_ready, i + 1 + LEAD)
                nc.scalar.activation(RK[:, i * T:(i + 1) * T], mem.bank[2 + i % 4][0:LD, :], ACT.Identity, bias=w["rk_b"]).then_inc(rk_stored, 1)

        @block.vector
        def _(dve):
            nc.vector.memset(RV[:, :, :, HD:HD + 1], 1.0).then_inc(ones, 1)
            nc.vector.tensor_reduce(pooled[:, :], U[:, :].rearrange("p (n c) -> p n c", c=POOLED), AX_X, ALU.add).then_inc(sums, 1)
            dve.wait_ge(sums, 1 + LEAD)
            nc.vector.tensor_scalar(pooled[:, :], pooled[:, :], 1.0 / POOLED, None, ALU.mult).then_inc(means, 1)
            dve.wait_ge(rv_ready, 1 + LEAD)
            bias = w["rv_b"].rearrange("p (h d) -> p h d", h=LHEADS)[0:LAT]
            for b in range(NSEQ):
                nc.vector.tensor_tensor(RV[:, b, :, 0:HD], mem.bank[6 + b // 16][0:LAT, (b % 16) * LD:(b % 16 + 1) * LD].rearrange("p (h d) -> p h d", h=LHEADS),
                                        bias, ALU.add)


def local_latent_attention(nc, mem, X, U, weights):
    layer_norm(nc, "loc_ln", mem, X, U)
    with weights("l1a") as held:
        lat = held.enter_context(nc.sbuf_tensor("lat_out", [LD, TOK], F32))
        with ExitStack() as inner:
            RK = inner.enter_context(nc.sbuf_tensor("RK", [LD, NSEQ * LAT], F32))
            RV = inner.enter_context(nc.sbuf_tensor("RV", [LAT, NSEQ, LHEADS, HD + 1], F32))
            pool_latents(nc, mem, U, lat, RK, RV)
            attend(nc, "lat", mem, rows=LD, groups=1, heads=LHEADS, widths=(LAT, LAT), chunk=LAT, q=lat, head_mask=mem.w["head_mask"][0:LD, 0:LHEADS],
                   keys=lambda b, width: RK[:, bass.ds(b * LAT, LAT)],
                   masks=[[(0, mem.masks[:, 3, 0:LAT])], [(0, mem.masks[:, 3, LAT:2 * LAT])]],
                   values=lambda b, c, h: RV[:, bass.ds(b, 1), h, :].rearrange("p a d -> p (a d)"), dst=lat,
                   valid=mem.w["sees_latent"])
        K = held.enter_context(nc.sbuf_tensor("loc_K", [D, TOK], F32))
        V = held.enter_context(nc.sbuf_tensor("loc_V", [128, NB, HEADS, HD + 1], F32))
        project_qkv(nc, "loc_qkv", mem, U, K, V, rope=False)
        attend(nc, "loc", mem, rows=D, groups=4, heads=4, widths=(128, 256), chunk=128, q=U, head_mask=mem.w["head_mask"],
               keys=lambda b, width: K[:, bass.ds(b * S, width)],
               masks=[[(0, mem.masks[:, 1, :])], [(0, mem.masks[:, 2, :]), (128, mem.masks[:, 1, :])]],
               values=lambda b, c, h: V[:, bass.ds(b * QB + c, 1), h, :].rearrange("p a d -> p (a d)"), dst=U,
               valid=mem.w["sees_key"], mix=GateMix(mem, lat))
        project_add(nc, "loc_out", mem, mem.w["o"], U, X, bias=mem.w["o_b"])


def rows_in_halves(a):
    return np.concatenate([a[0:128], a[128:256]], axis=1)


def pack_mamba(i):
    out = {}
    for c in DIRS:
        g = lambda name: i[f"L0_attn_a_{name}_{c}"]
        out["in_" + c] = g("in_w").T
        out["conv_b_" + c] = rows_in_halves(g("conv_b")[:, None])
        xp = g("xp_w").T
        bc = xp[:, RANK:]
        xp = np.concatenate([xp[:, 0:RANK], np.zeros((256, 32 - RANK), np.float32), bc, bc, bc], axis=1)
        out["xp_" + c] = rows_in_halves(xp)
        out["dtp_" + c] = g("dtp_w").T
        out["dtp_b_" + c] = rows_in_halves(g("dtp_b")[:, None])
        out["A_log_" + c] = rows_in_halves(g("A_log"))
        out["D_" + c] = rows_in_halves(g("D")[:, None])
        out["out_" + c] = g("out_w")
    for start in (64, 96):
        out["from_%d" % start] = (np.arange(D)[:, None] >= start).astype(np.float32)
    out["proj"] = rows_in_halves(i["L0_attn_a_proj_w"].T)
    out["proj_b"] = i["L0_attn_a_proj_b"][:, None]
    out["gamma_a"] = i["L0_attn_a_ln_gamma"][:, None]
    out["beta_a"] = i["L0_attn_a_ln_beta"][:, None]
    return out


def col(a):
    return a[:, None]


def pack_l0(i):
    f, r = (lambda name: i["L0_ffn_" + name]), (lambda name: i["L0_attn_b_" + name])
    return {
        "pw": f("pw_w").T, "dw": f("dw_kernel")[:, 0, :], "dw_bias": col(f("dw_bias")), "pw_b": col(f("pw_b")),
        "router": f("router_w").T, "router_b": np.repeat(f("router_b")[None, :], D, axis=0),
        "experts": f("expert_w").transpose(2, 0, 1).reshape(D, NE * D), "expert_b": f("expert_b").T,
        "out": f("out_w").T, "out_b": col(f("out_b")), "norm_w": col(f("norm_w")),
        "down": f("ff_down_w").T, "down_b": col(f("ff_down_b")), "up": f("ff_up_w").T, "up_b": col(f("ff_up_b")),
        "rnn_A": r("A").T, "rnn_B": r("B").T, "rnn_C": r("C").T, "rnn_gamma": col(r("gamma")), "rnn_beta": col(r("beta")),
    }


def pack_l1_norm(i):
    f = lambda name: i["L1_ffn_" + name]
    return {"l1_gamma": col(f("ln_gamma")), "l1_beta": col(f("ln_beta")), "l1_router": f("router_w")}


def pack_l1_moe(i):
    f = lambda name: i["L1_ffn_" + name]
    return {
        "gate_up": f("gate_up_w").transpose(1, 0, 2).reshape(D, NE * 2 * F),
        "l1_down": f("down_w").reshape(NE * CH, 128, D).transpose(1, 0, 2).reshape(128, NE * CH * D),
        "shared_gate": f("shared_gate_up_w")[:, 0:128], "shared_up": f("shared_gate_up_w")[:, 128:256],
        "shared_down": f("shared_down_w"),
    }


def shared_attention():
    p = np.arange(D)
    return {"head_mask": (p[:, None] // HD == np.arange(HEADS)[None, :]).astype(np.float32)}


def pack_l1a(i):
    f = lambda name: i["L1_attn_a_" + name]
    on_all = lambda v: np.repeat(v[None, :], D, axis=0)
    p = np.arange(D)[:, None]
    return {
        "q": f("qkv_w")[:, 0:D], "k": f("qkv_w")[:, D:2 * D], "v": f("qkv_w")[:, 2 * D:],
        "qk_b": f("qkv_b")[0:2 * D].reshape(2, D).T, "v_b": on_all(f("qkv_b")[2 * D:]),
        "rq": f("rq_w"), "rq_b": col(f("rq_b")), "rk": f("rkv_w")[:, 0:LD], "rk_b": col(f("rkv_b")[0:LD]),
        "rv": f("rkv_w")[:, LD:], "rv_b": on_all(f("rkv_b")[LD:]), "rout": f("rout_w"), "rout_b": on_all(f("rout_b")),
        "o": f("out_w"), "o_b": col(f("out_b")),
        "gl": on_all(np.tile(f("gl_w")[:, 0], HEADS)), "gr": on_all(np.tile(f("gr_w")[:, 0], HEADS)),
        "sees_key": (p >= 1).astype(np.float32), "sees_latent": (p >= POOLED).astype(np.float32),
        **shared_attention(),
    }


def pack_l1b(i):
    f = lambda name: i["L1_attn_b_" + name].T
    pairs = np.arange(D).reshape(-1, 2)[:, ::-1].ravel()
    half = HD // 2
    inv_freq = np.float32(10000.0) ** (-np.arange(half, dtype=np.float32) * np.float32(2.0) / np.float32(HD))
    angle = np.arange(S, dtype=np.float32)[None, :] * inv_freq[(np.arange(D) % HD) // 2][:, None]
    sign = np.where(np.arange(D) % 2 == 0, -1.0, 1.0)[:, None]
    return {
        "q": f("Wq"), "k": f("Wk"), "v": f("Wv"), "o": f("Wo"), "swap_q": f("Wq")[:, pairs], "swap_k": f("Wk")[:, pairs],
        "cos": np.cos(angle).astype(np.float32), "sin": (sign * np.sin(angle)).astype(np.float32), **shared_attention(),
    }


def attention_masks():
    q, k = np.arange(128)[:, None], np.arange(128)[None, :]
    latent = np.concatenate([np.arange(LAT)[None, :] < (q + qb * 128) // POOLED for qb in range(QB)], axis=1)
    seen = np.stack([k <= q, k < q, (k >= q) & (k >= 1), latent], axis=1)
    return np.where(seen, 0.0, -1e30).astype(np.float32)


def constants():
    full = lambda v: np.full((D, 1), v, np.float32)
    e = np.arange(NE)
    earlier = (e[None, :] < e[:, None]).astype(np.float32)
    return {"ident": np.eye(D, dtype=np.float32), "avg": np.full((D, D), 1.0 / D, np.float32),
            "eps": full(EPS), "eps2": full(EPS * EPS), "eps6": full(1e-6), "one": full(1.0), "zero": full(0.0),
            "earlier": np.repeat(earlier.reshape(1, NE * NE), D, axis=0)}


def pack_taps(i):
    return {"taps_" + c: np.repeat(i["L0_attn_a_conv_w_" + c][:, 0, :].T.reshape(1, 4 * 256), D, axis=0) for c in DIRS}


def one_hot_columns():
    sel = np.zeros((D, D), np.float32)
    for k in range(3):
        for e in range(NE):
            sel[k * NE + e, e] = 1.0
        for n in range(2 * NST):
            sel[32 * (k + 1) + n, NE + n] = 1.0
    return sel


def pack(parts):
    where, at = {}, 0
    for name, a in parts.items():
        where[name] = (a.shape[0], at, at + a.shape[1])
        at += a.shape[1]
    whole = np.zeros((D, at), np.float32)
    for name, a in parts.items():
        rows, lo, hi = where[name]
        whole[0:rows, lo:hi] = a
    return whole, where


def load_weights(nc, ctx, name, dram, where):
    held = ctx.enter_context(nc.sbuf_tensor(name, [D, dram.shape[1]], F32))
    return held, {k: held[0:rows, lo:hi] for k, (rows, lo, hi) in where.items()}


def program(nc, x_in, consts, consts16, packs, out):
    with ExitStack() as ctx:
        mem = Memory()
        PASSED[:] = [nc.alloc_semaphore("waits_passed")]
        mem.psum = ctx.enter_context(nc.psum_tensor("psum", [D, 8, T], F32))
        mem.bank = [mem.psum[:, b, :] for b in range(8)]
        X = ctx.enter_context(nc.sbuf_tensor("X", [D, TOK], F32))
        U = ctx.enter_context(nc.sbuf_tensor("U", [D, TOK], F32))
        held, const = load_weights(nc, ctx, "consts", consts[0], consts[1])
        mem.ident, mem.avg = const["ident"], const["avg"]
        mem.eps, mem.eps2, mem.one = const["eps"], const["eps2"], const["one"]
        mem.zero, mem.w, mem.const = const["zero"], {}, const

        uses = []

        @contextmanager
        def weights(group):
            uses.append(group)
            with ExitStack() as inner:
                dram, where = packs[group]
                mem.w_outer = mem.w
                held_w, mem.w = load_weights(nc, inner, "weights_%s%d" % (group, len(uses)), dram, where)
                mem.w.update(const)
                (landed,) = inner.enter_context(signals(nc, "load_%s%d" % (group, len(uses)), "landed"))
                with nc.Block() as block:
                    @block.sync
                    def _(sp):
                        sp.dma_start(held_w[:, :], dram).then_inc(landed, 16)
                        sp.wait_ge(landed, 16 + LEAD)
                yield inner

        held16 = ctx.enter_context(nc.sbuf_tensor("consts16", [D, 6, D], BF16))
        mem.ident16, mem.masks, mem.one_hot = held16[:, 0, :], held16[:, 1:5, :], held16[:, 5, :]
        mem.sel = held16[:, 5, NE:NE + 2 * NST]
        (loaded,) = ctx.enter_context(signals(nc, "load", "loaded"))
        with nc.Block() as block:
            @block.sync
            def _(sp):
                sp.dma_start(held[:, :], consts[0]).then_inc(loaded, 16)
                sp.dma_start(X[:, :], x_in).then_inc(loaded, 16)
                sp.dma_start(held16[:, :, :], consts16).then_inc(loaded, 16)
                sp.wait_ge(loaded, 48 + LEAD)

        with ExitStack() as stage:
            mem.A = stage.enter_context(nc.sbuf_tensor("A", [D, 2, 2 * NST], F32))
            mem.conv_in = stage.enter_context(nc.sbuf_tensor("conv_in", [D, 2, 4, 256], F32))
            mem.out_proj = stage.enter_context(nc.sbuf_tensor("out_proj", [D, 2, 2, D], F32))
            with weights("mamba"):
                with weights("taps"):
                    mem.w.update(mem.w_outer)
                    mamba_weights(nc, mem)
                mem.w = mem.w_outer
                layer_norm(nc, "ln_a", mem, X, U, affine=(mem.w["gamma_a"], mem.w["beta_a"]), twice=True, residual=X)
                mamba(nc, mem, X, U)
        with weights("l0") as held_l0:
            mem.pw_taps = held_l0.enter_context(nc.sbuf_tensor("pw_taps", [D, 3, D], F32))
            mem.pw_bias = held_l0.enter_context(nc.sbuf_tensor("pw_bias", [D, 1], F32))
            mem.expert_high = held_l0.enter_context(nc.sbuf_tensor("expert_high", [D, NE * D], F32R))
            mem.expert_low = held_l0.enter_context(nc.sbuf_tensor("expert_low", [D, NE * D], F32R))
            l0_weights(nc, mem)
            l0_ffn(nc, "ffn1", mem, X, U)
            recurrent(nc, mem, X, U)
            l0_ffn(nc, "ffn2", mem, X, U)
        local_latent_attention(nc, mem, X, U, weights)
        with weights("l1_norm"):
            l1_ffn(nc, "ffn3", mem, X, U, packs["l1_moe"])
        causal_attention(nc, mem, X, U, weights)
        with weights("l1_norm"):
            l1_ffn(nc, "ffn4", mem, X, U, packs["l1_moe"], out)


def kernel(**inputs):
    import concourse.bacc as bacc
    import ml_dtypes
    from concourse.bass_utils import run_bass_kernel_spmd

    i = {name: np.asarray(a) for name, a in inputs.items()}
    nc = bacc.Bacc("TRN2", target_bir_lowering=False, num_devices=1)
    arrays = {}

    def given(name, a):
        a = np.ascontiguousarray(a)
        arrays[name] = a
        return nc.dram_tensor(name, a.shape, mybir.dt.from_np(a.dtype), kind="ExternalInput").ap()

    def packed(name, parts):
        whole, where = pack(parts)
        return given("in_" + name, whole), where

    x_in = given("in_x", i["L0_attn_a_x"].reshape(TOK, D).T)
    consts = packed("consts", constants())
    consts16 = given("in_consts16", np.concatenate([np.eye(D)[:, None, :], attention_masks(), one_hot_columns()[:, None, :]], axis=1).astype(ml_dtypes.bfloat16))
    packs = {
        "mamba": packed("mamba", pack_mamba(i)), "taps": packed("taps", pack_taps(i)), "l0": packed("l0", pack_l0(i)),
        "l1_norm": packed("l1_norm", pack_l1_norm(i)),
        "l1_moe": packed("l1_moe", pack_l1_moe(i)), "l1a": packed("l1a", pack_l1a(i)), "l1b": packed("l1b", pack_l1b(i)),
    }
    out = nc.dram_tensor("out", (D, TOK), F32, kind="ExternalOutput").ap()
    program(nc, x_in, consts, consts16, packs, out)
    r = run_bass_kernel_spmd(nc, [arrays], core_ids=[0])
    return np.ascontiguousarray(r.results[0]["out"].T).reshape(NSEQ, S, D)
```
